# Optimizing a Trainium2 kernel written in Bass

```python
import numpy as np
import jax
import jax.numpy as jnp

def _softmax(x, axis=-1):
    return jax.nn.softmax(x, axis=axis)

def _gelu(x):
    return jax.nn.gelu(x, approximate=True)

def _silu(x):
    return jax.nn.silu(x)

def _sigmoid(x):
    return jax.nn.sigmoid(x)

def _layernorm(x, axis=-1, eps=1e-05):
    m = jnp.mean(x, axis=axis, keepdims=True)
    v = jnp.var(x, axis=axis, keepdims=True)
    return (x - m) / jnp.sqrt(v + eps)

def _scatter_add(tgt, idx, src, axis=0):
    return tgt.at[idx].add(src)

def _segment_sum(src, seg, n):
    return jax.ops.segment_sum(src, seg, n)
kernel_name = 'mk_gnn_ffn_d1_gnn_r8_7a2eb6'

def setup_inputs(seed: int=0):
    np.random.seed(seed)
    _w = jnp.asarray

    def _rec_inputs():
        import jax
        import jax.numpy as jnp
        _gk = jax.random.key(seed)
        x = -0.0002117 + 1 * jax.random.normal(jax.random.fold_in(_gk, 1), (1250, 1024), jnp.float32)
        src = jax.random.randint(jax.random.fold_in(_gk, 2), (40000,), 0, 1250, jnp.int32)
        dst = jnp.minimum((1250 * jax.random.uniform(jax.random.fold_in(_gk, 3), (40000,)) ** 2.0).astype(jnp.int32), 9999)
        _o = jnp.argsort(dst, stable=True)
        src = src[_o]
        dst = dst[_o]
        return (x, src, dst)
    x, src, dst = _rec_inputs()

    def _L0_gnn_setup():
        import jax, jax.numpy as jnp
        import numpy as np
        N_NODES = 3125
        N_EDGES = 50000
        D = 1024

        def _sage_layer(h, edge_src, edge_dst, deg_inv, W_self, W_neigh, b):
            msg = h[edge_src]
            agg = jax.ops.segment_sum(msg, edge_dst, num_segments=h.shape[0])
            mean = agg * deg_inv[:, None]
            return h @ W_self + mean @ W_neigh + b
        key = jax.random.key(seed)
        ks = jax.random.split(key, 8)
        s = 1.0 / np.sqrt(D)
        return {'x': jax.random.normal(ks[0], (N_NODES, D), dtype=jnp.float32), 'edge_src': jax.random.randint(ks[1], (N_EDGES,), 0, N_NODES, dtype=jnp.int32), 'edge_dst': jax.random.randint(ks[2], (N_EDGES,), 0, N_NODES, dtype=jnp.int32), 'W_self0': jax.random.normal(ks[3], (D, D), dtype=jnp.float32) * s, 'W_neigh0': jax.random.normal(ks[4], (D, D), dtype=jnp.float32) * s, 'b0': jnp.zeros((D,), dtype=jnp.float32), 'W_self1': jax.random.normal(ks[5], (D, D), dtype=jnp.float32) * s, 'W_neigh1': jax.random.normal(ks[6], (D, D), dtype=jnp.float32) * s, 'b1': jnp.zeros((D,), dtype=jnp.float32)}
    _L0_gnn_all = _L0_gnn_setup()
    _L0_gnn_in = {k: v for k, v in _L0_gnn_all.items() if k in ('W_self0', 'W_neigh0', 'b0', 'W_self1', 'W_neigh1', 'b1')}
    del _L0_gnn_all

    def _L0_ffn_setup():
        import jax, jax.numpy as jnp
        import numpy as np
        B, F, D, H, E, K = (4, 256, 1024, 256, 8, 2)
        key = jax.random.key(seed)
        ks = jax.random.split(key, 9)
        sc = lambda k, shape, fan_in: jax.random.normal(k, shape, jnp.float32) * fan_in ** (-0.5)
        return {'x': jax.random.normal(ks[0], (B, F, D), jnp.float32), 'rw1': sc(ks[1], (D, D), D), 'rb1': jnp.zeros((D,), jnp.float32), 'rw2': sc(ks[2], (D, E), D), 'rb2': jnp.zeros((E,), jnp.float32), 'ew1': sc(ks[3], (E, D, H), D), 'eb1': jnp.zeros((E, H), jnp.float32), 'ew2': sc(ks[4], (E, H, D), H), 'eb2': jnp.zeros((E, D), jnp.float32)}
    _L0_ffn_all = _L0_ffn_setup()
    _L0_ffn_in = {k: v for k, v in _L0_ffn_all.items() if k in ('rw1', 'rb1', 'rw2', 'rb2', 'ew1', 'eb1', 'ew2', 'eb2')}
    del _L0_ffn_all
    return {'x': x, 'src': src, 'dst': dst, 'L0_gnn_W_self0': _L0_gnn_in['W_self0'], 'L0_gnn_W_neigh0': _L0_gnn_in['W_neigh0'], 'L0_gnn_b0': _L0_gnn_in['b0'], 'L0_gnn_W_self1': _L0_gnn_in['W_self1'], 'L0_gnn_W_neigh1': _L0_gnn_in['W_neigh1'], 'L0_gnn_b1': _L0_gnn_in['b1'], 'L0_ffn_rw1': _L0_ffn_in['rw1'], 'L0_ffn_rb1': _L0_ffn_in['rb1'], 'L0_ffn_rw2': _L0_ffn_in['rw2'], 'L0_ffn_rb2': _L0_ffn_in['rb2'], 'L0_ffn_ew1': _L0_ffn_in['ew1'], 'L0_ffn_eb1': _L0_ffn_in['eb1'], 'L0_ffn_ew2': _L0_ffn_in['ew2'], 'L0_ffn_eb2': _L0_ffn_in['eb2']}

def reference(x, src, dst, L0_gnn_W_self0, L0_gnn_W_neigh0, L0_gnn_b0, L0_gnn_W_self1, L0_gnn_W_neigh1, L0_gnn_b1, L0_ffn_rw1, L0_ffn_rb1, L0_ffn_rw2, L0_ffn_rb2, L0_ffn_ew1, L0_ffn_eb1, L0_ffn_ew2, L0_ffn_eb2):
    import jax
    import jax.numpy as jnp

    def _L0_gnn_ref(x, edge_src, edge_dst, W_self0, W_neigh0, b0, W_self1, W_neigh1, b1):
        import jax, jax.numpy as jnp
        import numpy as np
        N_NODES = 3125
        N_EDGES = 50000
        D = 1024

        def _sage_layer(h, edge_src, edge_dst, deg_inv, W_self, W_neigh, b):
            msg = h[edge_src]
            agg = jax.ops.segment_sum(msg, edge_dst, num_segments=h.shape[0])
            mean = agg * deg_inv[:, None]
            return h @ W_self + mean @ W_neigh + b
        N = x.shape[0]
        deg = jax.ops.segment_sum(jnp.ones_like(edge_dst, dtype=x.dtype), edge_dst, num_segments=N)
        deg_inv = 1.0 / jnp.maximum(deg, 1.0)
        h = jax.nn.relu(_sage_layer(x, edge_src, edge_dst, deg_inv, W_self0, W_neigh0, b0))
        out = _sage_layer(h, edge_src, edge_dst, deg_inv, W_self1, W_neigh1, b1)
        return out

    def _L0_ffn_ref(x, rw1, rb1, rw2, rb2, ew1, eb1, ew2, eb2):
        import jax, jax.numpy as jnp
        import numpy as np
        B, F, D, H, E, K = (4, 256, 1024, 256, 8, 2)
        b, f, d = x.shape
        t = x.reshape(b * f, d)
        logits = jax.nn.silu(t @ rw1 + rb1) @ rw2 + rb2
        vals, idx = jax.lax.top_k(logits, K)
        rows = jnp.arange(t.shape[0])[:, None]
        masked = jnp.full_like(logits, -jnp.inf).at[rows, idx].set(vals)
        w = jax.nn.softmax(masked, axis=1)
        eh = jax.nn.silu(jnp.einsum('td,edh->teh', t, ew1) + eb1[None])
        eo = jnp.einsum('teh,ehd->ted', eh, ew2) + eb2[None]
        y = t + jnp.einsum('te,ted->td', w, eo)
        return y.reshape(b, f, d)
    x = x + _L0_gnn_ref(_layernorm(x, axis=-1), src, dst, L0_gnn_W_self0, L0_gnn_W_neigh0, L0_gnn_b0, L0_gnn_W_self1, L0_gnn_W_neigh1, L0_gnn_b1)
    x = x + _L0_ffn_ref(_layernorm(x, axis=-1)[None], L0_ffn_rw1, L0_ffn_rb1, L0_ffn_rw2, L0_ffn_rb2, L0_ffn_ew1, L0_ffn_eb1, L0_ffn_ew2, L0_ffn_eb2)[0]
    return x

_drawn_inputs = setup_inputs


def setup_inputs(seed=0):
    import zlib

    import numpy as np

    out = dict(_drawn_inputs(seed))
    spreads = {'L0_gnn_b0': (0.0, 0.1),
     'L0_gnn_b1': (0.0, 0.1),
     'L0_ffn_rb1': (0.0, 0.1),
     'L0_ffn_rb2': (0.0, 0.1),
     'L0_ffn_eb1': (0.0, 0.422),
     'L0_ffn_eb2': (0.0, 0.1)}
    factors = {}
    for name, (base, spread) in spreads.items():
        noise = np.random.default_rng([zlib.crc32(name.encode()), seed]).standard_normal(out[name].shape)
        drawn = base * np.exp(spread * noise) if base else spread * noise
        out[name] = jnp.asarray(drawn.astype(out[name].dtype))
    for name, factor in factors.items():
        out[name] = (out[name] * factor).astype(out[name].dtype)
    return out
```

```python
from contextlib import ExitStack

import concourse.bass as bass
from concourse import mybir

F32 = mybir.dt.float32
F32R = mybir.dt.float32r
BF16 = mybir.dt.bfloat16
F16 = mybir.dt.float16
I32 = mybir.dt.int32
U16 = mybir.dt.uint16
ALU = mybir.AluOpType
ACT = mybir.ActivationFunctionType
AX = mybir.AxisListType
ds = bass.ds

N = 1250
D = 1024
P = 125
NT = N // P
KT = D // 128
E = 40000
NCH = E // P
G = 8
HG = G // 2
EXACT = 4096.0
FAST = NCH // G + NT
FULL = NT * (NCH // G)
COLS = ((0, 418), (418, 416), (834, 416))
NX = 8
HID = 256
TOP = 2
M = 256
NS = (TOP * N + NX * (M - 1)) // M
SUB = M // 128
HK = HID // 128
EPS = 1e-5
ROUND = 1.5 * 2.0 ** 23


DEBUG = ()


def skewed(e, n, head, tail):
    head(0, 0, 0)
    with e.Fori(0, (n - 2) // 2) as q:
        head(2 * q + 1, 1, q)
        tail(2 * q, 0, q)
        head(2 * q + 2, 0, q + 1)
        tail(2 * q + 1, 1, q)
    for i in range((n - 2) // 2 * 2 + 1, n):
        head(i, i % 2, i // 2)
        tail(i - 1, (i - 1) % 2, (i - 1) // 2)
    tail(n - 1, (n - 1) % 2, (n - 1) // 2)


def build(nc, I, out):
    ctx = ExitStack()
    with ctx:
        prog = {k: [] for k in ("sync", "scalar", "vector", "gpsimd", "tensor")}

        def on(engine):
            return prog[engine].append

        def sem(name):
            return ctx.enter_context(nc.semaphore(name))

        top = nc.sbuf_base + (-nc.sbuf_base) % 32
        R_H, R_A, R_ACC, R_SLAB, R_WORK = (top + x for x in (0, 80000, 130016, 155040, 179616))
        R_CONST = R_WORK + 25344

        class Region:
            def __init__(self, at):
                self.at = at

            def __call__(self, name, shape, dt):
                t = nc.alloc_sbuf_tensor_at(name, shape, dt, offset=self.at)
                size = 2 if dt in (BF16, F16, U16) else 4
                for s in shape[1:]:
                    size *= s
                self.at += size + (-size) % 32
                return t

        C = Region(R_CONST)
        ident = C("ident", [128, 128], F32)
        ones = C("ones", [128, 128], F32)
        bias = C("bias", [128, 3, KT], F32)
        deg = C("deg", [P, NT], F32)
        dinv = C("dinv", [P, NT], F32)
        rw2 = C("rw2", [128, KT, NX], F32)
        mv = C("mv", [P, 2, 2], F32)
        stats = C("stats", [P, 2, 2, 6], F32)
        rstd = C("rstd", [P, 2, 4], F32)
        epst = C("epst", [128, 1], F32)
        logit = C("logit", [P, NT, NX], F32)
        flagi = C("flagi", [1, 8], I32)

        H = Region(R_H)
        h_hi = H("h_hi", [128, KT, N], F32R)
        h_lo = H("h_lo", [128, KT, N], F32R)

        adj = Region(R_A)("adj", [P, NT, N], F32R)
        acc = Region(R_ACC)("acc", [P, NT, N], U16)
        S = Region(R_A)
        src_hot = S("src_hot", [P, 2, G, N], BF16)
        dst_hot = S("dst_hot", [P, 2, G, P], BF16)
        node16 = S("node16", [P, N], F16)
        dcol = S("dcol", [P, NCH + G], F16)
        scol = S("scol", [P, NCH + G], F32)
        src_now = S("src_now", [P, 2, 1], F32)
        S = Region(R_WORK)
        nodei = S("nodei", [P, N], I32)
        d_seq = S("d_seq", [P, NCH], I32)
        d_next = S("d_next", [P, NCH], I32)
        d_rows = S("d_rows", [80, 4, P], I32)
        s_rows = S("s_rows", [80, 4, P], I32)
        d_rowf = S("d_rowf", [80, 4, P], F32)
        s_rowf = S("s_rowf", [80, 4, P], F32)
        junk = S("junk", [P, NCH], F32)
        counts = S("counts", [P, 12], F32)
        tb = S("tb", [1, 16, 12], F32)
        step_id = S("step_id", [1, FAST], I32)
        pairs = S("pairs", [1, FAST, 9], F32)
        S = Region(R_CONST + 3072)
        tabj = S("tabj", [1, FAST + FULL], I32)
        tabc = S("tabc", [1, FAST + FULL], I32)

        L = Region(R_SLAB)
        xin = L("xin", [P, 2, D], F32)
        xn = L("xn", [P, 2, D], F32)
        xsum = L("xsum", [P, 2, D], F32)

        L = Region(R_SLAB)
        w_raw = L("w_raw", [128, 2, KT, 128], F32)
        w_hi = L("w_hi", [128, 2, KT, 128], F32R)
        w_lo = L("w_lo", [128, 2, KT, 128], F32R)
        W = Region(R_WORK)
        yT = W("yT", [128, N], F32)
        self_part = W("self_part", [128, N], F32)
        dinv_row = W("dinv_row", [128, N], F32)
        y_hi = W("y_hi", [P, NT, 128], F32R)
        y_lo = W("y_lo", [P, NT, 128], F32R)
        L = Region(R_ACC)
        layer_out = L("layer_out", [128, N], F32)
        x_slab = L("x_slab", [P, NT, 128], F32)
        x2_slab = L("x2_slab", [P, NT, 128], F32)
        h_in = Region(R_ACC + 5024)("h_in", [128, 2, N], F32)
        L = Region(R_ACC)
        acc_row = Region(R_SLAB + 8192)("acc_row", [P, 2, N], F32)
        hidden = Region(R_ACC + 5024)("hidden", [128, 2, N], F32)

        S = Region(R_CONST + 3072)
        rb2b = S("rb2b", [P, NX], F32)
        eb1c = S("eb1c", [128, NX * HK], F32)
        ids_i = S("ids_i", [128, NS * SUB], I32)
        id_now = S("id_now", [128, 2, SUB], I32)
        slot_now = S("slot_now", [P, 2, TOP], I32)
        sloti = S("sloti", [P, TOP, NT], I32)
        weight = S("weight", [P, TOP, NT], F32)
        step_x = S("step_x", [1, NS], I32)
        taken = S("taken", [P, NX], F32)
        S = Region(R_WORK)
        before = S("before", [P, P], F32)
        below = S("below", [P, NX, NX], F32)
        toki = S("toki", [P, NT], I32)
        seqi = S("seqi", [P, 128], I32)
        tokf = S("tokf", [P, NT], F32)
        seqf = S("seqf", [P, 128], F32)
        peak = S("peak", [P, NT], F32)
        less = S("less", [P, NT, NX], F32)
        rank = S("rank", [P, NT, NX], F32)
        sel = S("sel", [P, NT, NX], F32)
        cum = S("cum", [P, NT, NX], F32)
        cmpa = S("cmpa", [P, NT, NX, NX], F32)
        cmpb = S("cmpb", [P, NT, NX, NX], F32)
        steps = S("steps", [P, NX], F32)
        first = S("first", [P, NX], F32)
        slotf = S("slotf", [P, TOP, NT], F32)
        block_ = S("block_", [P, TOP, NT], F32)
        step_past = S("step_past", [1, NS, NX - 1], F32)
        step_f = S("step_f", [1, NS], F32)
        place_hot = S("place_hot", [P, TOP * NT, 128], F16)
        block_hot = S("block_hot", [P, TOP * NT, NS * SUB], F16)

        S = Region(R_H)
        w1_raw = S("w1_raw", [128, 2, KT, HID], F32)
        w1_hi = S("w1_hi", [128, 2, KT, HID], F32R)
        w1_lo = S("w1_lo", [128, 2, KT, HID], F32R)
        w2_raw = S("w2_raw", [128, 2, HK, D], F32)
        w2_hi = S("w2_hi", [128, 2, HK, D], F32R)
        w2_lo = S("w2_lo", [128, 2, HK, D], F32R)
        x_rows = S("x_rows", [128, 2, SUB, D], F32)
        xt_hi = S("xt_hi", [128, 2, KT, M], F32R)
        xt_lo = S("xt_lo", [128, 2, KT, M], F32R)
        hid = S("hid", [128, 2, HK, M], F32)
        hid_hi = S("hid_hi", [128, 2, HK, M], F32R)
        hid_lo = S("hid_lo", [128, 2, HK, M], F32R)
        assert S.at <= R_WORK
        S = Region(R_WORK)
        o_rows = S("o_rows", [128, 2, SUB, D], F32)
        b2_row = S("b2_row", [128, 2, D], F32)
        assert S.at <= R_CONST
        S = Region(R_H)
        pick = S("pick", [P, 2, TOP, D], F32)
        r_rows = S("r_rows", [P, 2, D], F32)
        y_rows = S("y_rows", [P, 2, D], F32)

        ps = ctx.enter_context(nc.psum_tensor("ps", [128, 8, 512], F32))

        o_d = nc.dram_tensor("o_d", (NS * M, D), F32, kind="Internal").ap()
        h1_d = nc.dram_tensor("h1_d", (KT, 128, N), F32, kind="Internal").ap()
        x2_d = nc.dram_tensor("x2_d", (N, D), F32, kind="Internal").ap()
        t_d = nc.dram_tensor("t_d", (N, D), F32, kind="Internal").ap()
        r_d = nc.dram_tensor("r_d", (N, D), F32, kind="Internal").ap()

        s_id = sem("s_id")
        s_rb2 = sem("s_rb2")
        s_ones = sem("s_ones")
        s_none = sem("s_none")
        s_small = [sem(f"s_small{i}") for i in range(6)]

        def wait_apart(e, sem, value):
            e.wait_ge(sem, value)
            e.sem_inc(s_none, 1)

        @on("gpsimd")
        def _(e):
            e.memset(ident[:], 0.0).then_inc(s_id, 1)
            e.wait_ge(s_id, 1)
            e.affine_select(out=ident[:], in_=ident[:], compare_op=ALU.not_equal, fill=1.0, base=0,
                            pattern=[[-1, 128]], channel_multiplier=1).then_inc(s_id, 1)
            e.memset(ones[:], 1.0).then_inc(s_ones, 1)
            e.memset(epst[:], EPS).then_inc(s_ones, 1)

        @on("sync")
        def _(e):
            e.dma_start(s_rows[:], I["src"].rearrange("(t p n) -> p t n", p=80, n=P)).then_inc(s_small[1], 16)
            for b, name in enumerate(("L0_gnn_b0", "L0_gnn_b1", "L0_ffn_rb1")):
                e.dma_start(bias[:, b, :], I[name].rearrange("(k p) -> p k", p=128),
                            allow_slow_non_contiguous=True).then_inc(s_small[3 + b], 16)

        s_seq = sem("s_seq")
        s_next = sem("s_next")
        s_tb = sem("s_tb")
        s_iota = sem("s_iota")
        s_ecast = sem("s_ecast")
        s_etp = sem("s_etp")
        s_ecol = sem("s_ecol")
        s_cnt = sem("s_cnt")
        s_tab = sem("s_tab")
        s_dn = sem("s_dn")

        @on("scalar")
        def _(e):
            e.dma_start(d_seq[:], I["dst"].rearrange("(p n) -> p n", p=P)).then_inc(s_seq, 16)
            e.wait_ge(s_dn, 1)
            e.dma_start(d_next[0:P - 1, :], I["dst"][1:1 + (P - 1) * NCH].rearrange("(p n) -> p n", p=P - 1)).then_inc(s_next, 16)
            e.dma_start(d_next[P - 1:P, 0:NCH - 1], I["dst"][1 + (P - 1) * NCH:E].rearrange("(p n) -> p n", p=1)).then_inc(s_next, 16)
            e.dma_start(d_rows[:], I["dst"].rearrange("(t p n) -> p t n", p=80, n=P)).then_inc(s_small[0], 16)

        @on("gpsimd")
        def _(e):
            e.memset(d_next[:], 1 << 20).then_inc(s_dn, 1)
            e.iota(nodei[:], [[1, N]], base=0, channel_multiplier=0).then_inc(s_iota, 1)
            e.wait_ge(s_iota, 1)
            e.tensor_copy(node16[:], nodei[:]).then_inc(s_iota, 1)
            e.iota(step_id[:], [[1, FAST]], base=0, channel_multiplier=0).then_inc(s_iota, 1)
            e.iota(tabj[:, FAST:], [[1, NT], [0, NCH // G]], base=0, channel_multiplier=0).then_inc(s_iota, 1)
            e.iota(tabc[:, FAST:], [[0, NT], [G, NCH // G]], base=0, channel_multiplier=0).then_inc(s_iota, 1)
            e.memset(dcol[:, NCH:], -1.0).then_inc(s_iota, 1)
            e.memset(scol[:, NCH:], -1.0).then_inc(s_iota, 1)

        @on("vector")
        def _(e):
            e.wait_ge(s_small[0], 16)
            e.tensor_copy(d_rowf[:], d_rows[:]).then_inc(s_ecast, 1)
            e.wait_ge(s_small[1], 16)
            e.tensor_copy(s_rowf[:], s_rows[:]).then_inc(s_ecast, 1)
            e.wait_ge(s_seq, 16)
            for j in range(NT + 1):
                if j:
                    e.wait_ge(s_cnt, j)
                e.tensor_scalar(junk[:], d_seq[:], float(P * j), None, ALU.is_lt, ALU.add,
                                accum_out=counts[:, j:j + 1]).then_inc(s_cnt, 1)
            e.wait_ge(s_next, 32)
            e.wait_ge(s_cnt, NT + 1)
            e.tensor_tensor(junk[:], d_seq[:], d_next[:], ALU.is_gt).then_inc(s_cnt, 1)
            e.wait_ge(s_cnt, NT + 2)
            e.tensor_reduce(counts[:, NT + 1:NT + 2], junk[:], AX.X, ALU.add).then_inc(s_cnt, 1)
            e.wait_ge(s_etp, 1)
            e.tensor_copy(dcol[:, 0:NCH], ps[0:P, 0, 0:NCH]).then_inc(s_ecol, 1)
            e.wait_ge(s_etp, 2)
            e.tensor_copy(scol[:, 0:NCH], ps[0:P, 1, 0:NCH]).then_inc(s_ecol, 1)
            n = [0]

            def link(ins):
                n[0] += 1
                ins.then_inc(s_tb, 1)
                e.wait_ge(s_tb, n[0])

            row = {k: tb[:, i, :] for i, k in enumerate(("b", "c0", "e0", "n", "S", "o", "D", "r", "q"))}
            e.wait_ge(s_etp, 3)
            link(e.tensor_copy(row["b"], ps[0:1, 2, 0:12]))
            b = row["b"]
            rnd = lambda ap: link(e.tensor_scalar(ap, ap, ROUND, ROUND, ALU.add, ALU.subtract))
            link(e.tensor_scalar(row["c0"][:, 0:NT], b[:, 0:NT], 1.0 / P, 0.5 / P - 0.5, ALU.mult, ALU.add))
            rnd(row["c0"][:, 0:NT])
            link(e.tensor_scalar(row["e0"][:, 0:NT], b[:, 1:NT + 1], 1.0 / P, 0.5 - 0.5 / P, ALU.mult, ALU.add))
            rnd(row["e0"][:, 0:NT])
            link(e.tensor_tensor(row["n"][:, 0:NT], row["e0"][:, 0:NT], row["c0"][:, 0:NT], ALU.subtract))
            link(e.tensor_scalar(row["n"][:, 0:NT], row["n"][:, 0:NT], 1.0 / G, 0.5 - 0.5 / G, ALU.mult, ALU.add))
            rnd(row["n"][:, 0:NT])
            link(e.memset(row["S"], 0.0))
            for j in range(1, NT):
                link(e.tensor_tensor(row["S"][:, j:j + 1], row["S"][:, j - 1:j], row["n"][:, j - 1:j], ALU.add))
            link(e.tensor_scalar(row["o"][:, 0:NT], row["S"][:, 0:NT], -float(G), None, ALU.mult))
            link(e.tensor_tensor(row["o"][:, 0:NT], row["o"][:, 0:NT], row["c0"][:, 0:NT], ALU.add))
            link(e.tensor_tensor(row["D"][:, 0:NT - 1], row["o"][:, 1:NT], row["o"][:, 0:NT - 1], ALU.subtract))
            e.wait_ge(s_iota, 7)
            ids = step_id[:].rearrange("a (s t) -> a s t", t=1).to_broadcast([1, FAST, NT - 1])
            over = lambda r: r.rearrange("a (s t) -> a s t", s=1).to_broadcast([1, FAST, NT - 1])
            link(e.tensor_tensor(pairs[:], over(row["S"][:, 1:NT]), ids, ALU.is_le))
            jf = junk[0:1, 0:FAST]
            cf = junk[0:1, 64:64 + FAST]
            link(e.tensor_reduce(jf, pairs[:], AX.X, ALU.add))
            link(e.tensor_copy(tabj[:, 0:FAST], jf))
            link(e.tensor_tensor(pairs[:], pairs[:], over(row["D"][:, 0:NT - 1]), ALU.mult))
            link(e.tensor_reduce(cf, pairs[:], AX.X, ALU.add))
            link(e.scalar_tensor_tensor(out=cf, in0=step_id[:], scalar=float(G), in1=cf, op0=ALU.mult, op1=ALU.add))
            link(e.tensor_scalar(tabc[:, 0:FAST], cf, float(NCH), None, ALU.min))
            e.tensor_scalar(flagi[:, 0:1], b[:, NT + 1:NT + 2], 0.0, None, ALU.is_equal).then_inc(s_tab, 1)

        @on("tensor")
        def _(e):
            e.wait_ge(s_id, 2)
            for i, rows in enumerate((d_rowf, s_rowf)):
                e.wait_ge(s_ecast, i + 1)
                for t in range(4):
                    mm = e.transpose(ps[0:P, i, 80 * t:80 * t + 80], rows[:, t, :], ident[0:80, 0:80])
                mm.then_inc(s_etp, 1)
            e.wait_ge(s_ones, 1)
            e.wait_ge(s_cnt, NT + 3)
            e.matmul(ps[0:1, 2, 0:12], ones[0:P, 0:1], counts[:], start=True, stop=True).then_inc(s_etp, 1)

        def layer_norm(tag, src, free, t_out=None, r_out=None):
            x_in = [sem(f"{tag}_in{u}") for u in range(2)]
            st = sem(f"{tag}_st")
            sq = sem(f"{tag}_sq")
            xr = sem(f"{tag}_xr")
            tp = sem(f"{tag}_tp")
            hi = sem(f"{tag}_hi")
            lo = sem(f"{tag}_lo")
            sm = sem(f"{tag}_sm")
            t_st = [sem(f"{tag}_ts{u}") for u in range(2)]
            r_st = [sem(f"{tag}_rs{u}") for u in range(2)]

            @on("sync")
            def _(e):
                free(e)
                e.sem_inc(xr, 2)
                if t_out is not None:
                    e.sem_inc(sm, 2)

                def load(i, u, q):
                    e.wait_ge(xr, i + 1)
                    if t_out is not None:
                        e.wait_ge(sm, i + 1)
                    e.dma_start(xin[:, u, :], src[ds(i * P, P), :]).then_inc(x_in[u], 16)

                def store(i, u, q):
                    if t_out is None:
                        return
                    e.wait_ge(xr, i + 3)
                    e.dma_start(t_out[ds(i * P, P), :], xn[:, u, :]).then_inc(t_st[u], 16)
                    e.wait_ge(sm, i + 3)
                    e.dma_start(r_out[ds(i * P, P), :], xsum[:, u, :]).then_inc(r_st[u], 16)

                skewed(e, NT, load, store)

            @on("vector")
            def _(e):
                free(e)

                def head(i, u, q):
                    e.wait_ge(x_in[u], 16 * q + 16)
                    for g in range(2):
                        mm = e.bn_stats(stats[:, u, g, :], xin[:, u, 512 * g:512 * g + 512])
                    mm.then_inc(st, 1)
                    wait_apart(e, st, 4 * i + 1)
                    e.bn_aggr(mv[:, u, :], stats[:, u, :, :].rearrange("p a b -> p (a b)")).then_inc(st, 1)
                    e.wait_ge(sq, i + 1)
                    e.reciprocal(rstd[:, u, 1:2], rstd[:, u, 0:1]).then_inc(st, 1)
                    e.wait_ge(st, 4 * i + 3)
                    e.scalar_tensor_tensor(out=rstd[:, u, 2:3], in0=mv[:, u, 0:1], scalar=-1.0,
                                           in1=rstd[:, u, 1:2], op0=ALU.mult, op1=ALU.mult).then_inc(st, 1)

                def tail(i, u, q):
                    for g in range(2):
                        e.wait_ge(hi, 2 * i + g + 1)
                        cols = ps[:, 6 + g, 0:4 * P].rearrange("p (k n) -> p k n", k=4)
                        e.tensor_tensor(h_lo[:, 4 * g:4 * g + 4, ds(i * P, P)], cols,
                                        h_hi[:, 4 * g:4 * g + 4, ds(i * P, P)].bitcast(F32), ALU.subtract).then_inc(lo, 1)

                skewed(e, NT, head, tail)

            @on("scalar")
            def _(e):
                e.wait_ge(s_ones, 2)
                free(e)

                def head(i, u, q):
                    e.wait_ge(st, 4 * i + 2)
                    e.activation(rstd[:, u, 0:1], mv[:, u, 1:2], ACT.Sqrt, bias=epst[0:P, :]).then_inc(sq, 1)
                    e.wait_ge(st, 4 * i + 4)
                    e.wait_ge(tp, 2 * i)
                    if t_out is not None:
                        e.wait_ge(t_st[u], 16 * q)
                        e.wait_ge(sm, i + 1)
                    e.activation(xn[:, u, :], xin[:, u, :], ACT.Identity, bias=rstd[:, u, 2:3],
                                 scale=rstd[:, u, 1:2]).then_inc(xr, 1)

                def tail(i, u, q):
                    for g in range(2):
                        wait_apart(e, tp, 2 * i + g + 1 + 2)
                        cols = ps[:, 6 + g, 0:4 * P].rearrange("p (k n) -> p k n", k=4)
                        e.activation(h_hi[:, 4 * g:4 * g + 4, ds(i * P, P)], cols, ACT.Copy).then_inc(hi, 1)

                skewed(e, NT, head, tail)

            if t_out is not None:
                @on("gpsimd")
                def _(e):
                    def head(i, u, q):
                        e.wait_ge(xr, i + 3)
                        e.wait_ge(r_st[u], 16 * q)
                        e.tensor_tensor(xsum[:, u, :], xin[:, u, :], xn[:, u, :], ALU.add).then_inc(sm, 1)
                    skewed(e, NT, head, lambda i, u, q: None)

            @on("tensor")
            def _(e):
                free(e)
                e.sem_inc(tp, 2)
                e.sem_inc(lo, 2)

                def head(i, u, q):
                    e.wait_ge(xr, i + 3)
                    for g in range(2):
                        e.wait_ge(lo, 2 * i + g + 1)
                        for k in range(4):
                            mm = e.transpose(ps[:, 6 + g, k * P:k * P + P],
                                             xn[:, u, 128 * (4 * g + k):128 * (4 * g + k + 1)], ident[0:P, 0:P])
                        mm.then_inc(tp, 1)
                skewed(e, NT, head, lambda i, u, q: None)
            return dict(lo=(lo, 2 * NT + 2), xr=(xr, NT + 2), t_st=t_st, r_st=r_st, hi=(hi, 2 * NT))

        ln0 = layer_norm("ln0", I["x"], lambda e: None)

        s_az = sem("s_az")
        s_acc = sem("s_acc")

        @on("gpsimd")
        def _(e):
            e.memset(acc[:], 0).then_inc(s_az, 1)

        POOL = 1

        hot = sem("hot")
        hotp = sem("hotp")
        prod = sem("prod")
        took = sem("took")
        copied = sem("copied")

        def adjacency(base, steps):
            def one_hots(e, u, c, which, done):
                for g in which:
                    ins = e.tensor_scalar(src_hot[:, u, g, :], node16[:], scol[:, ds(c + g, 1)], None, ALU.is_equal)
                ins.then_inc(done, 1)

            def vector(e):
                def head(s, u, q):
                    j = e.value_load(tabj[0:1, ds(base + s, 1)], min_val=0, max_val=NT - 1)
                    c = e.value_load(tabc[0:1, ds(base + s, 1)], min_val=0, max_val=NCH)
                    e.wait_ge(prod, s)
                    tile = node16[:, ds(j * P, P)].rearrange("p (g n) -> p g n", g=1).to_broadcast([P, G, P])
                    dst = dcol[:, ds(c, G)].rearrange("p (g n) -> p g n", n=1).to_broadcast([P, G, P])
                    e.tensor_tensor(dst_hot[:, u, :, :], tile, dst, ALU.is_equal)
                    one_hots(e, u, c, range(POOL, G), hot)

                def tail(s, u, q):
                    j = e.value_load(tabj[0:1, ds(base + s, 1)], min_val=0, max_val=NT - 1)
                    e.wait_ge(prod, s + 2)
                    e.wait_ge(took, s + 1)
                    for c, (a, w) in enumerate(COLS):
                        rows = acc[:, ds(j, 1), a:a + w].rearrange("p a n -> p (a n)")
                        ins = e.tensor_tensor(rows, ps[0:P, 3 * u + c, 0:w], rows, ALU.add)
                    ins.then_inc(took, 1)
                skewed(e, steps, head, tail)
                e.wait_ge(took, steps + 1)
                e.sem_inc(s_acc, 1)

            def gpsimd(e):
                def head(s, u, q):
                    c = e.value_load(tabc[0:1, ds(base + s, 1)], min_val=0, max_val=NCH)
                    wait_apart(e, prod, s)
                    e.tensor_copy(src_now[:, u, :], scol[:, ds(c, POOL)]).then_inc(copied, 1)
                    wait_apart(e, copied, s + 1)
                    for g in range(POOL):
                        ins = e.tensor_scalar(src_hot[:, u, g, :], node16[:], src_now[:, u, g:g + 1], None, ALU.is_equal)
                    ins.then_inc(hotp, 1)
                skewed(e, steps, head, lambda s, u, q: None)

            def tensor(e):
                e.sem_inc(prod, 1)
                e.sem_inc(took, 1)
                def head(s, u, q):
                    e.wait_ge(hot, s + 1)
                    e.wait_ge(hotp, s + 1)
                    e.wait_ge(took, s)
                    for g in range(G):
                        for c, (a, w) in enumerate(COLS):
                            mm = e.matmul(ps[0:P, 3 * u + c, 0:w], dst_hot[:, u, g, :], src_hot[:, u, g, a:a + w],
                                          start=(g == 0), stop=(g == G - 1))
                    mm.then_inc(prod, 1)
                skewed(e, steps, head, lambda s, u, q: None)
            return dict(vector=vector, gpsimd=gpsimd, tensor=tensor)

        fast, full = adjacency(0, FAST), adjacency(FAST, FULL)

        def both(engine):
            @on(engine)
            def _(e):
                e.wait_ge(s_tab, 1)
                e.wait_ge(s_ecol, 2)
                e.wait_ge(s_iota, 7)
                e.wait_ge(s_az, 1)
                flag = e.value_load(flagi[0:1, 0:1], min_val=0, max_val=1)
                with e.If(flag):
                    fast[engine](e)
                with e.Else():
                    full[engine](e)
        for engine in ("vector", "gpsimd", "tensor"):
            both(engine)

        s_row = sem("s_row")
        s_turn = sem("s_turn")
        s_adj = sem("s_adj")
        s_dinv = sem("s_dinv")
        s_dmm = sem("s_dmm")
        s_drow = sem("s_drow")
        GROUPS = ((0, 4), (4, 4), (8, 2))

        @on("scalar")
        def _(e):
            e.wait_ge(s_acc, 1)

            def head(j, u, q):
                wait_apart(e, s_turn, 3 * j)
                e.activation(acc_row[:, u, :], acc[:, ds(j, 1), :].rearrange("p a n -> p (a n)"), ACT.Copy,
                             accum_out=deg[:, ds(j, 1)]).then_inc(s_row, 1)
            skewed(e, NT, head, lambda j, u, q: None)
            for g, (t, n) in enumerate(GROUPS):
                e.wait_ge(s_dmm, g + 1)
                e.activation(dinv_row[:, P * t:P * (t + n)], ps[:, g, 0:P * n], ACT.Copy).then_inc(s_drow, 1)

        @on("tensor")
        def _(e):
            e.sem_inc(s_turn, 3)
            e.sem_inc(s_adj, 6)

            def head(j, u, q):
                e.wait_ge(s_row, j + 1)
                for g, (t, n) in enumerate(GROUPS):
                    e.wait_ge(s_adj, 3 * j + g + 1)
                    for i in range(n):
                        mm = e.transpose(ps[0:P, 3 * u + g, P * i:P * i + P],
                                         acc_row[:, u, P * (t + i):P * (t + i + 1)], ident[0:P, 0:P])
                    mm.then_inc(s_turn, 1)
            skewed(e, NT, head, lambda j, u, q: None)
            e.wait_ge(s_dinv, 2)
            e.wait_ge(s_adj, 3 * NT + 6)
            for g, (t, n) in enumerate(GROUPS):
                for i in range(n):
                    mm = e.matmul(ps[:, g, P * i:P * i + P], dinv[:, t + i:t + i + 1].to_broadcast([P, 128]),
                                  ident[0:P, 0:P], start=True, stop=True)
                mm.then_inc(s_dmm, 1)

        @on("vector")
        def _(e):
            def tail(j, u, q):
                for g, (t, n) in enumerate(GROUPS):
                    e.wait_ge(s_turn, 3 * j + g + 1 + 3)
                    e.tensor_copy(adj[:, t:t + n, ds(j * P, P)],
                                  ps[0:P, 3 * u + g, 0:P * n].rearrange("p (k n) -> p k n", k=n)).then_inc(s_adj, 1)
            skewed(e, NT, lambda j, u, q: None, tail)
            e.wait_ge(s_row, NT)
            e.tensor_scalar(deg[:], deg[:], 1.0, None, ALU.max).then_inc(s_dinv, 1)
            e.wait_ge(s_dinv, 1)
            e.reciprocal(dinv[:], deg[:]).then_inc(s_dinv, 1)

        def split_slab(e, u, loaded, value, done):
            wait_apart(e, loaded, value)
            e.tensor_copy(w_hi[:, u, :, :], w_raw[:, u, :, :]).then_inc(done, 1)

        def rest_slab(e, u, done, value):
            e.wait_ge(done, value)
            e.tensor_tensor(w_lo[:, u, :, :], w_raw[:, u, :, :], w_hi[:, u, :, :].bitcast(F32), ALU.subtract).then_inc(done, 1)

        def product(e, bank, u, wait, full):
            for c, (a, w) in enumerate(COLS):
                wait(c)
                passes = ((w_hi, h_hi), (w_hi, h_lo), (w_lo, h_hi))
                n = 0
                for k in range(KT):
                    for wt, ht in passes:
                        n += 1
                        mm = e.matmul(ps[:, bank + c, 0:w], wt[:, u, k, :], ht[:, k, a:a + w],
                                      start=(n == 1), stop=(n == 3 * KT))
                mm.then_inc(full, 1)

        def layer(tag, w_self, w_neigh, b, last, free, h_ready):
            x_full = sem(f"{tag}_xfull")
            x_free = sem(f"{tag}_xfree")
            z_full = sem(f"{tag}_zfull")
            own_out = sem(f"{tag}_ownout")
            agg_out = sem(f"{tag}_aggout")
            t_full = sem(f"{tag}_tfull")
            t_hi = sem(f"{tag}_thi")
            t_free = sem(f"{tag}_tfree")
            w_in = [sem(f"{tag}_win{u}") for u in range(2)]
            w_ok = [sem(f"{tag}_wok{u}") for u in range(2)]
            sp_free = sem(f"{tag}_spfree")
            u_done = sem(f"{tag}_udone")
            x_in = sem(f"{tag}_xin")
            st = sem(f"{tag}_st")
            x2_ok = sem(f"{tag}_x2ok")
            T = 6 if last else 3
            view = lambda w: w.rearrange("(k p) n -> p k n", p=128)
            nat = lambda a: a.rearrange("(t p) n -> p t n", p=P)
            x_view, x2_view = nat(I["x"]), nat(x2_d)

            @on("sync")
            def _(e):
                free(e)
                with e.Fori(0, KT) as m:
                    for u, w in enumerate((w_neigh, w_self)):
                        e.wait_ge(w_ok[u], 2 * m)
                        e.dma_start(w_raw[:, u, :, :], view(w)[:, :, ds(m * 128, 128)]).then_inc(w_in[u], 16)

            @on("gpsimd")
            def _(e):
                free(e)
                with e.Fori(0, KT) as m:
                    for u, full, n in ((0, x_full, 3), (1, z_full, 6)):
                        e.wait_ge(full, n * m)
                        split_slab(e, u, w_in[u], 16 * m + 16, w_ok[u])
                        rest_slab(e, u, w_ok[u], 2 * m + 1)

            @on("tensor")
            def _(e):
                free(e)
                h_ready(e)
                e.sem_inc(x_free, 3)
                e.sem_inc(agg_out, 3)

                def neigh(m):
                    e.wait_ge(w_ok[0], 2 * m + 2)
                    product(e, 0, 0, lambda c: e.wait_ge(x_free, 3 * m + c + 1), x_full)

                def own(m):
                    e.wait_ge(w_ok[1], 2 * m + 2)
                    product(e, 3, 1, lambda c: e.wait_ge(agg_out, 3 * m + c + 1), z_full)

                def turn(n0, source, partitions, width):
                    for g, (t, n) in enumerate(GROUPS):
                        e.wait_ge(t_free, n0 + g // 2)
                        for i in range(n):
                            mm = e.transpose(ps[0:P, 6 + g % 2, 128 * i:128 * i + 128],
                                             source[:, P * (t + i):P * (t + i + 1)], ident[:])
                        mm.then_inc(t_full, 1)

                def aggregate(m):
                    e.wait_ge(t_free, T * m + 3)
                    for c, (a, w) in enumerate(COLS):
                        e.wait_ge(own_out, 3 * m + c + 1)
                        n = 0
                        for k in range(NT):
                            for y in (y_hi, y_lo):
                                n += 1
                                mm = e.matmul(ps[:, 3 + c, 0:w], y[:, k, :], adj[:, k, a:a + w],
                                              start=(n == 1), stop=(n == 2 * NT))
                        mm.then_inc(z_full, 1)

                def back(m):
                    e.wait_ge(u_done, 3 * m + 3)
                    turn(T * m + 3, layer_out, 128, P)

                def step(m, first=False, final=False):
                    own(m)
                    if last and not first:
                        back(m - 1)
                    e.wait_ge(x_free, 3 * m + 6)
                    turn(T * m, yT, 128, P)
                    if not final:
                        neigh(m + 1)
                    aggregate(m)

                neigh(0)
                step(0, first=True)
                with e.Fori(1, KT - 1) as m:
                    step(m)
                step(KT - 1, final=True)
                if last:
                    back(KT - 1)

            @on("scalar")
            def _(e):
                e.wait_ge(s_small[3 + b], 16)
                free(e)
                e.sem_inc(sp_free, 3)

                def neigh(m):
                    for c, (a, w) in enumerate(COLS):
                        e.wait_ge(x_full, 3 * m + c + 1)
                        e.activation(yT[:, a:a + w], ps[:, c, 0:w], ACT.Copy).then_inc(x_free, 1)

                def own(m):
                    for c, (a, w) in enumerate(COLS):
                        e.wait_ge(z_full, 6 * m + c + 1)
                        wait_apart(e, sp_free, 3 * m + c + 1)
                        e.activation(self_part[:, a:a + w], ps[:, 3 + c, 0:w], ACT.Identity,
                                     bias=bias[:, b, ds(m, 1)]).then_inc(own_out, 1)

                def high(m):
                    for g, (t, n) in enumerate(GROUPS):
                        e.wait_ge(t_full, T * m + g + 1)
                        e.activation(y_hi[:, t:t + n, :], ps[0:P, 6 + g % 2, 0:128 * n].rearrange("p (k n) -> p k n", k=n),
                                     ACT.Copy).then_inc(t_hi, 1)

                def store(m):
                    if not last:
                        e.wait_ge(u_done, 3 * m + 3)
                        e.dma_start(h1_d[ds(m, 1), :, :].rearrange("a p n -> p (a n)"), layer_out[:]).then_inc(st, 16)
                    else:
                        e.wait_ge(x2_ok, 3 * m + 3)
                        e.dma_start(x2_view[:, :, ds(m * 128, 128)], x2_slab[:]).then_inc(st, 16)

                def fetch(m):
                    if last:
                        e.dma_start(x_slab[:], x_view[:, :, ds(m * 128, 128)]).then_inc(x_in, 16)

                def step(m, first=False, final=False):
                    own(m)
                    if not last and not first:
                        store(m - 1)
                    high(m)
                    if not final:
                        neigh(m + 1)
                    if last and not first:
                        store(m - 1)
                    fetch(m)

                neigh(0)
                step(0, first=True)
                with e.Fori(1, KT - 1) as m:
                    step(m)
                step(KT - 1, final=True)
                store(KT - 1)

            @on("vector")
            def _(e):
                free(e)

                def low(m):
                    for g, (t, n) in enumerate(GROUPS):
                        e.wait_ge(t_hi, 3 * m + g + 1)
                        e.tensor_tensor(y_lo[:, t:t + n, :], ps[0:P, 6 + g % 2, 0:128 * n].rearrange("p (k n) -> p k n", k=n),
                                        y_hi[:, t:t + n, :].bitcast(F32), ALU.subtract).then_inc(t_free, 1)

                def total(m):
                    if not last:
                        e.wait_ge(st, 16 * m)
                    for c, (a, w) in enumerate(COLS):
                        e.wait_ge(z_full, 6 * m + 3 + c + 1)
                        e.tensor_tensor(layer_out[:, a:a + w], ps[:, 3 + c, 0:w], dinv_row[:, a:a + w], ALU.mult).then_inc(agg_out, 1)
                        e.wait_ge(agg_out, 3 * m + c + 1 + 3)
                        e.tensor_tensor(layer_out[:, a:a + w], layer_out[:, a:a + w], self_part[:, a:a + w], ALU.add)\
                            .then_inc(u_done, 1)
                        e.wait_ge(u_done, 3 * m + c + 1)
                        e.sem_inc(sp_free, 1)

                def residual(m):
                    e.wait_ge(x_in, 16 * m + 16)
                    e.wait_ge(st, 16 * m)
                    for g, (t, n) in enumerate(GROUPS):
                        e.wait_ge(t_full, T * m + 3 + g + 1)
                        e.tensor_tensor(x2_slab[:, t:t + n, :], ps[0:P, 6 + g % 2, 0:128 * n].rearrange("p (k n) -> p k n", k=n),
                                        x_slab[:, t:t + n, :], ALU.add).then_inc(x2_ok, 1)
                        e.wait_ge(x2_ok, 3 * m + g + 1)
                        e.sem_inc(t_free, 1)

                def step(m, first=False):
                    if last and not first:
                        residual(m - 1)
                    low(m)
                    total(m)

                step(0, first=True)
                with e.Fori(1, KT) as m:
                    step(m)
                if last:
                    residual(KT - 1)
            return dict(st=(st, 16 * KT), z_full=(z_full, 6 * KT), t_free=(t_free, T * KT), w_ok=w_ok)

        def turned(e):
            e.wait_ge(ln0["lo"][0], ln0["lo"][1])
            e.wait_ge(s_drow, 3)

        l0 = layer("l0", I["L0_gnn_W_self0"], I["L0_gnn_W_neigh0"], 0, False, turned, lambda e: None)

        h_got = [sem(f"h_got{u}") for u in range(2)]
        h_h = sem("h_h")
        h_l = sem("h_l")

        @on("sync")
        def _(e):
            e.wait_ge(*l0["st"])
            e.sem_inc(h_l, 2)

            def head(k, u, q):
                e.wait_ge(h_l, k + 1)
                e.dma_start(h_in[:, u, :], h1_d[ds(k, 1), :, :].rearrange("a p n -> p (a n)")).then_inc(h_got[u], 16)
            skewed(e, KT, head, lambda k, u, q: None)

        @on("scalar")
        def _(e):
            e.wait_ge(*l0["z_full"])
            def head(k, u, q):
                wait_apart(e, h_got[u], 16 * q + 16)
                e.activation(h_hi[:, ds(k, 1), :].rearrange("p a n -> p (a n)"), h_in[:, u, :], ACT.Relu).then_inc(h_h, 1)
            skewed(e, KT, head, lambda k, u, q: None)

        @on("vector")
        def _(e):
            def head(k, u, q):
                e.wait_ge(h_h, k + 1)
                row = lambda t: t[:, ds(k, 1), :].rearrange("p a n -> p (a n)")
                e.scalar_tensor_tensor(out=row(h_lo), in0=h_in[:, u, :], scalar=0.0, in1=row(h_hi).bitcast(F32),
                                       op0=ALU.max, op1=ALU.subtract).then_inc(h_l, 1)
            skewed(e, KT, head, lambda k, u, q: None)

        def relued(e):
            e.wait_ge(h_l, KT + 2)

        l1 = layer("l1", I["L0_gnn_W_self1"], I["L0_gnn_W_neigh1"], 1, True,
                   lambda e: (e.wait_ge(*l0["z_full"]), e.wait_ge(*l0["st"])), relued)

        ln2 = layer_norm("ln2", x2_d, lambda e: e.wait_ge(*l1["st"]), t_d, r_d)

        r_in = [sem(f"r_in{u}") for u in range(2)]
        r_ok = sem("r_ok")
        r_full = sem("r_full")
        r_hid = sem("r_hid")
        r_log = sem("r_log")
        r_zero = sem("r_zero")
        rw1_view = I["L0_ffn_rw1"].rearrange("(k p) n -> p k n", p=128)

        def normed(e):
            e.wait_ge(*ln2["lo"])
            for u in range(2):
                e.wait_ge(ln2["t_st"][u], 16 * (NT // 2))
                e.wait_ge(ln2["r_st"][u], 16 * (NT // 2))

        @on("sync")
        def _(e):
            e.dma_start(rw2[:], I["L0_ffn_rw2"].rearrange("(k p) n -> p k n", p=128)).then_inc(s_small[2], 16)
            normed(e)
            e.sem_inc(r_ok, 4)

            def head(m, u, q):
                e.wait_ge(r_ok, 2 * m + 2)
                e.dma_start(w_raw[:, u, :, :], rw1_view[:, :, ds(m * 128, 128)]).then_inc(r_in[u], 16)
            skewed(e, KT, head, lambda m, u, q: None)

        @on("gpsimd")
        def _(e):
            normed(e)

            def head(m, u, q):
                e.wait_ge(r_full, 3 * m)
                split_slab(e, u, r_in[u], 16 * q + 16, r_ok)
                rest_slab(e, u, r_ok, 2 * m + 1 + 4)
            skewed(e, KT, head, lambda m, u, q: None)

        @on("tensor")
        def _(e):
            normed(e)
            e.wait_ge(s_small[2], 16)
            e.sem_inc(r_full, 3)
            e.sem_inc(r_hid, 6)
            e.wait_ge(r_zero, 1)
            e.matmul(ps[0:P, 6, 0:NT * NX], hidden[:, 0, 0:P], hidden[:, 0, 0:NT * NX], start=True, stop=True,
                     skip_group_check=True).then_inc(r_zero, 1)

            def head(m, u, q):
                e.wait_ge(r_ok, 2 * m + 2 + 4)
                product(e, 3 * u, u, lambda c: e.wait_ge(r_hid, 3 * m + c + 1), r_full)

            def tail(m, u, q):
                e.wait_ge(r_hid, 3 * m + 3 + 6)
                for i in range(NT):
                    mm = e.matmul(ps[0:P, 6, NX * i:NX * i + NX], hidden[:, u, P * i:P * i + P],
                                  rw2[:, ds(m, 1), :].rearrange("p a n -> p (a n)"), start=False, stop=True,
                                  skip_group_check=True)
                mm.then_inc(r_log, 1)
            skewed(e, KT, head, tail)

        @on("scalar")
        def _(e):
            e.wait_ge(s_small[5], 16)
            normed(e)
            e.sem_inc(r_log, 2)

            def head(m, u, q):
                e.wait_ge(r_log, m + 1)
                for c, (a, w) in enumerate(COLS):
                    wait_apart(e, r_full, 3 * m + c + 1 + 3)
                    e.activation(hidden[:, u, a:a + w], ps[:, 3 * u + c, 0:w], ACT.Silu, bias=bias[:, 2, ds(m, 1)])\
                        .then_inc(r_hid, 1)
            e.wait_ge(r_zero, 2)
            skewed(e, KT, head, lambda m, u, q: None)

        @on("vector")
        def _(e):
            normed(e)
            e.memset(hidden[:, 0, :], 0.0).then_inc(r_zero, 1)
            e.wait_ge(r_log, KT + 2)

        g_c = sem("g_c")
        g_v = sem("g_v")
        g_ls = sem("g_ls")
        g_ex = sem("g_ex")
        g_r = sem("g_r")
        g_cnt = sem("g_cnt")
        g_hot = sem("g_hot")
        g_ids = sem("g_ids")
        g_ok = sem("g_ok")
        g_eb = sem("g_eb")

        @on("sync")
        def _(e):
            e.dma_start(rb2b[:], I["L0_ffn_rb2"].partition_broadcast(P)).then_inc(s_rb2, 16)
            e.dma_start(eb1c[:], I["L0_ffn_eb1"].rearrange("e (k p) -> p (e k)", p=128),
                        allow_slow_non_contiguous=True).then_inc(g_eb, 16)

        @on("gpsimd")
        def _(e):
            e.memset(below[:], 1.0).then_inc(g_c, 1)
            e.memset(before[:], 1.0).then_inc(g_c, 1)
            e.iota(toki[:], [[P, NT]], base=0, channel_multiplier=1).then_inc(g_c, 1)
            e.iota(seqi[:], [[1, 128]], base=0, channel_multiplier=0).then_inc(g_c, 1)
            e.wait_ge(g_c, 4)
            e.affine_select(out=below[:], in_=below[:], compare_op=ALU.is_gt, fill=0.0, base=0,
                            pattern=[[1, NX], [-1, NX]], channel_multiplier=0).then_inc(g_c, 1)
            e.affine_select(out=before[:], in_=before[:], compare_op=ALU.is_gt, fill=0.0, base=0,
                            pattern=[[1, P]], channel_multiplier=-1).then_inc(g_c, 1)
            e.tensor_copy(tokf[:], toki[:]).then_inc(g_c, 1)
            e.tensor_copy(seqf[:], seqi[:]).then_inc(g_c, 1)

        @on("vector")
        def _(e):
            n = [0]

            def link(ins):
                n[0] += 1
                ins.then_inc(g_v, 1)
                e.wait_ge(g_v, n[0])

            e.wait_ge(g_c, 8)
            e.wait_ge(s_rb2, 16)
            over = lambda ap, t: ap.rearrange("p (a n) -> p a n", a=1).to_broadcast([P, t, NX])
            each = lambda ap: ap.rearrange("p (t a) -> p t a", a=1).to_broadcast([P, NT, NX])
            link(e.tensor_tensor(logit[:], ps[0:P, 6, 0:NT * NX].rearrange("p (t n) -> p t n", n=NX), over(rb2b[:], NT), ALU.add))
            link(e.tensor_reduce(peak[:], logit[:], AX.X, ALU.max))
            e.tensor_tensor(less[:], logit[:], each(peak[:]), ALU.subtract).then_inc(g_ls, 1)
            lf = logit[:].rearrange("p t (a n) -> p t a n", a=1).to_broadcast([P, NT, NX, NX])
            le = logit[:].rearrange("p t (n a) -> p t n a", a=1).to_broadcast([P, NT, NX, NX])
            link(e.tensor_tensor(cmpa[:], lf, le, ALU.is_gt))
            link(e.tensor_tensor(cmpb[:], lf, le, ALU.is_ge))
            link(e.tensor_tensor(cmpb[:], cmpb[:],
                                 below[:].rearrange("p (a n) m -> p a n m", a=1).to_broadcast([P, NT, NX, NX]), ALU.mult))
            link(e.tensor_tensor(cmpa[:], cmpa[:], cmpb[:], ALU.max))
            link(e.tensor_reduce(rank[:], cmpa[:], AX.X, ALU.add))
            link(e.tensor_scalar(sel[:], rank[:], float(TOP - 1), None, ALU.is_le))
            e.tensor_reduce(taken[:], sel[:].rearrange("p t n -> p n t"), AX.X, ALU.add).then_inc(g_r, 1)
            e.wait_ge(g_ex, 1)
            link(e.tensor_tensor(less[:], less[:], sel[:], ALU.mult))
            link(e.tensor_reduce(peak[:], less[:], AX.X, ALU.add))
            link(e.reciprocal(peak[:], peak[:]))
            link(e.tensor_tensor(less[:], less[:], each(peak[:]), ALU.mult))
            e.wait_ge(g_cnt, 1)
            link(e.tensor_copy(cum[:, 0, :], ps[0:P, 7, 0:NX]))
            for t in range(1, NT):
                link(e.tensor_tensor(cum[:, t, :], cum[:, t - 1, :], sel[:, t - 1, :], ALU.add))
            link(e.tensor_scalar(steps[:], ps[0:P, 7, NX:2 * NX], 1.0 / M, 0.5 - 0.5 / M, ALU.mult, ALU.add))
            link(e.tensor_scalar(steps[:], steps[:], ROUND, ROUND, ALU.add, ALU.subtract))
            link(e.memset(first[:], 0.0))
            for x in range(1, NX):
                link(e.tensor_tensor(first[:, x:x + 1], first[:, x - 1:x], steps[:, x - 1:x], ALU.add))
            link(e.tensor_scalar(steps[:], first[:], float(M), None, ALU.mult))
            link(e.tensor_tensor(cum[:], cum[:], over(steps[:], NT), ALU.add))
            for c in range(TOP):
                link(e.tensor_scalar(sel[:], rank[:], float(c), None, ALU.is_equal))
                link(e.tensor_tensor(cmpa[:, :, 0, :], sel[:], cum[:], ALU.mult))
                link(e.tensor_tensor(cmpb[:, :, 0, :], sel[:], less[:], ALU.mult))
                link(e.tensor_reduce(slotf[:, c, :], cmpa[:, :, 0, :], AX.X, ALU.add))
                link(e.tensor_reduce(weight[:, c, :], cmpb[:, :, 0, :], AX.X, ALU.add))
            link(e.tensor_copy(sloti[:], slotf[:]))
            link(e.tensor_scalar(block_[:], slotf[:], 1.0 / 128, 0.5 / 128 - 0.5, ALU.mult, ALU.add))
            link(e.tensor_scalar(block_[:], block_[:], ROUND, ROUND, ALU.add, ALU.subtract))
            link(e.scalar_tensor_tensor(out=slotf[:], in0=block_[:], scalar=-128.0, in1=slotf[:], op0=ALU.mult, op1=ALU.add))
            flat = lambda t, w: t[:].rearrange("p c t -> p (c t)").rearrange("p (n a) -> p n a", a=1).to_broadcast([P, TOP * NT, w])
            row = lambda w: seqf[:, 0:w].rearrange("p (a n) -> p a n", a=1).to_broadcast([P, TOP * NT, w])
            link(e.tensor_tensor(place_hot[:], row(128), flat(slotf, 128), ALU.is_equal))
            link(e.tensor_tensor(block_hot[:], row(NS * SUB), flat(block_, NS * SUB), ALU.is_equal))
            for c in range(TOP):
                half = block_hot[:, c * NT:(c + 1) * NT, :]
                e.tensor_tensor(half, half, tokf[:].rearrange("p (n a) -> p n a", a=1).to_broadcast([P, NT, NS * SUB]),
                                ALU.mult).then_inc(g_hot, 1)
            ids = seqf[0:1, 0:NS].rearrange("p (n a) -> p n a", a=1).to_broadcast([1, NS, NX - 1])
            fst = first[0:1, 1:NX].rearrange("p (a n) -> p a n", a=1).to_broadcast([1, NS, NX - 1])
            link(e.tensor_tensor(step_past[:], fst, ids, ALU.is_le))
            link(e.tensor_reduce(step_f[:], step_past[:], AX.X, ALU.add))
            link(e.tensor_copy(step_x[:], step_f[:]))
            e.wait_ge(g_ids, 1)
            e.tensor_copy(ids_i[:], ps[:, 7, 64:64 + NS * SUB]).then_inc(g_ok, 1)

        @on("scalar")
        def _(e):
            e.wait_ge(g_ls, 1)
            e.activation(less[:], less[:], ACT.Exp).then_inc(g_ex, 1)

        @on("tensor")
        def _(e):
            e.wait_ge(g_r, 1)
            e.matmul(ps[0:P, 7, 0:NX], before[:], taken[:], start=True, stop=True, skip_group_check=True)
            e.matmul(ps[0:P, 7, NX:2 * NX], ones[0:P, 0:P], taken[:], start=False, stop=True,
                     skip_group_check=True).then_inc(g_cnt, 1)
            e.wait_ge(g_hot, 2)
            for i in range(TOP * NT):
                mm = e.matmul(ps[:, 7, 64:64 + NS * SUB], place_hot[:, i, :], block_hot[:, i, :],
                              start=(i == 0), stop=(i == TOP * NT - 1))
            mm.then_inc(g_ids, 1)

        m_win = [[sem(f"m_win{w}{u}") for u in range(2)] for w in range(2)]
        m_bin = [sem(f"m_bin{u}") for u in range(2)]
        m_whi = [sem(f"m_whi{w}") for w in range(2)]
        m_wlo = [sem(f"m_wlo{w}") for w in range(2)]
        m_idx = sem("m_idx")
        m_xin = [[sem(f"m_xin{u}{b}") for b in range(SUB)] for u in range(2)]
        m_tx = sem("m_tx")
        m_xhi = sem("m_xhi")
        m_xlo = sem("m_xlo")
        m_g1 = sem("m_g1")
        m_h = sem("m_h")
        m_hhi = sem("m_hhi")
        m_hlo = sem("m_hlo")
        m_g2 = sem("m_g2")
        m_out = sem("m_out")
        m_st = [sem(f"m_st{u}") for u in range(2)]
        NB = SUB * 2
        w1_view = I["L0_ffn_ew1"].rearrange("e (k p) h -> e p k h", p=128)
        w2_view = I["L0_ffn_ew2"].rearrange("e (k p) n -> e p k n", p=128)

        def gated(e):
            e.wait_ge(g_ok, 1)

        @on("sync")
        def _(e):
            gated(e)
            for w in range(2):
                e.sem_inc(m_wlo[w], 2)
            e.sem_inc(m_out, 2 * NB)

            def head(s, u, q):
                x = e.value_load(step_x[0:1, ds(s, 1)], min_val=0, max_val=NX - 1)
                for w, (raw, view) in enumerate(((w1_raw, w1_view), (w2_raw, w2_view))):
                    e.wait_ge(m_wlo[w], s + 1)
                    e.dma_start(raw[:, u], view[ds(x, 1)].rearrange("a p k n -> p (a k) n")).then_inc(m_win[w][u], 16)
                e.wait_ge(m_out, NB * s + NB)
                e.dma_start(b2_row[:, u, :], I["L0_ffn_eb2"][ds(x, 1), :].to_broadcast([128, D])).then_inc(m_bin[u], 16)
            skewed(e, NS, head, lambda s, u, q: None)

        @on("gpsimd")
        def _(e):
            gated(e)
            e.sem_inc(m_tx, 8)

            def head(s, u, q):
                wait_apart(e, m_tx, 4 * s + 4)
                e.tensor_copy(id_now[:, u, :], ids_i[:, ds(s * SUB, SUB)]).then_inc(m_idx, 1)
                wait_apart(e, m_idx, s + 1)
                for b in range(SUB):
                    e.indirect_dma_start(out=x_rows[:, u, b, :], out_offset=None, in_=t_d[:, :],
                                         in_offset=bass.IndirectOffsetOnAxis(ap=id_now[:, u, b:b + 1], axis=0)).then_inc(m_xin[u][b], 16)
            skewed(e, NS, head, lambda s, u, q: None)

        @on("tensor")
        def _(e):
            gated(e)
            e.sem_inc(m_xlo, 2)
            e.sem_inc(m_h, 2)
            e.sem_inc(m_g1, 4)
            e.sem_inc(m_g2, 2 * NB)

            def turn(s, u, q):
                for b in range(SUB):
                    e.wait_ge(m_xin[u][b], 16 * q + 16)
                for g in range(4):
                    e.wait_ge(m_xlo, 4 * s + g + 1)
                    for k in range(2):
                        for b in range(SUB):
                            mm = e.transpose(ps[:, g % 2, k * M + 128 * b:k * M + 128 * b + 128],
                                             x_rows[:, u, b, 128 * (2 * g + k):128 * (2 * g + k + 1)], ident[:])
                    mm.then_inc(m_tx, 1)

            def hidden_part(s, u, q):
                e.wait_ge(m_wlo[0], s + 3)
                e.wait_ge(m_xlo, 4 * s + 4 + 2)
                for j in range(HK):
                    e.wait_ge(m_h, HK * s + j + 1)
                    n = 0
                    for k in range(KT):
                        for wt, xt in ((w1_hi, xt_hi), (w1_hi, xt_lo), (w1_lo, xt_hi)):
                            n += 1
                            mm = e.matmul(ps[:, 2 + j, 0:M], wt[:, u, k, 128 * j:128 * j + 128], xt[:, u, k, :],
                                          start=(n == 1), stop=(n == 3 * KT))
                    mm.then_inc(m_g1, 1)

            def head(s, u, q):
                hidden_part(s, u, q)
                if not isinstance(s, int) or s < NS - 1:
                    turn(s + 1, 1 - u, q + u)

            def tail(s, u, q):
                e.wait_ge(m_hlo, s + 1)
                e.wait_ge(m_wlo[1], s + 3)
                for b in range(SUB):
                    for half in range(2):
                        e.wait_ge(m_out, NB * s + NB + 2 * b + half + 1)
                        n = 0
                        for j in range(HK):
                            for ht, wt in ((hid_hi, w2_hi), (hid_hi, w2_lo), (hid_lo, w2_hi)):
                                n += 1
                                mm = e.matmul(ps[:, 4 + 2 * b + half, :], ht[:, u, j, 128 * b:128 * b + 128],
                                              wt[:, u, j, 512 * half:512 * half + 512], start=(n == 1), stop=(n == 3 * HK))
                        mm.then_inc(m_g2, 1)
            turn(0, 0, 0)
            skewed(e, NS, head, tail)

        def more(s):
            return not isinstance(s, int) or s < NS - 1

        group = lambda t, u, g: t[:, u, 2 * g:2 * g + 2, :]
        bank = lambda g: ps[:, g % 2, :].rearrange("p (k n) -> p k n", k=2)

        @on("scalar")
        def _(e):
            gated(e)
            e.wait_ge(g_eb, 16)

            def w1(s, u, q):
                e.wait_ge(m_win[0][u], 16 * q + 16)
                e.wait_ge(m_g1, HK * s + HK)
                e.activation(w1_hi[:, u], w1_raw[:, u], ACT.Copy).then_inc(m_whi[0], 1)

            def w2(s, u, q):
                e.wait_ge(m_win[1][u], 16 * q + 16)
                e.wait_ge(m_g2, NB * s + NB)
                e.activation(w2_hi[:, u], w2_raw[:, u], ACT.Copy).then_inc(m_whi[1], 1)

            def rows(s, u, q):
                for g in range(4):
                    e.wait_ge(m_tx, 4 * s + g + 1 + 8)
                    e.activation(group(xt_hi, u, g), bank(g), ACT.Copy).then_inc(m_xhi, 1)

            def head(s, u, q):
                if more(s):
                    w1(s + 1, 1 - u, q + u)
                x = e.value_load(step_x[0:1, ds(s, 1)], min_val=0, max_val=NX - 1)
                for j in range(HK):
                    wait_apart(e, m_g1, HK * s + j + 1 + 4)
                    e.activation(hid[:, u, j, :], ps[:, 2 + j, 0:M], ACT.Silu, bias=eb1c[:, ds(x * HK + j, 1)]).then_inc(m_h, 1)
                e.wait_ge(m_h, HK * s + HK + 2)
                e.wait_ge(m_g2, NB * s + NB)
                e.activation(hid_hi[:, u], hid[:, u], ACT.Copy).then_inc(m_hhi, 1)
                if more(s):
                    rows(s + 1, 1 - u, q + u)
                w2(s, u, q)

            def tail(s, u, q):
                e.wait_ge(m_out, NB * s + NB + 2 * NB)
                e.dma_start(o_d[ds(s * M, M), :].rearrange("(b p) n -> p b n", p=128), o_rows[:, u]).then_inc(m_st[u], 16)

            w1(0, 0, 0)
            rows(0, 0, 0)
            skewed(e, NS, head, tail)

        @on("vector")
        def _(e):
            gated(e)

            def w(i, raw, hi, lo, s, u, q):
                e.wait_ge(m_whi[i], s + 1)
                e.tensor_tensor(lo[:, u], raw[:, u], hi[:, u].bitcast(F32), ALU.subtract).then_inc(m_wlo[i], 1)

            def rows(s, u, q):
                for g in range(4):
                    e.wait_ge(m_xhi, 4 * s + g + 1)
                    e.tensor_tensor(group(xt_lo, u, g), bank(g), group(xt_hi, u, g).bitcast(F32), ALU.subtract).then_inc(m_xlo, 1)

            def head(s, u, q):
                if more(s):
                    w(0, w1_raw, w1_hi, w1_lo, s + 1, 1 - u, q + u)
                e.wait_ge(m_hhi, s + 1)
                e.tensor_tensor(hid_lo[:, u], hid[:, u], hid_hi[:, u].bitcast(F32), ALU.subtract).then_inc(m_hlo, 1)
                if more(s):
                    rows(s + 1, 1 - u, q + u)
                w(1, w2_raw, w2_hi, w2_lo, s, u, q)

            def tail(s, u, q):
                e.wait_ge(m_bin[u], 16 * q + 16)
                e.wait_ge(m_st[u], 16 * q)
                for b in range(SUB):
                    for half in range(2):
                        e.wait_ge(m_g2, NB * s + 2 * b + half + 1 + 2 * NB)
                        cols = slice(512 * half, 512 * half + 512)
                        e.tensor_tensor(o_rows[:, u, b, cols], ps[:, 4 + 2 * b + half, :], b2_row[:, u, cols], ALU.add)\
                            .then_inc(m_out, 1)
            w(0, w1_raw, w1_hi, w1_lo, 0, 0, 0)
            rows(0, 0, 0)
            skewed(e, NS, head, tail)

        f_idx = sem("f_idx")
        f_oin = [[sem(f"f_oin{c}{u}") for u in range(2)] for c in range(TOP)]
        f_rin = [sem(f"f_rin{u}") for u in range(2)]
        f_mix = sem("f_mix")
        f_y = sem("f_y")
        f_st = [sem(f"f_st{u}") for u in range(2)]

        @on("sync")
        def _(e):
            e.sem_inc(f_y, 2)
            e.wait_ge(m_g1, HK * NS + 4)

            def head(i, u, q):
                e.wait_ge(f_y, i + 1)
                e.dma_start(r_rows[:, u, :], r_d[ds(i * P, P), :]).then_inc(f_rin[u], 16)

            def tail(i, u, q):
                e.wait_ge(f_y, i + 3)
                e.dma_start(out[ds(i * P, P), :], y_rows[:, u, :]).then_inc(f_st[u], 16)
            skewed(e, NT, head, tail)
            for u in range(2):
                e.wait_ge(f_st[u], 16 * (NT // 2))

        @on("gpsimd")
        def _(e):
            for u in range(2):
                e.wait_ge(m_st[u], 16 * ((NS + 1 - u) // 2))

            def head(i, u, q):
                wait_apart(e, f_y, i + 1)
                e.tensor_copy(slot_now[:, u, :], sloti[:, :, ds(i, 1)].rearrange("p c a -> p (c a)")).then_inc(f_idx, 1)
                wait_apart(e, f_idx, i + 1)
                for c in range(TOP):
                    e.indirect_dma_start(out=pick[:, u, c, :], out_offset=None, in_=o_d[:, :],
                                         in_offset=bass.IndirectOffsetOnAxis(ap=slot_now[:, u, c:c + 1], axis=0)).then_inc(f_oin[c][u], 16)
            skewed(e, NT, head, lambda i, u, q: None)

        @on("vector")
        def _(e):
            def head(i, u, q):
                e.wait_ge(f_rin[u], 16 * q + 16)
                e.wait_ge(f_oin[0][u], 16 * q + 16)
                e.wait_ge(f_st[u], 16 * q)
                e.scalar_tensor_tensor(out=y_rows[:, u, :], in0=pick[:, u, 0, :], scalar=weight[:, 0, ds(i, 1)],
                                       in1=r_rows[:, u, :], op0=ALU.mult, op1=ALU.add).then_inc(f_mix, 1)
                e.wait_ge(f_mix, i + 1)
                e.wait_ge(f_oin[1][u], 16 * q + 16)
                e.scalar_tensor_tensor(out=y_rows[:, u, :], in0=pick[:, u, 1, :], scalar=weight[:, 1, ds(i, 1)],
                                       in1=y_rows[:, u, :], op0=ALU.mult, op1=ALU.add).then_inc(f_y, 1)
            skewed(e, NT, head, lambda i, u, q: None)

        cb = ExitStack()
        block = cb.enter_context(nc.Block())
        for engine, parts in ((block.sync, prog["sync"]), (block.scalar, prog["scalar"]), (block.vector, prog["vector"]),
                              (block.gpsimd, prog["gpsimd"]), (block.tensor, prog["tensor"])):
            @engine
            def _(e, parts=parts):
                for part in parts:
                    part(e)
        cb.close()
        if DEBUG:
            loc = locals()
            s_dbg = sem("s_dbg")
            with nc.Block() as blk:
                @blk.sync
                def _(e):
                    n = 0
                    for name in DEBUG:
                        t = loc[name]
                        dt = F32 if t.dtype == F32R else t.dtype
                        d = nc.dram_tensor("dbg_" + name, tuple(t.shape), dt, kind="ExternalOutput").ap()
                        e.dma_start(d, t[:].bitcast(F32) if t.dtype == F32R else t[:]).then_inc(s_dbg, 16)
                        n += 16
                        e.wait_ge(s_dbg, n)


_INS = ["x", "src", "dst", "L0_gnn_W_self0", "L0_gnn_W_neigh0", "L0_gnn_b0", "L0_gnn_W_self1", "L0_gnn_W_neigh1",
        "L0_gnn_b1", "L0_ffn_rw1", "L0_ffn_rb1", "L0_ffn_rw2", "L0_ffn_rb2", "L0_ffn_ew1", "L0_ffn_eb1",
        "L0_ffn_ew2", "L0_ffn_eb2"]


def kernel(**inputs):
    import numpy as np
    import concourse.bacc as bacc
    from concourse.bass_utils import run_bass_kernel_spmd

    nc = bacc.Bacc("TRN2", target_bir_lowering=False, num_devices=1)
    arrays, aps = {}, {}
    for name in _INS:
        a = np.ascontiguousarray(inputs[name])
        arrays[f"in_{name}"] = a
        aps[name] = nc.dram_tensor(f"in_{name}", a.shape, mybir.dt.from_np(a.dtype), kind="ExternalInput").ap()
    out = nc.dram_tensor("out_0", (N, D), F32, kind="ExternalOutput").ap()
    build(nc, aps, out)
    r = run_bass_kernel_spmd(nc, [arrays], core_ids=[0])
    return r.results[0]["out_0"]
```

```python
from contextlib import ExitStack

import concourse.bass as bass
from concourse import mybir

F32 = mybir.dt.float32
F32R = mybir.dt.float32r
BF16 = mybir.dt.bfloat16
F16 = mybir.dt.float16
I32 = mybir.dt.int32
U16 = mybir.dt.uint16
ALU = mybir.AluOpType
ACT = mybir.ActivationFunctionType
AX = mybir.AxisListType
ds = bass.ds

N = 1250
D = 1024
P = 125
NT = N // P
KT = D // 128
E = 40000
NCH = E // P
G = 4
W = 25
NW = N // W
KW = NT * W
SPAN = 1024
EXACT = 4096.0
FAST = NCH // G + NW
ROUNDS = NCH // G
GROUPS = ((0, 4), (4, 4), (8, 2))
COLS = ((0, 418), (418, 416), (834, 416))
NX = 8
HID = 256
TOP = 2
M = 256
NS = (TOP * N + NX * (M - 1)) // M
SUB = M // 128
HK = HID // 128
H_IN = 4
EPS = 1e-5
ROUND = 1.5 * 2.0 ** 23


def pipeline(e, n, *stages):
    deepest = max(lag for lag, _ in stages)
    loops = (n - deepest - 1) // 2

    def plain(t):
        for lag, part in stages:
            if 0 <= t - lag < n:
                part(t - lag, (t - lag) % 2, (t - lag) // 2)
    for t in range(deepest):
        plain(t)
    with e.Fori(0, loops) as r:
        for b in range(2):
            for lag, part in stages:
                k = deepest + b - lag
                part(2 * r + k if k else 2 * r, k % 2, r + k // 2 if k // 2 else r)
    for t in range(deepest + 2 * loops, n + deepest):
        plain(t)


def skewed(e, n, head, tail):
    pipeline(e, n, (0, head), (1, tail))


def build(nc, I, out):
    ctx = ExitStack()
    with ctx:
        prog = {k: [] for k in ("sync", "scalar", "vector", "gpsimd", "tensor")}

        def on(engine):
            return prog[engine].append

        def sem(name):
            return ctx.enter_context(nc.semaphore(name))

        top = nc.sbuf_base + (-nc.sbuf_base) % 32
        R_H, R_A, R_ACC, R_SLAB, R_WORK = (top + x for x in (0, 80000, 130016, 155040, 179616))
        R_CONST = R_WORK + 25344

        class Region:
            def __init__(self, at):
                self.at = at

            def __call__(self, name, shape, dt):
                t = nc.alloc_sbuf_tensor_at(name, shape, dt, offset=self.at)
                size = 2 if dt in (BF16, F16, U16) else 4
                for s in shape[1:]:
                    size *= s
                self.at += size + (-size) % 32
                return t

        C = Region(R_CONST)
        ident = C("ident", [128, 128], F32)
        ones = C("ones", [128, 128], F32)
        bias = C("bias", [128, 3, KT], F32)
        ones_r = C("ones_r", [P, 128], F32R)
        rw2 = C("rw2", [128, KT, NX], F32)
        mv = C("mv", [P, 2, 2], F32)
        stats = C("stats", [P, 2, 2, 6], F32)
        rstd = C("rstd", [P, 2, 4], F32)
        epst = C("epst", [128, 1], F32)
        logit = C("logit", [P, NT, NX], F32)
        flagi = C("flagi", [1, 8], I32)

        H = Region(R_H)
        h_hi = H("h_hi", [128, KT, N], F32R)
        h_lo = H("h_lo", [128, KT, N], F32R)

        adj = Region(R_A)("adj", [P, NT, N], F32R)
        adj_f = adj[:].bitcast(F32)
        S = Region(R_WORK)
        src_hot = S("src_hot", [P, 2, G, P], BF16)
        key_hot = S("key_hot", [P, 2, G, KW], BF16)
        seq_i = S("seq_i", [P, KW], I32)
        seq16 = S("seq16", [P, KW], F16)
        dcol = S("dcol", [P, NCH], F32)
        scol = S("scol", [P, NCH + G], F32)
        key = S("key", [P, NCH + G], F32)
        part = S("part", [P, NCH], F32)
        d_seq = S("d_seq", [P, NCH], I32)
        d_next = S("d_next", [P, NCH], I32)
        junk = S("junk", [P, NCH], F32)
        src_now = S("src_now", [P, 2, G], F32)
        key_now = S("key_now", [P, 2, G], F32)
        counted = S("counted", [P, 2, KW], F32)
        step_i = S("step_i", [P, FAST], I32)
        step_n = S("step_n", [P, FAST], F32)
        past = S("past", [NW, FAST], F32)
        past_d = S("past_d", [NW, FAST], F32)
        window = S("window", [P, FAST], F32)
        earlier = S("earlier", [NW, NW], F32)
        differ = S("differ", [NW, NW], F32)
        edge_i = S("edge_i", [NW, 1], I32)
        col = S("col", [P, 16], F32)
        assert S.at <= R_CONST
        S = Region(R_ACC + 16384)
        d_rows = S("d_rows", [80, 4, P], I32)
        s_rows = S("s_rows", [80, 4, P], I32)
        d_rowf = S("d_rowf", [80, 4, P], F32)
        s_rowf = S("s_rowf", [80, 4, P], F32)
        S = Region(R_CONST + 3072)
        tabj = S("tabj", [1, FAST], I32)
        tabc = S("tabc", [1, FAST], I32)

        L = Region(R_ACC)
        xn = L("xn", [P, 2, D], F32)
        xin = L("xin", [P, 2, D], F32)

        L = Region(R_SLAB)
        w_raw = L("w_raw", [128, 2, KT, 128], F32)
        w_hi = L("w_hi", [128, 2, KT, 128], F32R)
        w_lo = L("w_lo", [128, 2, KT, 128], F32R)
        L = Region(R_WORK)
        yT = L("yT", [128, N], F32)
        self_part = L("self_part", [128, N], F32)
        dinv_row = L("dinv_row", [128, N], F32)
        y_hi = L("y_hi", [P, NT, 128], F32R)
        y_lo = L("y_lo", [P, NT, 128], F32R)
        L = Region(R_ACC)
        layer_out = L("layer_out", [128, N], F32)
        x_slab = L("x_slab", [P, NT, 128], F32)
        x2_slab = L("x2_slab", [P, NT, 128], F32)
        h_in = Region(R_ACC + 5024)("h_in", [128, H_IN, N], F32)
        x2_all = Region(R_A)("x2_all", [P, NT, D], F32)
        hidden = Region(R_ACC + 8192)("hidden", [128, 2, N], F32)

        S = Region(R_CONST + 3072)
        rb2b = S("rb2b", [P, NX], F32)
        eb1c = S("eb1c", [128, NX * HK], F32)
        ids_i = S("ids_i", [128, NS * SUB], I32)
        id_now = S("id_now", [128, 2, SUB], I32)
        slot_now = S("slot_now", [P, 2, TOP], I32)
        sloti = S("sloti", [P, TOP, NT], I32)
        weight = S("weight", [P, TOP, NT], F32)
        step_x = S("step_x", [1, NS], I32)
        taken = S("taken", [P, NX], F32)
        S = Region(R_WORK)
        before = S("before", [P, P], F32)
        below = S("below", [P, NX, NX], F32)
        toki = S("toki", [P, NT], I32)
        seqi = S("seqi", [P, 128], I32)
        tokf = S("tokf", [P, NT], F32)
        seqf = S("seqf", [P, 128], F32)
        peak = S("peak", [P, NT], F32)
        less = S("less", [P, NT, NX], F32)
        rank = S("rank", [P, NT, NX], F32)
        sel = S("sel", [P, NT, NX], F32)
        cum = S("cum", [P, NT, NX], F32)
        cmpa = S("cmpa", [P, NT, NX, NX], F32)
        cmpb = S("cmpb", [P, NT, NX, NX], F32)
        steps = S("steps", [P, NX], F32)
        first = S("first", [P, NX], F32)
        slotf = S("slotf", [P, TOP, NT], F32)
        block_ = S("block_", [P, TOP, NT], F32)
        step_past = S("step_past", [1, NS, NX - 1], F32)
        step_f = S("step_f", [1, NS], F32)
        place_hot = S("place_hot", [P, TOP * NT, 128], F16)
        block_hot = S("block_hot", [P, TOP * NT, NS * SUB], F16)

        S = Region(R_H)
        w1_raw = S("w1_raw", [128, 2, KT, HID], F32)
        w1_hi = S("w1_hi", [128, 2, KT, HID], F32R)
        w1_lo = S("w1_lo", [128, 2, KT, HID], F32R)
        w2_raw = S("w2_raw", [128, 2, HK, D], F32)
        w2_hi = S("w2_hi", [128, 2, HK, D], F32R)
        w2_lo = S("w2_lo", [128, 2, HK, D], F32R)
        x_rows = S("x_rows", [128, 2, SUB, D], F32)
        xt_hi = S("xt_hi", [128, 2, KT, M], F32R)
        xt_lo = S("xt_lo", [128, 2, KT, M], F32R)
        hid = S("hid", [128, 2, HK, M], F32)
        hid_hi = S("hid_hi", [128, 2, HK, M], F32R)
        hid_lo = S("hid_lo", [128, 2, HK, M], F32R)
        gate_T = S("gate_T", [NX, N], F32)
        eb2 = S("eb2", [NX, D], F32)
        assert S.at <= R_WORK
        S = Region(R_WORK)
        o_rows = S("o_rows", [128, 2, SUB, D], F32)
        assert S.at <= R_CONST
        S = Region(R_H)
        pick = S("pick", [P, 2, TOP, D], F32)
        r_rows = S("r_rows", [P, 2, D], F32)
        y_rows = S("y_rows", [P, 2, D], F32)

        ps = ctx.enter_context(nc.psum_tensor("ps", [128, 8, 512], F32))

        o_d = nc.dram_tensor("o_d", (NS * M, D), F32, kind="Internal").ap()
        h1_d = nc.dram_tensor("h1_d", (KT, 128, N), F32, kind="Internal").ap()
        x2_d = nc.dram_tensor("x2_d", (N, D), F32, kind="Internal").ap()
        t_d = nc.dram_tensor("t_d", (N, D), F32, kind="Internal").ap()
        r_d = nc.dram_tensor("r_d", (N, D), F32, kind="Internal").ap()

        s_id = sem("s_id")
        s_rb2 = sem("s_rb2")
        s_ones = sem("s_ones")
        s_none = sem("s_none")
        s_small = [sem(f"s_small{i}") for i in range(6)]

        def wait_apart(e, sem, value):
            e.wait_ge(sem, value)
            e.sem_inc(s_none, 1)

        @on("gpsimd")
        def _(e):
            e.memset(ident[:], 0.0).then_inc(s_id, 1)
            e.wait_ge(s_id, 1)
            e.affine_select(out=ident[:], in_=ident[:], compare_op=ALU.not_equal, fill=1.0, base=0,
                            pattern=[[-1, 128]], channel_multiplier=1).then_inc(s_id, 1)
            e.memset(ones[:], 1.0).then_inc(s_ones, 1)
            e.memset(epst[:], EPS).then_inc(s_ones, 1)

        @on("sync")
        def _(e):
            e.dma_start(s_rows[:], I["src"].rearrange("(t p n) -> p t n", p=80, n=P)).then_inc(s_small[1], 16)
            for b, name in enumerate(("L0_gnn_b0", "L0_gnn_b1", "L0_ffn_rb1")):
                e.dma_start(bias[:, b, :], I[name].rearrange("(k p) -> p k", p=128),
                            allow_slow_non_contiguous=True).then_inc(s_small[3 + b], 16)

        s_seq = sem("s_seq")
        s_next = sem("s_next")
        s_tb = sem("s_tb")
        s_iota = sem("s_iota")
        s_ecast = sem("s_ecast")
        s_etp = sem("s_etp")
        s_tab = sem("s_tab")
        s_dn = sem("s_dn")

        @on("scalar")
        def _(e):
            e.dma_start(d_rows[:], I["dst"].rearrange("(t p n) -> p t n", p=80, n=P)).then_inc(s_small[0], 16)
            e.dma_start(d_seq[:], I["dst"].rearrange("(p n) -> p n", p=P)).then_inc(s_seq, 16)
            e.wait_ge(s_dn, 1)
            e.dma_start(d_next[0:P - 1, :], I["dst"][1:1 + (P - 1) * NCH].rearrange("(p n) -> p n", p=P - 1)).then_inc(s_next, 16)
            e.dma_start(d_next[P - 1:P, 0:NCH - 1], I["dst"][1 + (P - 1) * NCH:E].rearrange("(p n) -> p n", p=1)).then_inc(s_next, 16)

        @on("gpsimd")
        def _(e):
            e.memset(d_next[:], 1 << 20).then_inc(s_dn, 1)
            e.iota(seq_i[:], [[1, KW]], base=0, channel_multiplier=0).then_inc(s_iota, 1)
            e.iota(step_i[:], [[1, FAST]], base=0, channel_multiplier=0).then_inc(s_iota, 1)
            e.iota(edge_i[:], [[1, 1]], base=0, channel_multiplier=W).then_inc(s_iota, 1)
            e.memset(earlier[:], 1.0).then_inc(s_iota, 1)
            e.memset(key[:, NCH:], -1.0).then_inc(s_iota, 1)
            e.memset(scol[:, NCH:], -1.0).then_inc(s_iota, 1)
            e.wait_ge(s_iota, 6)
            e.tensor_copy(seq16[:], seq_i[:]).then_inc(s_iota, 1)
            e.affine_select(out=earlier[:], in_=earlier[:], compare_op=ALU.is_gt, fill=0.0, base=0,
                            pattern=[[1, NW]], channel_multiplier=-1).then_inc(s_iota, 1)
            e.affine_select(out=differ[:], in_=ident[0:NW, 0:NW], compare_op=ALU.not_equal, fill=-1.0, base=-1,
                            pattern=[[1, NW]], channel_multiplier=-1).then_inc(s_iota, 1)

        @on("vector")
        def _(e):
            e.wait_ge(s_small[0], 16)
            e.tensor_copy(d_rowf[:], d_rows[:]).then_inc(s_ecast, 1)
            e.wait_ge(s_small[1], 16)
            e.tensor_copy(s_rowf[:], s_rows[:]).then_inc(s_ecast, 1)
            n = [0]

            def link(ins):
                n[0] += 1
                ins.then_inc(s_tb, 1)
                e.wait_ge(s_tb, n[0])

            def rounded(out, in_, d):
                link(e.tensor_scalar(out, in_, 1.0 / d, 0.5 / d - 0.5, ALU.mult, ALU.add))
                link(e.tensor_scalar(out, out, ROUND, ROUND, ALU.add, ALU.subtract))

            low, high, c0, e0, runs, first_, o, dd = (col[0:NW, i:i + 1] for i in range(8))
            e.wait_ge(s_etp, 1)
            link(e.tensor_copy(dcol[:], ps[0:P, 0, 0:NCH]))
            e.wait_ge(s_iota, 9)
            link(e.tensor_copy(low, edge_i[:]))
            link(e.tensor_scalar(high, low, float(W), None, ALU.add))
            link(e.tensor_copy(step_n[:], step_i[:]))
            e.wait_ge(s_etp, 2)
            link(e.tensor_scalar(junk[0:NW, :], ps[0:NW, 3, 0:NCH], low, None, ALU.is_lt))
            link(e.tensor_reduce(c0, junk[0:NW, :], AX.X, ALU.add))
            link(e.tensor_scalar(junk[0:NW, :], ps[0:NW, 2, 0:NCH], high, None, ALU.is_lt))
            link(e.tensor_reduce(e0, junk[0:NW, :], AX.X, ALU.add))
            link(e.tensor_tensor(runs, e0, c0, ALU.subtract))
            link(e.tensor_scalar(runs, runs, 1.0 / G, 0.5 - 0.5 / G, ALU.mult, ALU.add))
            link(e.tensor_scalar(runs, runs, ROUND, ROUND, ALU.add, ALU.subtract))
            e.sem_inc(s_ecast, 1)
            e.wait_ge(s_etp, 3)
            link(e.tensor_copy(scol[:, 0:NCH], ps[0:P, 1, 0:NCH]))
            rounded(key[:, 0:NCH], scol[:, 0:NCH], P)
            link(e.scalar_tensor_tensor(out=scol[:, 0:NCH], in0=key[:, 0:NCH], scalar=-float(P), in1=scol[:, 0:NCH],
                                        op0=ALU.mult, op1=ALU.add))
            link(e.scalar_tensor_tensor(out=key[:, 0:NCH], in0=key[:, 0:NCH], scalar=float(W), in1=dcol[:],
                                        op0=ALU.mult, op1=ALU.add))
            rounded(part[:], dcol[:], W)
            link(e.scalar_tensor_tensor(out=key[:, 0:NCH], in0=part[:], scalar=float(SPAN - W), in1=key[:, 0:NCH],
                                        op0=ALU.mult, op1=ALU.add))
            e.wait_ge(s_etp, 4)
            link(e.tensor_copy(first_, ps[0:NW, 4, 0:1]))
            link(e.scalar_tensor_tensor(out=o, in0=first_, scalar=-float(G), in1=c0, op0=ALU.mult, op1=ALU.add))
            e.sem_inc(s_ecast, 1)
            e.wait_ge(s_etp, 5)
            link(e.tensor_copy(dd, ps[0:NW, 4, 8:9]))
            link(e.tensor_scalar(past[:], step_n[0:NW, :], first_, None, ALU.is_ge))
            link(e.tensor_scalar(past_d[:], past[:], dd, None, ALU.mult))
            e.sem_inc(s_ecast, 1)
            e.wait_ge(s_next, 32)
            e.wait_ge(s_seq, 16)
            link(e.tensor_tensor(junk[:], d_seq[:], d_next[:], ALU.is_gt))
            link(e.tensor_reduce(col[:, 8:9], junk[:], AX.X, ALU.add))
            e.sem_inc(s_ecast, 1)
            e.wait_ge(s_etp, 6)
            link(e.tensor_scalar(window[:], ps[0:P, 5, 0:FAST], -float(SPAN), float(SPAN), ALU.mult, ALU.add))
            link(e.tensor_scalar(tabj[:], ps[0:1, 5, 0:FAST], 1.0, None, ALU.subtract))
            link(e.scalar_tensor_tensor(out=junk[0:1, 0:FAST], in0=step_n[0:1, :], scalar=float(G),
                                        in1=ps[0:1, 5, 256:256 + FAST], op0=ALU.mult, op1=ALU.add))
            link(e.tensor_scalar(tabc[:], junk[0:1, 0:FAST], float(NCH), None, ALU.min))
            e.wait_ge(s_etp, 7)
            link(e.tensor_scalar(flagi[:, 0:1], ps[0:1, 4, 16:17], 0.0, None, ALU.is_equal))
            link(e.memset(col[:, 9:10], 0.0))
            link(e.memset(col[:, 15:16], -float(SPAN)))
            e.tensor_copy(ones_r[:], ones[0:P, :]).then_inc(s_tab, 1)

        @on("tensor")
        def _(e):
            e.wait_ge(s_id, 2)
            e.wait_ge(s_ones, 1)

            def turn(i, rows):
                e.wait_ge(s_ecast, i + 1)
                for t in range(4):
                    mm = e.transpose(ps[0:P, i, 80 * t:80 * t + 80], rows[:, t, :], ident[0:80, 0:80])
                mm.then_inc(s_etp, 1)
            turn(0, d_rowf)
            e.wait_ge(s_tb, 1)
            for bank, row in ((2, 0), (3, P - 1)):
                mm = e.matmul(ps[0:NW, bank, 0:NCH], ident[0:P, row:row + 1].to_broadcast([P, NW]), dcol[:],
                              start=True, stop=True)
            mm.then_inc(s_etp, 1)
            turn(1, s_rowf)
            e.wait_ge(s_iota, 9)
            e.wait_ge(s_ecast, 3)
            e.matmul(ps[0:NW, 4, 0:1], earlier[:], col[0:NW, 4:5], start=True, stop=True).then_inc(s_etp, 1)
            e.wait_ge(s_ecast, 4)
            e.matmul(ps[0:NW, 4, 8:9], differ[:], col[0:NW, 6:7], start=True, stop=True).then_inc(s_etp, 1)
            e.wait_ge(s_ecast, 5)
            for at, t in ((0, past), (256, past_d)):
                mm = e.matmul(ps[0:P, 5, at:at + FAST], ones[0:NW, 0:P], t[:], start=True, stop=True)
            mm.then_inc(s_etp, 1)
            e.wait_ge(s_ecast, 6)
            e.matmul(ps[0:1, 4, 16:17], ones[0:P, 0:1], col[:, 8:9], start=True, stop=True).then_inc(s_etp, 1)

        def split_slab(e, u, loaded, value, done):
            wait_apart(e, loaded, value)
            e.tensor_copy(w_hi[:, u, :, :], w_raw[:, u, :, :]).then_inc(done, 1)

        def rest_slab(e, u, done, value):
            e.wait_ge(done, value)
            e.tensor_tensor(w_lo[:, u, :, :], w_raw[:, u, :, :], w_hi[:, u, :, :].bitcast(F32), ALU.subtract).then_inc(done, 1)

        def product(e, bank, u, wait, full):
            for c, (a, w) in enumerate(COLS):
                wait(c)
                passes = ((w_hi, h_hi), (w_hi, h_lo), (w_lo, h_hi))
                n = 0
                for k in range(KT):
                    for wt, ht in passes:
                        n += 1
                        mm = e.matmul(ps[:, bank + c, 0:w], wt[:, u, k, :], ht[:, k, a:a + w],
                                      start=(n == 1), stop=(n == 3 * KT))
                mm.then_inc(full, 1)

        view = lambda w: w.rearrange("(k p) n -> p k n", p=128)

        def first_slabs(tag, w_self, w_neigh, loadable, splittable):
            x_full = sem(f"{tag}_xfull")
            z_full = sem(f"{tag}_zfull")
            w_in = [sem(f"{tag}_win{u}") for u in range(2)]
            w_ok = [sem(f"{tag}_wok{u}") for u in range(2)]

            @on("sync")
            def _(e):
                loadable(e)
                for u, w in enumerate((w_neigh, w_self)):
                    e.dma_start(w_raw[:, u, :, :], view(w)[:, :, 0:128]).then_inc(w_in[u], 16)

            @on("gpsimd")
            def _(e):
                splittable(e)
                for u in range(2):
                    split_slab(e, u, w_in[u], 16, w_ok[u])
                    rest_slab(e, u, w_ok[u], 1)
            return w_self, w_neigh, x_full, z_full, w_in, w_ok

        nothing = lambda e: None
        slabs0 = first_slabs("l0", I["L0_gnn_W_self0"], I["L0_gnn_W_neigh0"], nothing, nothing)

        def layer_norm(tag, src, free, t_out=None, kept=None):
            rows = (lambda i, u: kept[:, ds(i, 1), :].rearrange("p a n -> p (a n)")) if kept is not None else \
                (lambda i, u: xin[:, u, :])
            x_in = [sem(f"{tag}_in{u}") for u in range(2)]
            st = sem(f"{tag}_st")
            sq = sem(f"{tag}_sq")
            xr = sem(f"{tag}_xr")
            tp = sem(f"{tag}_tp")
            hi = sem(f"{tag}_hi")
            lo = sem(f"{tag}_lo")
            t_st = [sem(f"{tag}_ts{u}") for u in range(2)] if kept is not None else []
            sm = sem(f"{tag}_sm") if kept is not None else None

            @on("sync")
            def _(e):
                free(e)
                e.sem_inc(xr, 2)

                def load(i, u):
                    e.dma_start(rows(i, u), src[ds(i * P, P), :]).then_inc(x_in[u], 16)

                def store(i, u):
                    e.wait_ge(xr, i + 3)
                    e.dma_start(t_out[ds(i * P, P), :], xn[:, u, :]).then_inc(t_st[u], 16)

                for u in range(2):
                    load(u, u)
                with e.Fori(1, NT // 2) as q:
                    for u in range(2):
                        if kept is None:
                            e.wait_ge(xr, 2 * q + u + 1)
                        else:
                            e.wait_ge(st, 8 * q + 4 * u - 7)
                        load(2 * q + u, u)
                        if kept is not None:
                            store(2 * q + u - 2, u)
                if kept is not None:
                    for u in range(2):
                        store(NT - 2 + u, u)

            def bank(u, g):
                return ps[:, 4 + 2 * u + g, 0:4 * P].rearrange("p (k n) -> p k n", k=4)

            def part_of(h, i, g):
                return h[:, 4 * g:4 * g + 4, ds(i * P, P)]

            @on("vector")
            def _(e):
                free(e)

                def moments(i, u, q):
                    e.wait_ge(x_in[u], 16 * q + 16)
                    for g in range(2):
                        mm = e.bn_stats(stats[:, u, g, :], rows(i, u)[:, 512 * g:512 * g + 512])
                    mm.then_inc(st, 1)
                    wait_apart(e, st, 4 * i + 1)
                    e.bn_aggr(mv[:, u, :], stats[:, u, :, :].rearrange("p a b -> p (a b)")).then_inc(st, 1)

                def low(i, u, q):
                    for g in range(2):
                        e.wait_ge(hi, 2 * i + g + 1)
                        e.tensor_tensor(part_of(h_lo, i, g), bank(u, g), part_of(h_hi, i, g).bitcast(F32),
                                        ALU.subtract).then_inc(lo, 1)

                def inverse(i, u, q):
                    e.wait_ge(sq, i + 1)
                    e.reciprocal(rstd[:, u, 1:2], rstd[:, u, 0:1]).then_inc(st, 1)
                    e.wait_ge(st, 4 * i + 3)
                    e.scalar_tensor_tensor(out=rstd[:, u, 2:3], in0=mv[:, u, 0:1], scalar=-1.0,
                                           in1=rstd[:, u, 1:2], op0=ALU.mult, op1=ALU.mult).then_inc(st, 1)

                pipeline(e, NT, (0, moments), (2, low), (0, inverse))

            @on("scalar")
            def _(e):
                e.wait_ge(s_ones, 2)
                free(e)
                if kept is not None:
                    for u in range(2):
                        e.sem_inc(t_st[u], 16)
                    e.sem_inc(sm, 2)

                def deviation(i, u, q):
                    e.wait_ge(st, 4 * i + 2)
                    e.activation(rstd[:, u, 0:1], mv[:, u, 1:2], ACT.Sqrt, bias=epst[0:P, :]).then_inc(sq, 1)

                def high(i, u, q):
                    for g in range(2):
                        wait_apart(e, tp, 2 * i + g + 1 + 2)
                        e.activation(part_of(h_hi, i, g), bank(u, g), ACT.Copy).then_inc(hi, 1)

                def normal(i, u, q):
                    e.wait_ge(st, 4 * i + 4)
                    e.wait_ge(tp, 2 * i)
                    if kept is not None:
                        e.wait_ge(t_st[u], 16 * q + 16)
                        wait_apart(e, sm, i + 1)
                    e.activation(xn[:, u, :], rows(i, u), ACT.Identity, bias=rstd[:, u, 2:3],
                                 scale=rstd[:, u, 1:2]).then_inc(xr, 1)

                pipeline(e, NT, (0, deviation), (1, high), (0, normal))

            @on("tensor")
            def _(e):
                free(e)
                e.sem_inc(tp, 2)
                e.sem_inc(lo, 4)

                def head(i, u, q):
                    e.wait_ge(xr, i + 3)
                    for g in range(2):
                        e.wait_ge(lo, 2 * i + g + 1)
                        for k in range(4):
                            mm = e.transpose(ps[:, 4 + 2 * u + g, k * P:k * P + P],
                                             xn[:, u, 128 * (4 * g + k):128 * (4 * g + k + 1)], ident[0:P, 0:P])
                        mm.then_inc(tp, 1)
                pipeline(e, NT, (0, head))
            if kept is not None:
                @on("gpsimd")
                def _(e):
                    def add(i, u, q):
                        e.wait_ge(xr, i + 3)
                        e.tensor_tensor(rows(i, u), rows(i, u), xn[:, u, :], ALU.add).then_inc(sm, 1)
                    pipeline(e, NT, (0, add))
            return dict(lo=(lo, 2 * NT + 4), t_st=t_st, sm=(sm, NT + 2))

        ln0 = layer_norm("ln0", I["x"], lambda e: None)

        s_az = sem("s_az")
        s_acc = sem("s_acc")

        @on("gpsimd")
        def _(e):
            e.memset(adj_f, 0.0).then_inc(s_az, 1)

        now = sem("now")
        hot = sem("hot")
        prod = sem("prod")
        out_ = sem("out_")
        took = sem("took")
        moved = sem("moved")

        class Counts:
            def scalar(e, n, u, c, base):
                wait_apart(e, hot, n + 1)
                e.activation(src_now[:, u, :], scol[:, ds(c, G)], ACT.Copy)
                e.activation(key_now[:, u, :], key[:, ds(c, G)], ACT.Identity, bias=base).then_inc(now, 1)

            def evict(e, n, u):
                e.wait_ge(took, n + 1)
                wait_apart(e, prod, n + 3)
                e.activation(counted[:, u, :], ps[0:P, u, 0:KW], ACT.Copy).then_inc(out_, 1)

            def vector(e, n, u):
                e.wait_ge(now, n + 1)
                e.wait_ge(prod, n + 1)
                for g in range(G):
                    e.tensor_scalar(src_hot[:, u, g, :], seq16[:, 0:P], src_now[:, u, g:g + 1], None, ALU.is_equal)
                for g in range(G):
                    ins = e.tensor_scalar(key_hot[:, u, g, :], seq16[:], key_now[:, u, g:g + 1], None, ALU.is_equal)
                ins.then_inc(hot, 1)

            def tensor(e, n, u):
                e.wait_ge(hot, n + 3)
                e.wait_ge(out_, n + 1)
                for g in range(G):
                    mm = e.matmul(ps[0:P, u, 0:KW], src_hot[:, u, g, :], key_hot[:, u, g, :], start=(g == 0), stop=(g == G - 1))
                mm.then_inc(prod, 1)

            def gpsimd(e, n, u, j):
                e.wait_ge(out_, n + 3)
                wait_apart(e, took, n + 2)
                cols = adj_f[:, :, ds(j * W, W)]
                e.tensor_tensor(cols, counted[:, u, :].rearrange("p (t w) -> p t w", t=NT), cols, ALU.add).then_inc(took, 1)

        def window_of(e, s):
            return e.value_load(tabj[0:1, ds(s, 1)], min_val=0, max_val=NW - 1)

        def chunk_of(e, s):
            return e.value_load(tabc[0:1, ds(s, 1)], min_val=0, max_val=NCH)

        def fast(engine, e):
            pipeline(e, FAST, *dict(
                scalar=((0, lambda s, u, q: Counts.scalar(e, s, u, chunk_of(e, s), window[:, ds(s, 1)])),
                        (2, lambda s, u, q: Counts.evict(e, s, u))),
                vector=((0, lambda s, u, q: Counts.vector(e, s, u)),),
                tensor=((0, lambda s, u, q: Counts.tensor(e, s, u)),),
                gpsimd=((0, lambda s, u, q: Counts.gpsimd(e, s, u, window_of(e, s))),))[engine])

        def full(engine, e):
            base = col[:, 9:10]
            with e.Fori(0, NW) as j:
                n = j * ROUNDS
                pipeline(e, ROUNDS, *dict(
                    scalar=((0, lambda s, u, q: Counts.scalar(e, n + s, u, s * G, base)),
                            (2, lambda s, u, q: Counts.evict(e, n + s, u))),
                    vector=((0, lambda s, u, q: Counts.vector(e, n + s, u)),),
                    tensor=((0, lambda s, u, q: Counts.tensor(e, n + s, u)),),
                    gpsimd=((0, lambda s, u, q: Counts.gpsimd(e, n + s, u, j)),))[engine])
                if engine == "scalar":
                    wait_apart(e, now, n + ROUNDS)
                    e.activation(base, base, ACT.Identity, bias=col[:, 15:16]).then_inc(moved, 1)
                    e.wait_ge(moved, j + 1)

        def both(engine):
            @on(engine)
            def _(e):
                e.wait_ge(s_tab, 1)
                e.wait_ge(s_az, 1)
                if engine == "tensor":
                    e.sem_inc(hot, 2)
                    e.sem_inc(prod, 2)
                    e.sem_inc(out_, 2)
                    e.sem_inc(took, 2)
                flag = e.value_load(flagi[0:1, 0:1], min_val=0, max_val=1)
                with e.If(flag):
                    fast(engine, e)
                    if engine == "gpsimd":
                        e.wait_ge(took, FAST + 2)
                with e.Else():
                    full(engine, e)
                    if engine == "gpsimd":
                        e.wait_ge(took, NW * ROUNDS + 2)
                if engine == "gpsimd":
                    e.sem_inc(s_acc, 1)
        for engine in ("scalar", "vector", "gpsimd", "tensor"):
            both(engine)

        s_deg = sem("s_deg")
        s_big = sem("s_big")
        s_drow = sem("s_drow")

        def sums(e, ones_, adj_):
            for c, (a, w) in enumerate(COLS):
                for k in range(NT):
                    mm = e.matmul(ps[:, 3 + c, 0:w], ones_, adj_[:, k, a:a + w], start=(k == 0), stop=(k == NT - 1))
                mm.then_inc(s_deg, 1)

        @on("tensor")
        def _(e):
            e.wait_ge(s_acc, 1)
            sums(e, ones_r[:], adj)
            e.wait_ge(s_big, 6)
            big = e.value_load(flagi[0:1, 1:2], min_val=0, max_val=1)
            with e.If(big):
                sums(e, ones[0:P, :], adj_f)
            with e.Else():
                e.sem_inc(s_deg, 3)

        @on("vector")
        def _(e):
            for c, (a, w) in enumerate(COLS):
                e.wait_ge(s_deg, c + 1)
                e.tensor_reduce(col[0:1, 10 + c:11 + c], ps[0:1, 3 + c, 0:w], AX.X, ALU.max).then_inc(s_big, 1)
            e.wait_ge(s_big, 3)
            e.tensor_reduce(col[0:1, 13:14], col[0:1, 10:13], AX.X, ALU.max).then_inc(s_big, 1)
            e.wait_ge(s_big, 4)
            e.tensor_scalar(col[0:1, 14:15], col[0:1, 13:14], EXACT, None, ALU.is_ge).then_inc(s_big, 1)
            e.wait_ge(s_big, 5)
            e.tensor_copy(flagi[:, 1:2], col[0:1, 14:15]).then_inc(s_big, 1)
            e.wait_ge(s_deg, 6)
            for c, (a, w) in enumerate(COLS):
                e.tensor_scalar(self_part[:, a:a + w], ps[:, 3 + c, 0:w], 1.0, None, ALU.max).then_inc(s_drow, 1)
                e.wait_ge(s_drow, 2 * c + 1)
                e.reciprocal(dinv_row[:, a:a + w], self_part[:, a:a + w]).then_inc(s_drow, 1)

        def layer(tag, slabs, b, last, free, h_ready, own_ready, meanwhile=None):
            w_self, w_neigh, x_full, z_full, w_in, w_ok = slabs
            x_free = sem(f"{tag}_xfree")
            own_out = sem(f"{tag}_ownout")
            agg_out = sem(f"{tag}_aggout")
            t_full = sem(f"{tag}_tfull")
            t_hi = sem(f"{tag}_thi")
            t_free = sem(f"{tag}_tfree")
            sp_free = sem(f"{tag}_spfree")
            u_done = sem(f"{tag}_udone")
            x_in = sem(f"{tag}_xin")
            st = sem(f"{tag}_st")
            x2_ok = sem(f"{tag}_x2ok")
            T = 6 if last else 3
            nat = lambda a: a.rearrange("(t p) n -> p t n", p=P)
            x_view, x2_view = nat(I["x"]), nat(x2_d)

            @on("sync")
            def _(e):
                with e.Fori(1, KT) as m:
                    for u, w in enumerate((w_neigh, w_self)):
                        e.wait_ge(w_ok[u], 2 * m)
                        e.dma_start(w_raw[:, u, :, :], view(w)[:, :, ds(m * 128, 128)]).then_inc(w_in[u], 16)

            @on("gpsimd")
            def _(e):
                with e.Fori(1, KT) as m:
                    for u, full, n in ((0, x_full, 3 * m), (1, z_full, 6 * m - 3)):
                        e.wait_ge(full, n)
                        split_slab(e, u, w_in[u], 16 * m + 16, w_ok[u])
                        rest_slab(e, u, w_ok[u], 2 * m + 1)

            @on("tensor")
            def _(e):
                free(e)
                h_ready(e)
                big = e.value_load(flagi[0:1, 1:2], min_val=0, max_val=1)
                e.sem_inc(x_free, 3)
                e.sem_inc(agg_out, 3)

                def neigh(m):
                    e.wait_ge(w_ok[0], 2 * m + 2)
                    product(e, 0, 0, lambda c: e.wait_ge(x_free, 3 * m + c + 1), x_full)

                def own(m):
                    e.wait_ge(w_ok[1], 2 * m + 2)
                    product(e, 3, 1, lambda c: e.wait_ge(agg_out, 3 * m + c + 1), z_full)

                def turn(n0, source, partitions, width):
                    for g, (t, n) in enumerate(GROUPS):
                        e.wait_ge(t_free, n0 + g // 2)
                        for i in range(n):
                            mm = e.transpose(ps[0:P, 6 + g % 2, 128 * i:128 * i + 128],
                                             source[:, P * (t + i):P * (t + i + 1)], ident[:])
                        mm.then_inc(t_full, 1)

                def sums(m, parts, adj_):
                    for c, (a, w) in enumerate(COLS):
                        e.wait_ge(own_out, 3 * m + c + 1)
                        n = 0
                        for k in range(NT):
                            for y in parts:
                                n += 1
                                mm = e.matmul(ps[:, 3 + c, 0:w], y[:, k, :], adj_[:, k, a:a + w],
                                              start=(n == 1), stop=(n == 2 * NT))
                        mm.then_inc(z_full, 1)

                def aggregate(m):
                    e.wait_ge(t_free, T * m + 3)
                    with e.If(big):
                        sums(m, (y_hi[:].bitcast(F32), y_lo[:].bitcast(F32)), adj_f)
                    with e.Else():
                        sums(m, (y_hi, y_lo), adj)

                def back(m):
                    e.wait_ge(u_done, 3 * m + 3)
                    turn(T * m + 3, layer_out, 128, P)

                def step(m, first=False, final=False):
                    if first:
                        own_ready(e)
                    own(m)
                    if last and not first:
                        back(m - 1)
                    e.wait_ge(x_free, 3 * m + 6)
                    turn(T * m, yT, 128, P)
                    if not final:
                        neigh(m + 1)
                    aggregate(m)

                neigh(0)
                step(0, first=True)
                with e.Fori(1, KT - 1) as m:
                    step(m)
                step(KT - 1, final=True)
                if last:
                    back(KT - 1)

            @on("scalar")
            def _(e):
                e.wait_ge(s_small[3 + b], 16)
                free(e)
                own_ready(e)
                e.sem_inc(sp_free, 3)
                if last:
                    e.sem_inc(st, 16)

                def neigh(m):
                    for c, (a, w) in enumerate(COLS):
                        e.wait_ge(x_full, 3 * m + c + 1)
                        e.activation(yT[:, a:a + w], ps[:, c, 0:w], ACT.Copy).then_inc(x_free, 1)

                def own(m):
                    for c, (a, w) in enumerate(COLS):
                        e.wait_ge(z_full, 6 * m + c + 1)
                        wait_apart(e, sp_free, 3 * m + c + 1)
                        e.activation(self_part[:, a:a + w], ps[:, 3 + c, 0:w], ACT.Identity,
                                     bias=bias[:, b, ds(m, 1)]).then_inc(own_out, 1)

                def high(m):
                    for g, (t, n) in enumerate(GROUPS):
                        e.wait_ge(t_full, T * m + g + 1)
                        e.activation(y_hi[:, t:t + n, :], ps[0:P, 6 + g % 2, 0:128 * n].rearrange("p (k n) -> p k n", k=n),
                                     ACT.Copy).then_inc(t_hi, 1)

                def store(m):
                    if not last:
                        e.wait_ge(u_done, 3 * m + 3)
                        e.dma_start(h1_d[ds(m, 1), :, :].rearrange("a p n -> p (a n)"), layer_out[:]).then_inc(st, 16)
                    else:
                        e.wait_ge(x2_ok, 3 * m + 3)
                        e.dma_start(x2_view[:, :, ds(m * 128, 128)], x2_slab[:]).then_inc(st, 16)

                def fetch(m):
                    if last:
                        e.dma_start(x_slab[:], x_view[:, :, ds(m * 128, 128)]).then_inc(x_in, 16)

                def step(m, first=False, final=False):
                    own(m)
                    if not last and not first:
                        store(m - 1)
                    high(m)
                    if not final:
                        neigh(m + 1)
                    if last and not first:
                        store(m - 1)
                    fetch(m)

                neigh(0)
                step(0, first=True)
                with e.Fori(1, KT - 1) as m:
                    step(m)
                step(KT - 1, final=True)
                if last:
                    store(KT - 1)

            @on("vector")
            def _(e):
                free(e)

                def low(m):
                    for g, (t, n) in enumerate(GROUPS):
                        e.wait_ge(t_hi, 3 * m + g + 1)
                        e.tensor_tensor(y_lo[:, t:t + n, :], ps[0:P, 6 + g % 2, 0:128 * n].rearrange("p (k n) -> p k n", k=n),
                                        y_hi[:, t:t + n, :].bitcast(F32), ALU.subtract).then_inc(t_free, 1)

                def total(m):
                    if not last:
                        e.wait_ge(st, 16 * m)
                    for c, (a, w) in enumerate(COLS):
                        e.wait_ge(z_full, 6 * m + 3 + c + 1)
                        e.tensor_tensor(layer_out[:, a:a + w], ps[:, 3 + c, 0:w], dinv_row[:, a:a + w], ALU.mult).then_inc(agg_out, 1)
                        e.wait_ge(agg_out, 3 * m + c + 1 + 3)
                        e.tensor_tensor(layer_out[:, a:a + w], layer_out[:, a:a + w], self_part[:, a:a + w], ALU.add)\
                            .then_inc(u_done, 1)
                        e.wait_ge(u_done, 3 * m + c + 1)
                        e.sem_inc(sp_free, 1)

                def residual(m):
                    e.wait_ge(x_in, 16 * m + 16)
                    e.wait_ge(st, 16 * m + 16)
                    for g, (t, n) in enumerate(GROUPS):
                        e.wait_ge(t_full, T * m + 3 + g + 1)
                        e.tensor_tensor(x2_slab[:, t:t + n, :], ps[0:P, 6 + g % 2, 0:128 * n].rearrange("p (k n) -> p k n", k=n),
                                        x_slab[:, t:t + n, :], ALU.add).then_inc(x2_ok, 1)
                        e.wait_ge(x2_ok, 3 * m + g + 1)
                        e.sem_inc(t_free, 1)

                def step(m, first=False, final=False):
                    if last and not first:
                        residual(m - 1)
                    low(m)
                    if final and meanwhile:
                        meanwhile(e)
                    total(m)

                step(0, first=True)
                with e.Fori(1, KT - 1) as m:
                    step(m)
                step(KT - 1, final=True)
                if last:
                    residual(KT - 1)
            return dict(st=st, z_full=(z_full, 6 * KT), w_ok=w_ok, u_done=u_done)

        def turned(e):
            e.wait_ge(ln0["lo"][0], ln0["lo"][1])
            e.wait_ge(s_acc, 1)

        h_got = [sem(f"h_got{u}") for u in range(H_IN)]
        h_h = sem("h_h")
        h_l = sem("h_l")
        h_row = lambda t, k: t[:, ds(k, 1), :].rearrange("p a n -> p (a n)")

        def relu_low(e, k, source):
            e.wait_ge(h_h, k + 1)
            e.scalar_tensor_tensor(out=h_row(h_lo, k), in0=source, scalar=0.0, in1=h_row(h_hi, k).bitcast(F32),
                                   op0=ALU.max, op1=ALU.subtract).then_inc(h_l, 1)

        l0 = layer("l0", slabs0, 0, False, turned, nothing, lambda e: e.wait_ge(s_drow, 6),
                   lambda e: [relu_low(e, k, h_in[:, k % H_IN, :]) for k in range(KT - 1)])

        def l0_products(e):
            e.wait_ge(l0["z_full"][0], 6 * (KT - 1) + 3)

        def l0_split(e):
            for u in range(2):
                e.wait_ge(l0["w_ok"][u], 2 * KT)

        slabs1 = first_slabs("l1", I["L0_gnn_W_self1"], I["L0_gnn_W_neigh1"], l0_split, l0_products)

        @on("sync")
        def _(e):
            for k in range(KT - 1):
                e.wait_ge(l0["st"], 16 * k + 16)
                if k >= H_IN:
                    e.wait_ge(h_l, k - H_IN + 1)
                e.dma_start(h_in[:, k % H_IN, :], h1_d[k]).then_inc(h_got[k % H_IN], 16)

        @on("scalar")
        def _(e):
            l0_products(e)
            for k in range(KT - 1):
                e.wait_ge(h_got[k % H_IN], 16 * (k // H_IN) + 16)
                e.activation(h_row(h_hi, k), h_in[:, k % H_IN, :], ACT.Relu).then_inc(h_h, 1)
            e.wait_ge(l0["u_done"], 3 * KT)
            e.activation(h_row(h_hi, KT - 1), layer_out[:], ACT.Relu).then_inc(h_h, 1)

        @on("vector")
        def _(e):
            relu_low(e, KT - 1, layer_out[:])

        def relued(e):
            e.wait_ge(h_l, KT)

        l1 = layer("l1", slabs1, 1, True, lambda e: (e.wait_ge(*l0["z_full"]), e.wait_ge(l0["st"], 16 * (KT - 1))),
                   relued, nothing)

        r_in = [sem(f"r_in{u}") for u in range(2)]
        r_ok = sem("r_ok")
        r_full = sem("r_full")
        rw1_view = I["L0_ffn_rw1"].rearrange("(k p) n -> p k n", p=128)

        @on("sync")
        def _(e):
            e.dma_start(rw2[:], I["L0_ffn_rw2"].rearrange("(k p) n -> p k n", p=128)).then_inc(s_small[2], 16)
            for u in range(2):
                e.wait_ge(l1["w_ok"][u], 2 * KT)
                e.dma_start(w_raw[:, u, :, :], rw1_view[:, :, 128 * u:128 * u + 128]).then_inc(r_in[u], 16)

        @on("gpsimd")
        def _(e):
            e.wait_ge(l1["z_full"][0], 6 * (KT - 1) + 3)
            for u in range(2):
                split_slab(e, u, r_in[u], 16, r_ok)
                rest_slab(e, u, r_ok, 2 * u + 1)

        ln2 = layer_norm("ln2", x2_d, lambda e: e.wait_ge(l1["st"], 16 * KT + 16), t_d, x2_all)

        r_hid = sem("r_hid")
        r_log = sem("r_log")
        r_zero = sem("r_zero")

        def normed(e):
            e.wait_ge(*ln2["lo"])

        @on("sync")
        def _(e):
            with e.Fori(1, KT // 2) as q:
                for u in range(2):
                    e.wait_ge(r_ok, 4 * q + 2 * u - 2)
                    e.dma_start(w_raw[:, u, :, :], rw1_view[:, :, ds(q * 256 + 128 * u, 128)]).then_inc(r_in[u], 16)

        @on("gpsimd")
        def _(e):
            with e.Fori(1, KT // 2) as q:
                for u in range(2):
                    e.wait_ge(r_full, 6 * q + 3 * u)
                    split_slab(e, u, r_in[u], 16 * q + 16, r_ok)
                    rest_slab(e, u, r_ok, 4 * q + 2 * u + 1)

        @on("tensor")
        def _(e):
            normed(e)
            e.wait_ge(s_small[2], 16)
            e.sem_inc(r_full, 3)
            e.sem_inc(r_hid, 6)
            e.wait_ge(r_zero, 1)
            e.matmul(ps[0:P, 6, 0:NT * NX], hidden[:, 0, 0:P], hidden[:, 0, 0:NT * NX], start=True, stop=True,
                     skip_group_check=True).then_inc(r_zero, 1)

            def head(m, u, q):
                e.wait_ge(r_ok, 2 * m + 2)
                product(e, 3 * u, u, lambda c: e.wait_ge(r_hid, 3 * m + c + 1), r_full)

            def tail(m, u, q):
                e.wait_ge(r_hid, 3 * m + 3 + 6)
                for i in range(NT):
                    mm = e.matmul(ps[0:P, 6, NX * i:NX * i + NX], hidden[:, u, P * i:P * i + P],
                                  rw2[:, ds(m, 1), :].rearrange("p a n -> p (a n)"), start=False, stop=True,
                                  skip_group_check=True)
                mm.then_inc(r_log, 1)
            skewed(e, KT, head, tail)

        @on("scalar")
        def _(e):
            e.wait_ge(s_small[5], 16)
            normed(e)
            e.sem_inc(r_log, 2)

            def head(m, u, q):
                e.wait_ge(r_log, m + 1)
                for c, (a, w) in enumerate(COLS):
                    wait_apart(e, r_full, 3 * m + c + 1 + 3)
                    e.activation(hidden[:, u, a:a + w], ps[:, 3 * u + c, 0:w], ACT.Silu, bias=bias[:, 2, ds(m, 1)])\
                        .then_inc(r_hid, 1)
            e.wait_ge(r_zero, 2)
            skewed(e, KT, head, lambda m, u, q: None)

        @on("vector")
        def _(e):
            normed(e)
            e.memset(hidden[:, 0, :], 0.0).then_inc(r_zero, 1)
            e.wait_ge(r_log, KT + 2)

        b_st = sem("b_st")

        @on("sync")
        def _(e):
            e.wait_ge(*ln2["sm"])
            e.dma_start(r_d.rearrange("(t p) n -> p t n", p=P), x2_all[:]).then_inc(b_st, 16)

        g_c = sem("g_c")
        g_v = sem("g_v")
        g_ls = sem("g_ls")
        g_ex = sem("g_ex")
        g_r = sem("g_r")
        g_cnt = sem("g_cnt")
        g_hot = sem("g_hot")
        g_ids = sem("g_ids")
        g_x = sem("g_x")
        g_ok = sem("g_ok")
        g_eb = sem("g_eb")
        g_w = sem("g_w")
        g_wT = sem("g_wT")
        g_b2 = sem("g_b2")

        @on("sync")
        def _(e):
            e.dma_start(rb2b[:], I["L0_ffn_rb2"].partition_broadcast(P)).then_inc(s_rb2, 16)
            e.dma_start(eb1c[:], I["L0_ffn_eb1"].rearrange("e (k p) -> p (e k)", p=128),
                        allow_slow_non_contiguous=True).then_inc(g_eb, 16)
            e.wait_ge(r_full, 3 * KT + 3)
            e.dma_start(eb2[:], I["L0_ffn_eb2"]).then_inc(g_b2, 16)

        @on("gpsimd")
        def _(e):
            e.memset(below[:], 1.0).then_inc(g_c, 1)
            e.memset(before[:], 1.0).then_inc(g_c, 1)
            e.iota(toki[:], [[P, NT]], base=0, channel_multiplier=1).then_inc(g_c, 1)
            e.iota(seqi[:], [[1, 128]], base=0, channel_multiplier=0).then_inc(g_c, 1)
            e.wait_ge(g_c, 4)
            e.affine_select(out=below[:], in_=below[:], compare_op=ALU.is_gt, fill=0.0, base=0,
                            pattern=[[1, NX], [-1, NX]], channel_multiplier=0).then_inc(g_c, 1)
            e.affine_select(out=before[:], in_=before[:], compare_op=ALU.is_gt, fill=0.0, base=0,
                            pattern=[[1, P]], channel_multiplier=-1).then_inc(g_c, 1)
            e.tensor_copy(tokf[:], toki[:]).then_inc(g_c, 1)
            e.tensor_copy(seqf[:], seqi[:]).then_inc(g_c, 1)

        @on("vector")
        def _(e):
            n = [0]

            def link(ins):
                n[0] += 1
                ins.then_inc(g_v, 1)
                e.wait_ge(g_v, n[0])

            e.wait_ge(g_c, 8)
            e.wait_ge(s_rb2, 16)
            over = lambda ap, t: ap.rearrange("p (a n) -> p a n", a=1).to_broadcast([P, t, NX])
            each = lambda ap: ap.rearrange("p (t a) -> p t a", a=1).to_broadcast([P, NT, NX])
            link(e.tensor_tensor(logit[:], ps[0:P, 6, 0:NT * NX].rearrange("p (t n) -> p t n", n=NX), over(rb2b[:], NT), ALU.add))
            link(e.tensor_reduce(peak[:], logit[:], AX.X, ALU.max))
            e.tensor_tensor(less[:], logit[:], each(peak[:]), ALU.subtract).then_inc(g_ls, 1)
            lf = logit[:].rearrange("p t (a n) -> p t a n", a=1).to_broadcast([P, NT, NX, NX])
            le = logit[:].rearrange("p t (n a) -> p t n a", a=1).to_broadcast([P, NT, NX, NX])
            link(e.tensor_tensor(cmpa[:], lf, le, ALU.is_gt))
            link(e.tensor_tensor(cmpb[:], lf, le, ALU.is_ge))
            link(e.tensor_tensor(cmpb[:], cmpb[:],
                                 below[:].rearrange("p (a n) m -> p a n m", a=1).to_broadcast([P, NT, NX, NX]), ALU.mult))
            link(e.tensor_tensor(cmpa[:], cmpa[:], cmpb[:], ALU.max))
            link(e.tensor_reduce(rank[:], cmpa[:], AX.X, ALU.add))
            link(e.tensor_scalar(sel[:], rank[:], float(TOP - 1), None, ALU.is_le))
            e.tensor_reduce(taken[:], sel[:].rearrange("p t n -> p n t"), AX.X, ALU.add).then_inc(g_r, 1)
            e.wait_ge(g_ex, 1)
            link(e.tensor_tensor(less[:], less[:], sel[:], ALU.mult))
            link(e.tensor_reduce(peak[:], less[:], AX.X, ALU.add))
            link(e.reciprocal(peak[:], peak[:]))
            link(e.tensor_tensor(less[:], less[:], each(peak[:]), ALU.mult))
            e.sem_inc(g_w, 1)
            e.wait_ge(g_cnt, 1)
            link(e.tensor_copy(cum[:, 0, :], ps[0:P, 7, 0:NX]))
            for t in range(1, NT):
                link(e.tensor_tensor(cum[:, t, :], cum[:, t - 1, :], sel[:, t - 1, :], ALU.add))
            link(e.tensor_scalar(steps[:], ps[0:P, 7, NX:2 * NX], 1.0 / M, 0.5 - 0.5 / M, ALU.mult, ALU.add))
            link(e.tensor_scalar(steps[:], steps[:], ROUND, ROUND, ALU.add, ALU.subtract))
            link(e.memset(first[:], 0.0))
            for x in range(1, NX):
                link(e.tensor_tensor(first[:, x:x + 1], first[:, x - 1:x], steps[:, x - 1:x], ALU.add))
            ids = seqf[0:1, 0:NS].rearrange("p (n a) -> p n a", a=1).to_broadcast([1, NS, NX - 1])
            fst = first[0:1, 1:NX].rearrange("p (a n) -> p a n", a=1).to_broadcast([1, NS, NX - 1])
            link(e.tensor_tensor(step_past[:], fst, ids, ALU.is_le))
            link(e.tensor_reduce(step_f[:], step_past[:], AX.X, ALU.add))
            e.tensor_copy(step_x[:], step_f[:]).then_inc(g_x, 1)
            link(e.tensor_scalar(steps[:], first[:], float(M), None, ALU.mult))
            link(e.tensor_tensor(cum[:], cum[:], over(steps[:], NT), ALU.add))
            for c in range(TOP):
                link(e.tensor_scalar(sel[:], rank[:], float(c), None, ALU.is_equal))
                link(e.tensor_tensor(cmpa[:, :, 0, :], sel[:], cum[:], ALU.mult))
                link(e.tensor_tensor(cmpb[:, :, 0, :], sel[:], less[:], ALU.mult))
                link(e.tensor_reduce(slotf[:, c, :], cmpa[:, :, 0, :], AX.X, ALU.add))
                link(e.tensor_reduce(weight[:, c, :], cmpb[:, :, 0, :], AX.X, ALU.add))
            link(e.tensor_copy(sloti[:], slotf[:]))
            link(e.tensor_scalar(block_[:], slotf[:], 1.0 / 128, 0.5 / 128 - 0.5, ALU.mult, ALU.add))
            link(e.tensor_scalar(block_[:], block_[:], ROUND, ROUND, ALU.add, ALU.subtract))
            link(e.scalar_tensor_tensor(out=slotf[:], in0=block_[:], scalar=-128.0, in1=slotf[:], op0=ALU.mult, op1=ALU.add))
            flat = lambda t, w: t[:].rearrange("p c t -> p (c t)").rearrange("p (n a) -> p n a", a=1).to_broadcast([P, TOP * NT, w])
            row = lambda w: seqf[:, 0:w].rearrange("p (a n) -> p a n", a=1).to_broadcast([P, TOP * NT, w])
            link(e.tensor_tensor(place_hot[:], row(128), flat(slotf, 128), ALU.is_equal))
            link(e.tensor_tensor(block_hot[:], row(NS * SUB), flat(block_, NS * SUB), ALU.is_equal))
            for c in range(TOP):
                half = block_hot[:, c * NT:(c + 1) * NT, :]
                e.tensor_tensor(half, half, tokf[:].rearrange("p (n a) -> p n a", a=1).to_broadcast([P, NT, NS * SUB]),
                                ALU.mult).then_inc(g_hot, 1)
            e.wait_ge(g_ids, 1)
            e.tensor_copy(ids_i[:], ps[:, 7, 64:64 + NS * SUB]).then_inc(g_ok, 1)

        @on("scalar")
        def _(e):
            e.wait_ge(g_ls, 1)
            e.activation(less[:], less[:], ACT.Exp).then_inc(g_ex, 1)
            for g, (t, n) in enumerate(GROUPS):
                e.wait_ge(g_wT, g + 1)
                e.activation(gate_T[:, P * t:P * (t + n)], ps[0:NX, g, 0:P * n], ACT.Copy).then_inc(g_w, 1)

        @on("tensor")
        def _(e):
            e.wait_ge(g_r, 1)
            e.matmul(ps[0:P, 7, 0:NX], before[:], taken[:], start=True, stop=True, skip_group_check=True)
            e.matmul(ps[0:P, 7, NX:2 * NX], ones[0:P, 0:P], taken[:], start=False, stop=True,
                     skip_group_check=True).then_inc(g_cnt, 1)
            e.wait_ge(g_w, 1)
            e.wait_ge(r_hid, 3 * KT + 6)
            for g, (t, n) in enumerate(GROUPS):
                for i in range(n):
                    mm = e.transpose(ps[0:NX, g, P * i:P * i + P], less[:, t + i, :], ident[0:P, 0:P])
                mm.then_inc(g_wT, 1)
            e.wait_ge(g_hot, 2)
            for i in range(TOP * NT):
                mm = e.matmul(ps[:, 7, 64:64 + NS * SUB], place_hot[:, i, :], block_hot[:, i, :],
                              start=(i == 0), stop=(i == TOP * NT - 1))
            mm.then_inc(g_ids, 1)

        m_win = [[sem(f"m_win{w}{u}") for u in range(2)] for w in range(2)]
        m_whi = [sem(f"m_whi{w}") for w in range(2)]
        m_wlo = [sem(f"m_wlo{w}") for w in range(2)]
        m_idx = sem("m_idx")
        m_xin = [[sem(f"m_xin{u}{b}") for b in range(SUB)] for u in range(2)]
        m_tx = sem("m_tx")
        m_xhi = sem("m_xhi")
        m_xlo = sem("m_xlo")
        m_g1 = sem("m_g1")
        m_h = sem("m_h")
        m_hhi = sem("m_hhi")
        m_hlo = sem("m_hlo")
        m_g2 = sem("m_g2")
        m_out = sem("m_out")
        m_st = [sem(f"m_st{u}") for u in range(2)]
        NB = SUB * 2
        w1_view = I["L0_ffn_ew1"].rearrange("e (k p) h -> e p k h", p=128)
        w2_view = I["L0_ffn_ew2"].rearrange("e (k p) n -> e p k n", p=128)

        def gated(e):
            e.wait_ge(g_x, 1)
            e.wait_ge(b_st, 16)
            e.wait_ge(g_w, 4)
            for u in range(2):
                e.wait_ge(ln2["t_st"][u], 16 * (NT // 2) + 16)

        @on("sync")
        def _(e):
            gated(e)
            for w in range(2):
                e.sem_inc(m_wlo[w], 2)

            def head(s, u, q):
                x = e.value_load(step_x[0:1, ds(s, 1)], min_val=0, max_val=NX - 1)
                for w, (raw, view) in enumerate(((w1_raw, w1_view), (w2_raw, w2_view))):
                    e.wait_ge(m_wlo[w], s + 1)
                    e.dma_start(raw[:, u], view[ds(x, 1)].rearrange("a p k n -> p (a k) n")).then_inc(m_win[w][u], 16)
            skewed(e, NS, head, lambda s, u, q: None)

        @on("gpsimd")
        def _(e):
            gated(e)
            e.wait_ge(g_ok, 1)
            e.sem_inc(m_tx, 8)

            def head(s, u, q):
                wait_apart(e, m_tx, 4 * s + 4)
                e.tensor_copy(id_now[:, u, :], ids_i[:, ds(s * SUB, SUB)]).then_inc(m_idx, 1)
                wait_apart(e, m_idx, s + 1)
                for b in range(SUB):
                    e.indirect_dma_start(out=x_rows[:, u, b, :], out_offset=None, in_=t_d[:, :],
                                         in_offset=bass.IndirectOffsetOnAxis(ap=id_now[:, u, b:b + 1], axis=0)).then_inc(m_xin[u][b], 16)
            skewed(e, NS, head, lambda s, u, q: None)

        @on("tensor")
        def _(e):
            gated(e)
            e.sem_inc(m_xlo, 2)
            e.sem_inc(m_h, 2)
            e.sem_inc(m_g1, 4)
            e.sem_inc(m_g2, 2 * NB)

            def turn(s, u, q, groups=range(4)):
                if groups[0] == 0:
                    for b in range(SUB):
                        e.wait_ge(m_xin[u][b], 16 * q + 16)
                for g in groups:
                    e.wait_ge(m_xlo, 4 * s + g + 1)
                    for k in range(2):
                        for b in range(SUB):
                            mm = e.transpose(ps[:, g % 2, k * M + 128 * b:k * M + 128 * b + 128],
                                             x_rows[:, u, b, 128 * (2 * g + k):128 * (2 * g + k + 1)], ident[:])
                    mm.then_inc(m_tx, 1)

            def head(s, u, q):
                e.wait_ge(m_wlo[0], s + 3)
                e.wait_ge(m_xlo, 4 * s + 4 + 2)
                for j in range(HK):
                    e.wait_ge(m_h, HK * s + j + 1)
                    n = 0
                    for k in range(KT):
                        for wt, xt in ((w1_hi, xt_hi), (w1_hi, xt_lo), (w1_lo, xt_hi)):
                            n += 1
                            mm = e.matmul(ps[:, 2 + j, 0:M], wt[:, u, k, 128 * j:128 * j + 128], xt[:, u, k, :],
                                          start=(n == 1), stop=(n == 3 * KT))
                    mm.then_inc(m_g1, 1)
                    if not isinstance(s, int) or s < NS - 1:
                        turn(s + 1, 1 - u, q + u, range(2 * j, 2 * j + 2))

            def tail(s, u, q):
                e.wait_ge(m_hlo, s + 1)
                e.wait_ge(m_wlo[1], s + 3)
                for b in range(SUB):
                    for half in range(2):
                        e.wait_ge(m_out, NB * s + NB + 2 * b + half + 1)
                        n = 0
                        for j in range(HK):
                            for ht, wt in ((hid_hi, w2_hi), (hid_hi, w2_lo), (hid_lo, w2_hi)):
                                n += 1
                                mm = e.matmul(ps[:, 4 + 2 * b + half, :], ht[:, u, j, 128 * b:128 * b + 128],
                                              wt[:, u, j, 512 * half:512 * half + 512], start=(n == 1), stop=(n == 3 * HK))
                        mm.then_inc(m_g2, 1)
            turn(0, 0, 0)
            skewed(e, NS, head, tail)

        def more(s):
            return not isinstance(s, int) or s < NS - 1

        group = lambda t, u, g: t[:, u, 2 * g:2 * g + 2, :]
        bank = lambda g: ps[:, g % 2, :].rearrange("p (k n) -> p k n", k=2)

        @on("scalar")
        def _(e):
            gated(e)
            e.wait_ge(g_eb, 16)

            def w1(s, u, q):
                e.wait_ge(m_win[0][u], 16 * q + 16)
                e.wait_ge(m_g1, HK * s + HK)
                e.activation(w1_hi[:, u], w1_raw[:, u], ACT.Copy).then_inc(m_whi[0], 1)

            def w2(s, u, q):
                e.wait_ge(m_win[1][u], 16 * q + 16)
                e.wait_ge(m_g2, NB * s + NB)
                e.activation(w2_hi[:, u], w2_raw[:, u], ACT.Copy).then_inc(m_whi[1], 1)

            def rows(s, u, q, groups=range(4)):
                for g in groups:
                    e.wait_ge(m_tx, 4 * s + g + 1 + 8)
                    e.activation(group(xt_hi, u, g), bank(g), ACT.Copy).then_inc(m_xhi, 1)

            def head(s, u, q):
                x = e.value_load(step_x[0:1, ds(s, 1)], min_val=0, max_val=NX - 1)
                for j in range(HK):
                    wait_apart(e, m_g1, HK * s + j + 1 + 4)
                    e.activation(hid[:, u, j, :], ps[:, 2 + j, 0:M], ACT.Silu, bias=eb1c[:, ds(x * HK + j, 1)]).then_inc(m_h, 1)
                    if more(s):
                        rows(s + 1, 1 - u, q + u, range(2 * j, 2 * j + 2))
                e.wait_ge(m_h, HK * s + HK + 2)
                e.wait_ge(m_g2, NB * s + NB)
                e.activation(hid_hi[:, u], hid[:, u], ACT.Copy).then_inc(m_hhi, 1)
                if more(s):
                    w1(s + 1, 1 - u, q + u)
                w2(s, u, q)

            def tail(s, u, q):
                e.wait_ge(m_out, NB * s + NB + 2 * NB)
                e.dma_start(o_d[ds(s * M, M), :].rearrange("(b p) n -> p b n", p=128), o_rows[:, u]).then_inc(m_st[u], 16)

            e.sem_inc(m_out, 2 * NB)
            for u in range(2):
                e.sem_inc(m_st[u], 16)
            w1(0, 0, 0)
            rows(0, 0, 0)
            skewed(e, NS, head, tail)

        @on("vector")
        def _(e):
            gated(e)

            def w(i, raw, hi, lo, s, u, q):
                e.wait_ge(m_whi[i], s + 1)
                e.tensor_tensor(lo[:, u], raw[:, u], hi[:, u].bitcast(F32), ALU.subtract).then_inc(m_wlo[i], 1)

            def rows(s, u, q, groups=range(4)):
                for g in groups:
                    e.wait_ge(m_xhi, 4 * s + g + 1)
                    e.tensor_tensor(group(xt_lo, u, g), bank(g), group(xt_hi, u, g).bitcast(F32), ALU.subtract).then_inc(m_xlo, 1)

            def head(s, u, q):
                if more(s):
                    rows(s + 1, 1 - u, q + u)
                e.wait_ge(m_hhi, s + 1)
                e.tensor_tensor(hid_lo[:, u], hid[:, u], hid_hi[:, u].bitcast(F32), ALU.subtract).then_inc(m_hlo, 1)
                if more(s):
                    w(0, w1_raw, w1_hi, w1_lo, s + 1, 1 - u, q + u)
                w(1, w2_raw, w2_hi, w2_lo, s, u, q)

            def tail(s, u, q):
                e.wait_ge(m_st[u], 16 * q + 16)
                for b in range(SUB):
                    for half in range(2):
                        e.wait_ge(m_g2, NB * s + 2 * b + half + 1 + 2 * NB)
                        cols = slice(512 * half, 512 * half + 512)
                        e.tensor_copy(o_rows[:, u, b, cols], ps[:, 4 + 2 * b + half, :]).then_inc(m_out, 1)
            w(0, w1_raw, w1_hi, w1_lo, 0, 0, 0)
            rows(0, 0, 0)
            skewed(e, NS, head, tail)

        f_idx = sem("f_idx")
        f_oin = [[sem(f"f_oin{c}{u}") for u in range(2)] for c in range(TOP)]
        f_rin = [sem(f"f_rin{u}") for u in range(2)]
        f_mix = sem("f_mix")
        f_bias = sem("f_bias")
        f_free = sem("f_free")
        f_y = sem("f_y")
        f_st = [sem(f"f_st{u}") for u in range(2)]

        @on("sync")
        def _(e):
            e.sem_inc(f_y, 2)
            for u in range(2):
                e.sem_inc(f_st[u], 16)
            e.wait_ge(m_g1, HK * NS + 4)

            def head(i, u, q):
                e.wait_ge(f_y, i + 1)
                e.dma_start(r_rows[:, u, :], r_d[ds(i * P, P), :]).then_inc(f_rin[u], 16)

            def tail(i, u, q):
                e.wait_ge(f_y, i + 3)
                e.dma_start(out[ds(i * P, P), :], y_rows[:, u, :]).then_inc(f_st[u], 16)
            skewed(e, NT, head, tail)
            for u in range(2):
                e.wait_ge(f_st[u], 16 * (NT // 2) + 16)

        @on("gpsimd")
        def _(e):
            for u in range(2):
                e.wait_ge(m_st[u], 16 * ((NS + 1 - u) // 2) + 16)

            def head(i, u, q):
                wait_apart(e, f_y, i + 1)
                e.tensor_copy(slot_now[:, u, :], sloti[:, :, ds(i, 1)].rearrange("p c a -> p (c a)")).then_inc(f_idx, 1)
                wait_apart(e, f_idx, i + 1)
                for c in range(TOP):
                    e.indirect_dma_start(out=pick[:, u, c, :], out_offset=None, in_=o_d[:, :],
                                         in_offset=bass.IndirectOffsetOnAxis(ap=slot_now[:, u, c:c + 1], axis=0)).then_inc(f_oin[c][u], 16)
            skewed(e, NT, head, lambda i, u, q: None)

        @on("vector")
        def _(e):
            def head(i, u, q):
                e.wait_ge(f_rin[u], 16 * q + 16)
                e.wait_ge(f_st[u], 16 * q + 16)
                e.wait_ge(f_bias, i + 1)
                y = y_rows[:, u, :]
                for half in range(2):
                    cols = slice(512 * half, 512 * half + 512)
                    mm = e.tensor_tensor(y[:, cols], ps[0:P, 4 + 2 * u + half, :], r_rows[:, u, cols], ALU.add)
                mm.then_inc(f_free, 1)
                for c in range(TOP):
                    e.wait_ge(f_free, TOP * i + c + 1 + 2)
                    e.wait_ge(f_oin[c][u], 16 * q + 16)
                    e.scalar_tensor_tensor(out=y, in0=pick[:, u, c, :], scalar=weight[:, c, ds(i, 1)], in1=y,
                                           op0=ALU.mult, op1=ALU.add).then_inc((f_free, f_y)[c], 1)
            pipeline(e, NT, (0, head))

        @on("tensor")
        def _(e):
            e.wait_ge(g_b2, 16)
            e.wait_ge(m_out, NB * NS + 2 * NB)
            e.sem_inc(f_free, 2)

            for i in range(NT):
                u = i % 2
                e.wait_ge(f_free, max(TOP * i - 1, 1))
                for half in range(2):
                    mm = e.matmul(ps[0:P, 4 + 2 * u + half, :], gate_T[:, P * i:P * i + P], eb2[:, 512 * half:512 * half + 512],
                                  start=True, stop=True)
                mm.then_inc(f_bias, 1)

        with nc.Block() as block:
            for engine, parts in ((block.sync, prog["sync"]), (block.scalar, prog["scalar"]),
                                  (block.vector, prog["vector"]), (block.gpsimd, prog["gpsimd"]),
                                  (block.tensor, prog["tensor"])):
                @engine
                def _(e, parts=parts):
                    for part in parts:
                        part(e)


_INS = ["x", "src", "dst", "L0_gnn_W_self0", "L0_gnn_W_neigh0", "L0_gnn_b0", "L0_gnn_W_self1", "L0_gnn_W_neigh1",
        "L0_gnn_b1", "L0_ffn_rw1", "L0_ffn_rb1", "L0_ffn_rw2", "L0_ffn_rb2", "L0_ffn_ew1", "L0_ffn_eb1",
        "L0_ffn_ew2", "L0_ffn_eb2"]


def kernel(**inputs):
    import numpy as np
    import concourse.bacc as bacc
    from concourse.bass_utils import run_bass_kernel_spmd

    nc = bacc.Bacc("TRN2", target_bir_lowering=False, num_devices=1)
    arrays, aps = {}, {}
    for name in _INS:
        a = np.ascontiguousarray(inputs[name])
        arrays[f"in_{name}"] = a
        aps[name] = nc.dram_tensor(f"in_{name}", a.shape, mybir.dt.from_np(a.dtype), kind="ExternalInput").ap()
    out = nc.dram_tensor("out_0", (N, D), F32, kind="ExternalOutput").ap()
    build(nc, aps, out)
    r = run_bass_kernel_spmd(nc, [arrays], core_ids=[0])
    return r.results[0]["out_0"]
```

```python
from contextlib import ExitStack

import concourse.bass as bass
from concourse import mybir

F32 = mybir.dt.float32
F32R = mybir.dt.float32r
BF16 = mybir.dt.bfloat16
F16 = mybir.dt.float16
I32 = mybir.dt.int32
U16 = mybir.dt.uint16
ALU = mybir.AluOpType
ACT = mybir.ActivationFunctionType
AX = mybir.AxisListType
ds = bass.ds

N = 1250
D = 1024
P = 125
NT = N // P
KT = D // 128
E = 40000
NCH = E // P
G = 4
W = 25
NW = N // W
KW = NT * W
SPAN = 1024
EXACT = 4096.0
FAST = NCH // G + NW
ROUNDS = NCH // G
SLOTS = 2 * KT
LEAD = 2
GROUPS = ((0, 4), (4, 4), (8, 2))
COLS = ((0, 418), (418, 416), (834, 416))
NX = 8
HID = 256
TOP = 2
M = 256
NS = (TOP * N + NX * (M - 1)) // M
SUB = M // 128
HK = HID // 128
EPS = 1e-5
ROUND = 1.5 * 2.0 ** 23


def pipeline(e, n, *stages):
    deepest = max(lag for lag, _ in stages)
    loops = (n - deepest - 1) // 2

    def plain(t):
        for lag, part in stages:
            if 0 <= t - lag < n:
                part(t - lag, (t - lag) % 2, (t - lag) // 2)
    for t in range(deepest):
        plain(t)
    with e.Fori(0, loops) as r:
        for b in range(2):
            for lag, part in stages:
                k = deepest + b - lag
                part(2 * r + k if k else 2 * r, k % 2, r + k // 2 if k // 2 else r)
    for t in range(deepest + 2 * loops, n + deepest):
        plain(t)


def skewed(e, n, head, tail):
    pipeline(e, n, (0, head), (1, tail))


def build(nc, I, out):
    ctx = ExitStack()
    with ctx:
        prog = {k: [] for k in ("sync", "scalar", "vector", "gpsimd", "tensor")}

        def on(engine):
            return prog[engine].append

        def sem(name):
            return ctx.enter_context(nc.semaphore(name))

        top = nc.sbuf_base + (-nc.sbuf_base) % 32
        R_H, R_A, R_ACC, R_SLAB, R_WORK = (top + x for x in (0, 80000, 130016, 155040, 179616))
        R_CONST = R_WORK + 25344

        class Region:
            def __init__(self, at):
                self.at = at

            def __call__(self, name, shape, dt):
                t = nc.alloc_sbuf_tensor_at(name, shape, dt, offset=self.at)
                size = 2 if dt in (BF16, F16, U16) else 4
                for s in shape[1:]:
                    size *= s
                self.at += size + (-size) % 32
                return t

        C = Region(R_CONST)
        ident = C("ident", [128, 128], F32)
        ones = C("ones", [128, 128], F32)
        bias = C("bias", [128, 3, KT], F32)
        ones_r = C("ones_r", [P, 128], F32R)
        rw2 = C("rw2", [128, KT, NX], F32)
        mv = C("mv", [P, 2, 2], F32)
        stats = C("stats", [P, 2, 2, 6], F32)
        rstd = C("rstd", [P, 2, 4], F32)
        epst = C("epst", [128, 1], F32)
        logit = C("logit", [P, NT, NX], F32)
        flagi = C("flagi", [1, 8], I32)
        deg_max = C("deg_max", [1, 8], F32)
        assert C.at <= R_CONST + 3072

        H = Region(R_H)
        h_hi = H("h_hi", [128, KT, N], F32R)
        h_lo = H("h_lo", [128, KT, N], F32R)

        adj = Region(R_A)("adj", [P, NT, N], F32R)
        adj_f = adj[:].bitcast(F32)
        S = Region(R_WORK)
        src_hot = S("src_hot", [P, 2, G, P], BF16)
        key_hot = S("key_hot", [P, 2, G, KW], BF16)
        seq_i = S("seq_i", [P, KW], I32)
        seq16 = S("seq16", [P, KW], F16)
        dcol = S("dcol", [P, NCH], F32)
        scol = S("scol", [P, NCH + G], F32)
        key = S("key", [P, NCH + G], F32)
        part = S("part", [P, NCH], F32)
        d_seq = S("d_seq", [P, NCH], I32)
        d_next = S("d_next", [P, NCH], I32)
        junk = S("junk", [P, NCH], F32)
        src_now = S("src_now", [P, 2, G], F32)
        key_now = S("key_now", [P, 2, G], F32)
        counted = S("counted", [P, 2, KW], F32)
        step_i = S("step_i", [P, FAST], I32)
        step_n = S("step_n", [P, FAST], F32)
        past = S("past", [NW, FAST], F32)
        past_d = S("past_d", [NW, FAST], F32)
        window = S("window", [P, FAST], F32)
        earlier = S("earlier", [NW, NW], F32)
        differ = S("differ", [NW, NW], F32)
        edge_i = S("edge_i", [NW, 1], I32)
        col = S("col", [P, 16], F32)
        assert S.at <= R_CONST
        S = Region(R_ACC + 16384)
        d_rows = S("d_rows", [80, 4, P], I32)
        s_rows = S("s_rows", [80, 4, P], I32)
        d_rowf = S("d_rowf", [80, 4, P], F32)
        s_rowf = S("s_rowf", [80, 4, P], F32)
        S = Region(R_CONST + 3072)
        tabj = S("tabj", [1, FAST], I32)
        tabc = S("tabc", [1, FAST], I32)

        L = Region(R_ACC)
        xn = L("xn", [P, 2, D], F32)
        xin = L("xin", [P, 2, D], F32)

        L = Region(R_SLAB)
        w_raw = L("w_raw", [128, 2, KT, 128], F32)
        w_hi = L("w_hi", [128, 2, KT, 128], F32R)
        w_lo = L("w_lo", [128, 2, KT, 128], F32R)
        L = Region(R_WORK)
        yT = L("yT", [128, N], F32)
        self_part = L("self_part", [128, N], F32)
        dinv_row = L("dinv_row", [128, N], F32)
        y_hi = L("y_hi", [P, NT, 128], F32R)
        y_lo = L("y_lo", [P, NT, 128], F32R)
        L = Region(R_ACC)
        layer_out = L("layer_out", [128, N], F32)
        x_slab = L("x_slab", [P, NT, 128], F32)
        x2_slab = L("x2_slab", [P, NT, 128], F32)
        L = Region(R_ACC)
        yT0 = L("yT0", [128, N], F32)
        self0 = L("self0", [128, N], F32)
        y_hi0 = L("y_hi0", [P, NT, 128], F32R)
        y_lo0 = L("y_lo0", [P, NT, 128], F32R)
        x2_all = Region(R_A)("x2_all", [P, NT, D], F32)
        hidden = Region(R_ACC + 8192)("hidden", [128, 2, N], F32)

        S = Region(R_CONST + 3072)
        rb2b = S("rb2b", [P, NX], F32)
        eb1c = S("eb1c", [128, NX * HK], F32)
        ids_i = S("ids_i", [128, NS * SUB], I32)
        id_now = S("id_now", [128, 2, SUB], I32)
        slot_now = S("slot_now", [P, 2, TOP], I32)
        sloti = S("sloti", [P, TOP, NT], I32)
        weight = S("weight", [P, TOP, NT], F32)
        step_x = S("step_x", [1, NS], I32)
        taken = S("taken", [P, NX], F32)
        S = Region(R_WORK)
        before = S("before", [P, P], F32)
        below = S("below", [P, NX, NX], F32)
        toki = S("toki", [P, NT], I32)
        seqi = S("seqi", [P, 128], I32)
        tokf = S("tokf", [P, NT], F32)
        seqf = S("seqf", [P, 128], F32)
        peak = S("peak", [P, NT], F32)
        less = S("less", [P, NT, NX], F32)
        rank = S("rank", [P, NT, NX], F32)
        sel = S("sel", [P, NT, NX], F32)
        cum = S("cum", [P, NT, NX], F32)
        cmpa = S("cmpa", [P, NT, NX, NX], F32)
        cmpb = S("cmpb", [P, NT, NX, NX], F32)
        steps = S("steps", [P, NX], F32)
        first = S("first", [P, NX], F32)
        slotf = S("slotf", [P, TOP, NT], F32)
        block_ = S("block_", [P, TOP, NT], F32)
        step_past = S("step_past", [1, NS, NX - 1], F32)
        step_f = S("step_f", [1, NS], F32)
        place_hot = S("place_hot", [P, TOP * NT, 128], F16)
        block_hot = S("block_hot", [P, TOP * NT, NS * SUB], F16)

        S = Region(R_H)
        w1_raw = S("w1_raw", [128, 2, KT, HID], F32)
        w1_hi = S("w1_hi", [128, 2, KT, HID], F32R)
        w1_lo = S("w1_lo", [128, 2, KT, HID], F32R)
        w2_raw = S("w2_raw", [128, 2, HK, D], F32)
        w2_hi = S("w2_hi", [128, 2, HK, D], F32R)
        w2_lo = S("w2_lo", [128, 2, HK, D], F32R)
        x_rows = S("x_rows", [128, 2, SUB, D], F32)
        xt_hi = S("xt_hi", [128, 2, KT, M], F32R)
        xt_lo = S("xt_lo", [128, 2, KT, M], F32R)
        hid = S("hid", [128, 2, HK, M], F32)
        hid_hi = S("hid_hi", [128, 2, HK, M], F32R)
        hid_lo = S("hid_lo", [128, 2, HK, M], F32R)
        gate_T = S("gate_T", [NX, N], F32)
        eb2 = S("eb2", [NX, D], F32)
        assert S.at <= R_WORK
        S = Region(R_WORK)
        o_rows = S("o_rows", [128, 2, SUB, D], F32)
        assert S.at <= R_CONST
        r_all = Region(R_H)("r_all", [P, NT, D], F32)
        pick = Region(R_H + 49152)("pick", [P, 2, TOP, D], F32)

        ps = ctx.enter_context(nc.psum_tensor("ps", [128, 8, 512], F32))

        o_d = nc.dram_tensor("o_d", (NS * M, D), F32, kind="Internal").ap()
        y_d = nc.dram_tensor("y_d", (KT, 2, P, NT, 128), F32, kind="Internal").ap()
        self_d = nc.dram_tensor("self_d", (KT, 128, N), F32, kind="Internal").ap()
        x2_d = nc.dram_tensor("x2_d", (N, D), F32, kind="Internal").ap()
        t_d = nc.dram_tensor("t_d", (N, D), F32, kind="Internal").ap()
        r_d = nc.dram_tensor("r_d", (N, D), F32, kind="Internal").ap()

        s_id = sem("s_id")
        s_rb2 = sem("s_rb2")
        s_ones = sem("s_ones")
        s_none = sem("s_none")
        s_small = [sem(f"s_small{i}") for i in range(6)]

        def wait_apart(e, sem, value):
            e.wait_ge(sem, value)
            e.sem_inc(s_none, 1)

        @on("gpsimd")
        def _(e):
            e.memset(ident[:], 0.0).then_inc(s_id, 1)
            e.wait_ge(s_id, 1)
            e.affine_select(out=ident[:], in_=ident[:], compare_op=ALU.not_equal, fill=1.0, base=0,
                            pattern=[[-1, 128]], channel_multiplier=1).then_inc(s_id, 1)
            e.memset(ones[:], 1.0).then_inc(s_ones, 1)
            e.memset(epst[:], EPS).then_inc(s_ones, 1)

        @on("sync")
        def _(e):
            e.dma_start(s_rows[:], I["src"].rearrange("(t p n) -> p t n", p=80, n=P)).then_inc(s_small[1], 16)
            for b, name in enumerate(("L0_gnn_b0", "L0_gnn_b1", "L0_ffn_rb1")):
                e.dma_start(bias[:, b, :], I[name].rearrange("(k p) -> p k", p=128),
                            allow_slow_non_contiguous=True).then_inc(s_small[3 + b], 16)

        s_seq = sem("s_seq")
        s_next = sem("s_next")
        s_tb = sem("s_tb")
        s_iota = sem("s_iota")
        s_ecast = sem("s_ecast")
        s_etp = sem("s_etp")
        s_tab = sem("s_tab")
        s_dn = sem("s_dn")

        @on("scalar")
        def _(e):
            e.dma_start(d_rows[:], I["dst"].rearrange("(t p n) -> p t n", p=80, n=P)).then_inc(s_small[0], 16)
            e.dma_start(d_seq[:], I["dst"].rearrange("(p n) -> p n", p=P)).then_inc(s_seq, 16)
            e.wait_ge(s_dn, 1)
            e.dma_start(d_next[0:P - 1, :], I["dst"][1:1 + (P - 1) * NCH].rearrange("(p n) -> p n", p=P - 1)).then_inc(s_next, 16)
            e.dma_start(d_next[P - 1:P, 0:NCH - 1], I["dst"][1 + (P - 1) * NCH:E].rearrange("(p n) -> p n", p=1)).then_inc(s_next, 16)

        @on("gpsimd")
        def _(e):
            e.memset(d_next[:], 1 << 20).then_inc(s_dn, 1)
            e.iota(seq_i[:], [[1, KW]], base=0, channel_multiplier=0).then_inc(s_iota, 1)
            e.iota(step_i[:], [[1, FAST]], base=0, channel_multiplier=0).then_inc(s_iota, 1)
            e.iota(edge_i[:], [[1, 1]], base=0, channel_multiplier=W).then_inc(s_iota, 1)
            e.memset(earlier[:], 1.0).then_inc(s_iota, 1)
            e.memset(key[:, NCH:], -1.0).then_inc(s_iota, 1)
            e.memset(scol[:, NCH:], -1.0).then_inc(s_iota, 1)
            e.wait_ge(s_iota, 6)
            e.tensor_copy(seq16[:], seq_i[:]).then_inc(s_iota, 1)
            e.affine_select(out=earlier[:], in_=earlier[:], compare_op=ALU.is_gt, fill=0.0, base=0,
                            pattern=[[1, NW]], channel_multiplier=-1).then_inc(s_iota, 1)
            e.affine_select(out=differ[:], in_=ident[0:NW, 0:NW], compare_op=ALU.not_equal, fill=-1.0, base=-1,
                            pattern=[[1, NW]], channel_multiplier=-1).then_inc(s_iota, 1)

        @on("vector")
        def _(e):
            e.wait_ge(s_small[0], 16)
            e.tensor_copy(d_rowf[:], d_rows[:]).then_inc(s_ecast, 1)
            e.wait_ge(s_small[1], 16)
            e.tensor_copy(s_rowf[:], s_rows[:]).then_inc(s_ecast, 1)
            n = [0]

            def link(ins):
                n[0] += 1
                ins.then_inc(s_tb, 1)
                e.wait_ge(s_tb, n[0])

            def rounded(out, in_, d):
                link(e.tensor_scalar(out, in_, 1.0 / d, 0.5 / d - 0.5, ALU.mult, ALU.add))
                link(e.tensor_scalar(out, out, ROUND, ROUND, ALU.add, ALU.subtract))

            low, high, c0, e0, runs, first_, o, dd = (col[0:NW, i:i + 1] for i in range(8))
            e.wait_ge(s_etp, 1)
            link(e.tensor_copy(dcol[:], ps[0:P, 0, 0:NCH]))
            e.wait_ge(s_iota, 9)
            link(e.tensor_copy(low, edge_i[:]))
            link(e.tensor_scalar(high, low, float(W), None, ALU.add))
            link(e.tensor_copy(step_n[:], step_i[:]))
            e.wait_ge(s_etp, 2)
            link(e.tensor_scalar(junk[0:NW, :], ps[0:NW, 3, 0:NCH], low, None, ALU.is_lt))
            link(e.tensor_reduce(c0, junk[0:NW, :], AX.X, ALU.add))
            link(e.tensor_scalar(junk[0:NW, :], ps[0:NW, 2, 0:NCH], high, None, ALU.is_lt))
            link(e.tensor_reduce(e0, junk[0:NW, :], AX.X, ALU.add))
            link(e.tensor_tensor(runs, e0, c0, ALU.subtract))
            link(e.tensor_scalar(runs, runs, 1.0 / G, 0.5 - 0.5 / G, ALU.mult, ALU.add))
            link(e.tensor_scalar(runs, runs, ROUND, ROUND, ALU.add, ALU.subtract))
            e.sem_inc(s_ecast, 1)
            e.wait_ge(s_etp, 3)
            link(e.tensor_copy(scol[:, 0:NCH], ps[0:P, 1, 0:NCH]))
            rounded(key[:, 0:NCH], scol[:, 0:NCH], P)
            link(e.scalar_tensor_tensor(out=scol[:, 0:NCH], in0=key[:, 0:NCH], scalar=-float(P), in1=scol[:, 0:NCH],
                                        op0=ALU.mult, op1=ALU.add))
            link(e.scalar_tensor_tensor(out=key[:, 0:NCH], in0=key[:, 0:NCH], scalar=float(W), in1=dcol[:],
                                        op0=ALU.mult, op1=ALU.add))
            rounded(part[:], dcol[:], W)
            link(e.scalar_tensor_tensor(out=key[:, 0:NCH], in0=part[:], scalar=float(SPAN - W), in1=key[:, 0:NCH],
                                        op0=ALU.mult, op1=ALU.add))
            e.wait_ge(s_etp, 4)
            link(e.tensor_copy(first_, ps[0:NW, 4, 0:1]))
            link(e.scalar_tensor_tensor(out=o, in0=first_, scalar=-float(G), in1=c0, op0=ALU.mult, op1=ALU.add))
            e.sem_inc(s_ecast, 1)
            e.wait_ge(s_etp, 5)
            link(e.tensor_copy(dd, ps[0:NW, 4, 8:9]))
            link(e.tensor_scalar(past[:], step_n[0:NW, :], first_, None, ALU.is_ge))
            link(e.tensor_scalar(past_d[:], past[:], dd, None, ALU.mult))
            e.sem_inc(s_ecast, 1)
            e.wait_ge(s_next, 32)
            e.wait_ge(s_seq, 16)
            link(e.tensor_tensor(junk[:], d_seq[:], d_next[:], ALU.is_gt))
            link(e.tensor_reduce(col[:, 8:9], junk[:], AX.X, ALU.add))
            e.sem_inc(s_ecast, 1)
            e.wait_ge(s_etp, 6)
            link(e.tensor_scalar(window[:], ps[0:P, 5, 0:FAST], -float(SPAN), float(SPAN), ALU.mult, ALU.add))
            link(e.tensor_scalar(tabj[:], ps[0:1, 5, 0:FAST], 1.0, None, ALU.subtract))
            e.wait_ge(s_etp, 7)
            link(e.tensor_scalar(col[0:1, 14:15], ps[0:1, 4, 16:17], 0.0, None, ALU.is_gt))
            link(e.tensor_copy(flagi[:, 0:1], col[0:1, 14:15]))
            link(e.tensor_scalar(col[0:1, 13:14], col[0:1, 14:15], float(NCH), None, ALU.mult))
            link(e.scalar_tensor_tensor(out=junk[0:1, 0:FAST], in0=step_n[0:1, :], scalar=float(G),
                                        in1=ps[0:1, 5, 256:256 + FAST], op0=ALU.mult, op1=ALU.add))
            link(e.tensor_scalar(tabc[:], junk[0:1, 0:FAST], col[0:1, 13:14], float(NCH), ALU.max, ALU.min))
            link(e.memset(col[:, 9:10], 0.0))
            link(e.memset(col[:, 15:16], -float(SPAN)))
            e.tensor_copy(ones_r[:], ones[0:P, :]).then_inc(s_tab, 1)

        @on("tensor")
        def _(e):
            e.wait_ge(s_id, 2)
            e.wait_ge(s_ones, 1)

            def turn(i, rows):
                e.wait_ge(s_ecast, i + 1)
                for t in range(4):
                    mm = e.transpose(ps[0:P, i, 80 * t:80 * t + 80], rows[:, t, :], ident[0:80, 0:80])
                mm.then_inc(s_etp, 1)
            turn(0, d_rowf)
            e.wait_ge(s_tb, 1)
            for bank, row in ((2, 0), (3, P - 1)):
                mm = e.matmul(ps[0:NW, bank, 0:NCH], ident[0:P, row:row + 1].to_broadcast([P, NW]), dcol[:],
                              start=True, stop=True)
            mm.then_inc(s_etp, 1)
            turn(1, s_rowf)
            e.wait_ge(s_iota, 9)
            e.wait_ge(s_ecast, 3)
            e.matmul(ps[0:NW, 4, 0:1], earlier[:], col[0:NW, 4:5], start=True, stop=True).then_inc(s_etp, 1)
            e.wait_ge(s_ecast, 4)
            e.matmul(ps[0:NW, 4, 8:9], differ[:], col[0:NW, 6:7], start=True, stop=True).then_inc(s_etp, 1)
            e.wait_ge(s_ecast, 5)
            for at, t in ((0, past), (256, past_d)):
                mm = e.matmul(ps[0:P, 5, at:at + FAST], ones[0:NW, 0:P], t[:], start=True, stop=True)
            mm.then_inc(s_etp, 1)
            e.wait_ge(s_ecast, 6)
            e.matmul(ps[0:1, 4, 16:17], ones[0:P, 0:1], col[:, 8:9], start=True, stop=True).then_inc(s_etp, 1)

        def split_slab(e, u, loaded, value, done):
            wait_apart(e, loaded, value)
            e.tensor_copy(w_hi[:, u, :, :], w_raw[:, u, :, :]).then_inc(done, 1)

        def rest_slab(e, u, done, value):
            e.wait_ge(done, value)
            e.tensor_tensor(w_lo[:, u, :, :], w_raw[:, u, :, :], w_hi[:, u, :, :].bitcast(F32), ALU.subtract).then_inc(done, 1)

        def product(e, bank, u, wait, full):
            for c, (a, w) in enumerate(COLS):
                wait(c)
                passes = ((w_hi, h_hi), (w_hi, h_lo), (w_lo, h_hi))
                n = 0
                for k in range(KT):
                    for wt, ht in passes:
                        n += 1
                        mm = e.matmul(ps[:, bank + c, 0:w], wt[:, u, k, :], ht[:, k, a:a + w],
                                      start=(n == 1), stop=(n == 3 * KT))
                mm.then_inc(full, 1)

        view = lambda w: w.rearrange("(k p) n -> p k n", p=128)

        def first_slabs(tag, w_self, w_neigh, loadable, splittable, split=2):
            x_full = sem(f"{tag}_xfull")
            z_full = sem(f"{tag}_zfull")
            w_in = [sem(f"{tag}_win{u}") for u in range(2)]
            w_ok = [sem(f"{tag}_wok{u}") for u in range(2)]

            @on("sync")
            def _(e):
                loadable(e)
                for u, w in enumerate((w_neigh, w_self)):
                    e.dma_start(w_raw[:, u, :, :], view(w)[:, :, 0:128]).then_inc(w_in[u], 16)

            @on("gpsimd")
            def _(e):
                splittable(e)
                for u in range(split):
                    split_slab(e, u, w_in[u], 16, w_ok[u])
                    rest_slab(e, u, w_ok[u], 1)
            return w_self, w_neigh, x_full, z_full, w_in, w_ok

        nothing = lambda e: None
        slabs0 = first_slabs("l0", I["L0_gnn_W_self0"], I["L0_gnn_W_neigh0"], nothing, nothing, 1)

        def layer_norm(tag, src, free, t_out=None, kept=None):
            rows = (lambda i, u: kept[:, ds(i, 1), :].rearrange("p a n -> p (a n)")) if kept is not None else \
                (lambda i, u: xin[:, u, :])
            x_in = [sem(f"{tag}_in{u}") for u in range(2)]
            st = sem(f"{tag}_st")
            sq = sem(f"{tag}_sq")
            xr = sem(f"{tag}_xr")
            tp = sem(f"{tag}_tp")
            hi = sem(f"{tag}_hi")
            lo = sem(f"{tag}_lo")
            t_st = [sem(f"{tag}_ts{u}") for u in range(2)] if kept is not None else []
            sm = sem(f"{tag}_sm") if kept is not None else None

            @on("sync")
            def _(e):
                free(e)
                e.sem_inc(xr, 2)

                def load(i, u):
                    e.dma_start(rows(i, u), src[ds(i * P, P), :]).then_inc(x_in[u], 16)

                def store(i, u):
                    e.wait_ge(xr, i + 3)
                    e.dma_start(t_out[ds(i * P, P), :], xn[:, u, :]).then_inc(t_st[u], 16)

                for u in range(2):
                    load(u, u)
                with e.Fori(1, NT // 2) as q:
                    for u in range(2):
                        if kept is None:
                            e.wait_ge(xr, 2 * q + u + 1)
                        else:
                            e.wait_ge(st, 8 * q + 4 * u - 7)
                        load(2 * q + u, u)
                        if kept is not None:
                            store(2 * q + u - 2, u)
                if kept is not None:
                    for u in range(2):
                        store(NT - 2 + u, u)

            def bank(u, g):
                return ps[:, 4 + 2 * u + g, 0:4 * P].rearrange("p (k n) -> p k n", k=4)

            def part_of(h, i, g):
                return h[:, 4 * g:4 * g + 4, ds(i * P, P)]

            @on("vector")
            def _(e):
                free(e)

                def moments(i, u, q):
                    e.wait_ge(x_in[u], 16 * q + 16)
                    for g in range(2):
                        mm = e.bn_stats(stats[:, u, g, :], rows(i, u)[:, 512 * g:512 * g + 512])
                    mm.then_inc(st, 1)
                    wait_apart(e, st, 4 * i + 1)
                    e.bn_aggr(mv[:, u, :], stats[:, u, :, :].rearrange("p a b -> p (a b)")).then_inc(st, 1)

                def low(i, u, q):
                    for g in range(2):
                        e.wait_ge(hi, 2 * i + g + 1)
                        e.tensor_tensor(part_of(h_lo, i, g), bank(u, g), part_of(h_hi, i, g).bitcast(F32),
                                        ALU.subtract).then_inc(lo, 1)

                def inverse(i, u, q):
                    e.wait_ge(sq, i + 1)
                    e.reciprocal(rstd[:, u, 1:2], rstd[:, u, 0:1]).then_inc(st, 1)
                    e.wait_ge(st, 4 * i + 3)
                    e.scalar_tensor_tensor(out=rstd[:, u, 2:3], in0=mv[:, u, 0:1], scalar=-1.0,
                                           in1=rstd[:, u, 1:2], op0=ALU.mult, op1=ALU.mult).then_inc(st, 1)

                pipeline(e, NT, (0, moments), (2, low), (0, inverse))

            @on("scalar")
            def _(e):
                e.wait_ge(s_ones, 2)
                free(e)
                if kept is not None:
                    for u in range(2):
                        e.sem_inc(t_st[u], 16)
                    e.sem_inc(sm, 2)

                def deviation(i, u, q):
                    e.wait_ge(st, 4 * i + 2)
                    e.activation(rstd[:, u, 0:1], mv[:, u, 1:2], ACT.Sqrt, bias=epst[0:P, :]).then_inc(sq, 1)

                def high(i, u, q):
                    for g in range(2):
                        wait_apart(e, tp, 2 * i + g + 1 + 2)
                        e.activation(part_of(h_hi, i, g), bank(u, g), ACT.Copy).then_inc(hi, 1)

                def normal(i, u, q):
                    e.wait_ge(st, 4 * i + 4)
                    e.wait_ge(tp, 2 * i)
                    if kept is not None:
                        e.wait_ge(t_st[u], 16 * q + 16)
                        wait_apart(e, sm, i + 1)
                    e.activation(xn[:, u, :], rows(i, u), ACT.Identity, bias=rstd[:, u, 2:3],
                                 scale=rstd[:, u, 1:2]).then_inc(xr, 1)

                pipeline(e, NT, (0, deviation), (1, high), (0, normal))

            @on("tensor")
            def _(e):
                free(e)
                e.sem_inc(tp, 2)
                e.sem_inc(lo, 4)

                def head(i, u, q):
                    e.wait_ge(xr, i + 3)
                    for g in range(2):
                        e.wait_ge(lo, 2 * i + g + 1)
                        for k in range(4):
                            mm = e.transpose(ps[:, 4 + 2 * u + g, k * P:k * P + P],
                                             xn[:, u, 128 * (4 * g + k):128 * (4 * g + k + 1)], ident[0:P, 0:P])
                        mm.then_inc(tp, 1)
                pipeline(e, NT, (0, head))
            if kept is not None:
                @on("gpsimd")
                def _(e):
                    def add(i, u, q):
                        e.wait_ge(xr, i + 3)
                        e.tensor_tensor(rows(i, u), rows(i, u), xn[:, u, :], ALU.add).then_inc(sm, 1)
                    pipeline(e, NT, (0, add))
            return dict(lo=(lo, 2 * NT + 4), t_st=t_st, sm=(sm, NT + 2))

        ln0 = layer_norm("ln0", I["x"], lambda e: None)

        s_az = sem("s_az")
        s_acc = sem("s_acc")

        @on("gpsimd")
        def _(e):
            e.memset(adj_f, 0.0).then_inc(s_az, 1)

        class Counts:
            def __init__(self, tag):
                self.now = sem(f"{tag}_now")
                self.hot = sem(f"{tag}_hot")
                self.prod = sem(f"{tag}_prod")
                self.out = sem(f"{tag}_out")
                self.took = sem(f"{tag}_took")

            def start(self, e):
                e.sem_inc(self.hot, 2)
                e.sem_inc(self.prod, 2)
                e.sem_inc(self.out, 1)
                e.sem_inc(self.took, 2)

            def place(self, e, n, u, c, base):
                wait_apart(e, self.hot, n + 1)
                e.activation(src_now[:, u, :], scol[:, ds(c, G)], ACT.Copy)
                e.activation(key_now[:, u, :], key[:, ds(c, G)], ACT.Identity, bias=base).then_inc(self.now, 1)

            def evict(self, e, n, u):
                e.wait_ge(self.took, n + 1)
                wait_apart(e, self.prod, n + 3)
                e.activation(counted[:, u, :], ps[0:P, 6, 0:KW], ACT.Copy).then_inc(self.out, 1)

            def rows(self, e, n, u):
                e.wait_ge(self.now, n + 1)
                e.wait_ge(self.prod, n + 1)
                for g in range(G):
                    e.tensor_scalar(src_hot[:, u, g, :], seq16[:, 0:P], src_now[:, u, g:g + 1], None, ALU.is_equal)
                for g in range(G):
                    ins = e.tensor_scalar(key_hot[:, u, g, :], seq16[:], key_now[:, u, g:g + 1], None, ALU.is_equal)
                ins.then_inc(self.hot, 1)

            def multiply(self, e, n, u):
                e.wait_ge(self.hot, n + 3)
                e.wait_ge(self.out, n + 1)
                for g in range(G):
                    mm = e.matmul(ps[0:P, 6, 0:KW], src_hot[:, u, g, :], key_hot[:, u, g, :], start=(g == 0), stop=(g == G - 1))
                mm.then_inc(self.prod, 1)

            def add(self, e, n, u, j):
                e.wait_ge(self.out, n + 2)
                wait_apart(e, self.took, n + 2)
                cols = adj_f[:, :, ds(j * W, W)]
                e.tensor_tensor(cols, counted[:, u, :].rearrange("p (t w) -> p t w", t=NT), cols, ALU.add).then_inc(self.took, 1)

        def window_of(e, s):
            return e.value_load(tabj[0:1, ds(s, 1)], min_val=0, max_val=NW - 1)

        def chunk_of(e, s):
            return e.value_load(tabc[0:1, ds(s, 1)], min_val=0, max_val=NCH)

        moved = sem("moved")
        s_any = sem("s_any")
        any_order, by_order = Counts("any"), Counts("sorted")

        def unsorted(engine):
            @on(engine)
            def _(e):
                e.wait_ge(s_tab, 1)
                e.wait_ge(s_az, 1)
                if engine == "tensor":
                    any_order.start(e)
                    by_order.start(e)
                base = col[:, 9:10]
                flag = e.value_load(flagi[0:1, 0:1], min_val=0, max_val=1)
                with e.If(flag):
                    with e.Fori(0, NW) as j:
                        n = j * ROUNDS
                        pipeline(e, ROUNDS, *dict(
                            scalar=((0, lambda s, u, q: any_order.place(e, n + s, u, s * G, base)),
                                    (2, lambda s, u, q: any_order.evict(e, n + s, u))),
                            vector=((0, lambda s, u, q: any_order.rows(e, n + s, u)),),
                            tensor=((0, lambda s, u, q: any_order.multiply(e, n + s, u)),),
                            gpsimd=((0, lambda s, u, q: any_order.add(e, n + s, u, j)),))[engine])
                        if engine == "scalar":
                            wait_apart(e, any_order.now, n + ROUNDS)
                            e.activation(base, base, ACT.Identity, bias=col[:, 15:16]).then_inc(moved, 1)
                            e.wait_ge(moved, j + 1)
                    if engine == "gpsimd":
                        e.wait_ge(any_order.took, NW * ROUNDS + 2)
                with e.Else():
                    e.sem_inc(s_none, 1)
                if engine == "gpsimd":
                    e.sem_inc(s_any, 1)
        for engine in ("scalar", "vector", "gpsimd", "tensor"):
            unsorted(engine)

        assert FAST == SLOTS * KT + LEAD
        _, _, x_full, z_full, w_in, w_ok = slabs0
        x_free = sem("x_free")
        own_out = sem("own_out")
        t_full = sem("t_full")
        t_hi = sem("t_hi")
        t_free = sem("t_free")
        y_st = sem("y_st")
        TURNS = {9: 0, 12: 1, 15: 2}

        def high_group(e, g, out):
            t, n = GROUPS[g]
            return out[:, t:t + n, :], ps[0:P, 7, 0:128 * n].rearrange("p (k n) -> p k n", k=n)

        def tiles(e, body):
            with e.Fori(0, KT - 1) as m:
                body(m, False)
            body(KT - 1, True)

        @on("tensor")
        def _(e):
            e.wait_ge(*ln0["lo"])
            e.sem_inc(x_free, 3)
            e.sem_inc(own_out, 3)
            e.sem_inc(z_full, 3)
            e.sem_inc(t_free, 1)

            def body(m, last):
                for t in range(SLOTS):
                    own, k = divmod(t, KT)
                    if k == 0:
                        e.wait_ge(w_ok[own], 2 * m + 2)
                    for p, (wt, ht) in enumerate(((w_hi, h_hi), (w_hi, h_lo), (w_lo, h_hi))):
                        for c, (a, w) in enumerate(COLS):
                            if k == 0 and p == 0:
                                e.wait_ge((x_free, own_out)[own], 3 * m + c + 1)
                            mm = e.matmul(ps[:, 3 * own + c, 0:w], wt[:, own, k, :], ht[:, k, a:a + w],
                                          start=(k == 0 and p == 0), stop=(k == KT - 1 and p == 2))
                            if k == KT - 1 and p == 2:
                                mm.then_inc((x_full, z_full)[own], 1)
                    if t in TURNS:
                        g = TURNS[t]
                        e.wait_ge(x_free, 3 * m + 6)
                        e.wait_ge(t_free, 3 * m + g + 1)
                        i0, n = GROUPS[g]
                        for i in range(n):
                            mm = e.transpose(ps[0:P, 7, 128 * i:128 * i + 128], yT0[:, P * (i0 + i):P * (i0 + i + 1)], ident[:])
                        mm.then_inc(t_full, 1)
                    by_order.multiply(e, SLOTS * m + t, t % 2)
            tiles(e, body)
            for n in range(SLOTS * KT, FAST):
                by_order.multiply(e, n, n % 2)

        @on("scalar")
        def _(e):
            e.wait_ge(s_small[3], 16)
            e.wait_ge(*ln0["lo"])
            e.wait_ge(s_any, 1)

            def place(s, u):
                by_order.place(e, s, u, chunk_of(e, s), window[:, ds(s, 1)])
            for s in range(LEAD):
                place(s, s % 2)

            def body(m, last):
                for t in range(SLOTS):
                    place(SLOTS * m + t + LEAD, t % 2)
                    by_order.evict(e, SLOTS * m + t, t % 2)
                    if t == KT - 1:
                        for c, (a, w) in enumerate(COLS):
                            e.wait_ge(x_full, 3 * m + c + 1)
                            e.activation(yT0[:, a:a + w], ps[:, c, 0:w], ACT.Copy).then_inc(x_free, 1)
                    if t in TURNS:
                        if TURNS[t] == 0:
                            e.wait_ge(y_st, 48 * m + 16)
                        e.wait_ge(t_full, 3 * m + TURNS[t] + 1)
                        to, bank = high_group(e, TURNS[t], y_hi0)
                        e.activation(to, bank, ACT.Copy).then_inc(t_hi, 1)
                    if t == SLOTS - 1:
                        for c, (a, w) in enumerate(COLS):
                            wait_apart(e, z_full, 3 * m + c + 1 + 3)
                            e.activation(self0[:, a:a + w], ps[:, 3 + c, 0:w], ACT.Identity,
                                         bias=bias[:, 0, ds(m, 1)]).then_inc(own_out, 1)
            tiles(e, body)
            for n in range(SLOTS * KT, FAST):
                by_order.evict(e, n, n % 2)

        @on("vector")
        def _(e):
            for s in range(LEAD):
                by_order.rows(e, s, s % 2)

            def body(m, last):
                for t in range(SLOTS):
                    by_order.rows(e, SLOTS * m + t + LEAD, t % 2)
                    if t in TURNS:
                        e.wait_ge(t_hi, 3 * m + TURNS[t] + 1)
                        to, bank = high_group(e, TURNS[t], y_lo0)
                        e.tensor_tensor(to, bank, high_group(e, TURNS[t], y_hi0)[0].bitcast(F32),
                                        ALU.subtract).then_inc(t_free, 1)
            tiles(e, body)

        @on("gpsimd")
        def _(e):
            def body(m, last):
                for t in range(SLOTS):
                    s = SLOTS * m + t
                    by_order.add(e, s, t % 2, window_of(e, s))
                    if t == 1:
                        e.wait_ge(z_full, 3 * m + 3)
                        split_slab(e, 1, w_in[1], 16 * m + 16, w_ok[1])
                    if t == 4:
                        rest_slab(e, 1, w_ok[1], 2 * m + 1)
                    if t == KT + 1 and not last:
                        e.wait_ge(x_full, 3 * m + 3)
                        split_slab(e, 0, w_in[0], 16 * m + 32, w_ok[0])
                    if t == KT + 4 and not last:
                        rest_slab(e, 0, w_ok[0], 2 * m + 3)
            tiles(e, body)
            for n in range(SLOTS * KT, FAST):
                by_order.add(e, n, n % 2, window_of(e, n))
            e.wait_ge(by_order.took, FAST + 2)
            e.sem_inc(s_acc, 1)

        @on("sync")
        def _(e):
            e.sem_inc(y_st, 16)
            with e.Fori(1, KT) as m:
                for u, w in enumerate((I["L0_gnn_W_neigh0"], I["L0_gnn_W_self0"])):
                    e.wait_ge(w_ok[u], 2 * m)
                    e.dma_start(w_raw[:, u, :, :], view(w)[:, :, ds(m * 128, 128)]).then_inc(w_in[u], 16)
                e.wait_ge(t_free, 3 * m + 1)
                for i, t in enumerate((y_hi0, y_lo0)):
                    e.dma_start(y_d[ds(m - 1, 1), i].rearrange("a p t n -> p (a t) n"),
                                t[:].bitcast(F32)).then_inc(y_st, 16)
                e.wait_ge(own_out, 3 * m + 3)
                e.dma_start(self_d[ds(m - 1, 1)].rearrange("a p n -> p (a n)"), self0[:]).then_inc(y_st, 16)

        s_deg = sem("s_deg")
        s_big = sem("s_big")
        s_drow = sem("s_drow")

        def sums(e, ones_, adj_):
            for c, (a, w) in enumerate(COLS):
                for k in range(NT):
                    mm = e.matmul(ps[:, 3 + c, 0:w], ones_, adj_[:, k, a:a + w], start=(k == 0), stop=(k == NT - 1))
                mm.then_inc(s_deg, 1)

        @on("tensor")
        def _(e):
            e.wait_ge(s_acc, 1)
            e.wait_ge(own_out, 3 * KT + 3)
            sums(e, ones_r[:], adj)
            e.wait_ge(s_big, 6)
            big = e.value_load(flagi[0:1, 1:2], min_val=0, max_val=1)
            with e.If(big):
                sums(e, ones[0:P, :], adj_f)
            with e.Else():
                e.sem_inc(s_deg, 3)

        @on("vector")
        def _(e):
            for c, (a, w) in enumerate(COLS):
                e.wait_ge(s_deg, c + 1)
                e.tensor_reduce(deg_max[:, c:c + 1], ps[0:1, 3 + c, 0:w], AX.X, ALU.max).then_inc(s_big, 1)
            e.wait_ge(s_big, 3)
            e.tensor_reduce(deg_max[:, 3:4], deg_max[:, 0:3], AX.X, ALU.max).then_inc(s_big, 1)
            e.wait_ge(s_big, 4)
            e.tensor_scalar(deg_max[:, 4:5], deg_max[:, 3:4], EXACT, None, ALU.is_ge).then_inc(s_big, 1)
            e.wait_ge(s_big, 5)
            e.tensor_copy(flagi[:, 1:2], deg_max[:, 4:5]).then_inc(s_big, 1)
            e.wait_ge(s_deg, 6)
            for c, (a, w) in enumerate(COLS):
                e.tensor_scalar(yT[:, a:a + w], ps[:, 3 + c, 0:w], 1.0, None, ALU.max).then_inc(s_drow, 1)
                e.wait_ge(s_drow, 2 * c + 1)
                e.reciprocal(dinv_row[:, a:a + w], yT[:, a:a + w]).then_inc(s_drow, 1)

        z2_full = sem("z2_full")
        part_done = sem("part_done")
        u_done = sem("u_done")
        h_h = sem("h_h")
        h_l = sem("h_l")
        y_in = [sem(f"y_in{u}") for u in range(2)]
        held = ((y_hi0, y_lo0, self0), (y_hi, y_lo, self_part))
        h_row = lambda t, k: t[:, ds(k, 1), :].rearrange("p a n -> p (a n)")

        def aggregate(e, banks, parts, big, ready, full):
            def sums(parts, adj_):
                for c, (a, w) in enumerate(COLS):
                    ready(c)
                    n = 0
                    for k in range(NT):
                        for y in parts:
                            n += 1
                            mm = e.matmul(ps[:, banks + c, 0:w], y[:, k, :], adj_[:, k, a:a + w],
                                          start=(n == 1), stop=(n == 2 * NT))
                    mm.then_inc(full, 1)
            with e.If(big):
                sums([y[:].bitcast(F32) for y in parts], adj_f)
            with e.Else():
                sums(parts, adj)

        @on("sync")
        def _(e):
            e.wait_ge(s_acc, 1)
            e.wait_ge(y_st, 48 * (KT - 1) + 16)
            e.sem_inc(u_done, 3)

            def load(i, u, q):
                e.wait_ge(u_done, 3 * i + 3)
                for t, d in zip(held[1 - u], (y_d[ds(i, 1), 0], y_d[ds(i, 1), 1], self_d[ds(i, 1)])):
                    if t.dtype == F32R:
                        e.dma_start(t[:].bitcast(F32), d.rearrange("a p t n -> p (a t) n")).then_inc(y_in[1 - u], 16)
                    else:
                        e.dma_start(t[:], d.rearrange("a p n -> p (a n)")).then_inc(y_in[1 - u], 16)
            pipeline(e, KT - 1, (0, load))

        @on("tensor")
        def _(e):
            big = e.value_load(flagi[0:1, 1:2], min_val=0, max_val=1)
            e.wait_ge(t_free, 3 * KT + 1)
            aggregate(e, 0, held[0][:2], big, lambda c: None, z2_full)
            e.wait_ge(s_drow, 6)

            def item(i, u, q):
                e.wait_ge(y_in[1 - u], 48 * q + 48)
                aggregate(e, 3 - 3 * u, held[1 - u][:2], big, lambda c: e.wait_ge(u_done, 3 * i + c + 1), z2_full)
            pipeline(e, KT - 1, (0, item))

        @on("vector")
        def _(e):
            def total(n, k, banks, self_):
                for c, (a, w) in enumerate(COLS):
                    e.wait_ge(z2_full, 3 * n + c + 1)
                    e.tensor_tensor(layer_out[:, a:a + w], ps[:, banks + c, 0:w], dinv_row[:, a:a + w], ALU.mult).then_inc(part_done, 1)
                    e.wait_ge(part_done, 3 * n + c + 1)
                    e.tensor_tensor(layer_out[:, a:a + w], layer_out[:, a:a + w], self_[:, a:a + w], ALU.add)\
                        .then_inc(u_done, 1)
                e.wait_ge(h_h, n + 1)
                e.scalar_tensor_tensor(out=h_row(h_lo, k), in0=layer_out[:], scalar=0.0, in1=h_row(h_hi, k).bitcast(F32),
                                       op0=ALU.max, op1=ALU.subtract).then_inc(h_l, 1)
                e.wait_ge(h_l, n + 1)
            total(0, KT - 1, 0, self0)

            def item(i, u, q):
                e.wait_ge(y_in[1 - u], 48 * q + 48)
                total(i + 1, i, 3 - 3 * u, held[1 - u][2])
            pipeline(e, KT - 1, (0, item))

        @on("scalar")
        def _(e):
            def relu(n, k):
                wait_apart(e, u_done, 3 * n + 6)
                e.activation(h_row(h_hi, k), layer_out[:], ACT.Relu).then_inc(h_h, 1)
            relu(0, KT - 1)
            pipeline(e, KT - 1, (0, lambda i, u, q: relu(i + 1, i)))

        def l0_products(e):
            e.wait_ge(x_full, 3 * KT)
            e.wait_ge(z_full, 3 * KT + 3)

        def l0_split(e):
            for u in range(2):
                e.wait_ge(w_ok[u], 2 * KT)

        slabs1 = first_slabs("l1", I["L0_gnn_W_self1"], I["L0_gnn_W_neigh1"], l0_split, l0_products)

        def layer(tag, slabs, b, free):
            w_self, w_neigh, x_full, z_full, w_in, w_ok = slabs
            x_free = sem(f"{tag}_xfree")
            own_out = sem(f"{tag}_ownout")
            agg_out = sem(f"{tag}_aggout")
            t_full = sem(f"{tag}_tfull")
            t_hi = sem(f"{tag}_thi")
            t_free = sem(f"{tag}_tfree")
            sp_free = sem(f"{tag}_spfree")
            u_done = sem(f"{tag}_udone")
            x_in = sem(f"{tag}_xin")
            st = sem(f"{tag}_st")
            x2_ok = sem(f"{tag}_x2ok")
            T = 6
            nat = lambda a: a.rearrange("(t p) n -> p t n", p=P)
            x_view, x2_view = nat(I["x"]), nat(x2_d)

            @on("sync")
            def _(e):
                with e.Fori(1, KT) as m:
                    for u, w in enumerate((w_neigh, w_self)):
                        e.wait_ge(w_ok[u], 2 * m)
                        e.dma_start(w_raw[:, u, :, :], view(w)[:, :, ds(m * 128, 128)]).then_inc(w_in[u], 16)

            @on("gpsimd")
            def _(e):
                with e.Fori(1, KT) as m:
                    for u, full, n in ((0, x_full, 3 * m), (1, z_full, 6 * m - 3)):
                        e.wait_ge(full, n)
                        split_slab(e, u, w_in[u], 16 * m + 16, w_ok[u])
                        rest_slab(e, u, w_ok[u], 2 * m + 1)

            @on("tensor")
            def _(e):
                free(e)
                big = e.value_load(flagi[0:1, 1:2], min_val=0, max_val=1)
                e.sem_inc(x_free, 3)
                e.sem_inc(agg_out, 3)

                def neigh(m):
                    e.wait_ge(w_ok[0], 2 * m + 2)
                    product(e, 0, 0, lambda c: e.wait_ge(x_free, 3 * m + c + 1), x_full)

                def own(m):
                    e.wait_ge(w_ok[1], 2 * m + 2)
                    product(e, 3, 1, lambda c: e.wait_ge(agg_out, 3 * m + c + 1), z_full)

                def turn(n0, source, partitions, width):
                    for g, (t, n) in enumerate(GROUPS):
                        e.wait_ge(t_free, n0 + g // 2)
                        for i in range(n):
                            mm = e.transpose(ps[0:P, 6 + g % 2, 128 * i:128 * i + 128],
                                             source[:, P * (t + i):P * (t + i + 1)], ident[:])
                        mm.then_inc(t_full, 1)

                def aggregated(m):
                    e.wait_ge(t_free, T * m + 3)
                    aggregate(e, 3, (y_hi, y_lo), big, lambda c: e.wait_ge(own_out, 3 * m + c + 1), z_full)

                def back(m):
                    e.wait_ge(u_done, 3 * m + 3)
                    turn(T * m + 3, layer_out, 128, P)

                def step(m, first=False, final=False):
                    own(m)
                    if not first:
                        back(m - 1)
                    e.wait_ge(x_free, 3 * m + 6)
                    turn(T * m, yT, 128, P)
                    if not final:
                        neigh(m + 1)
                    aggregated(m)

                neigh(0)
                step(0, first=True)
                with e.Fori(1, KT - 1) as m:
                    step(m)
                step(KT - 1, final=True)
                back(KT - 1)

            @on("scalar")
            def _(e):
                e.wait_ge(s_small[3 + b], 16)
                free(e)
                e.sem_inc(sp_free, 3)
                e.sem_inc(st, 16)

                def neigh(m):
                    for c, (a, w) in enumerate(COLS):
                        e.wait_ge(x_full, 3 * m + c + 1)
                        e.activation(yT[:, a:a + w], ps[:, c, 0:w], ACT.Copy).then_inc(x_free, 1)

                def own(m):
                    for c, (a, w) in enumerate(COLS):
                        e.wait_ge(z_full, 6 * m + c + 1)
                        wait_apart(e, sp_free, 3 * m + c + 1)
                        e.activation(self_part[:, a:a + w], ps[:, 3 + c, 0:w], ACT.Identity,
                                     bias=bias[:, b, ds(m, 1)]).then_inc(own_out, 1)

                def high(m):
                    for g, (t, n) in enumerate(GROUPS):
                        e.wait_ge(t_full, T * m + g + 1)
                        e.activation(y_hi[:, t:t + n, :], ps[0:P, 6 + g % 2, 0:128 * n].rearrange("p (k n) -> p k n", k=n),
                                     ACT.Copy).then_inc(t_hi, 1)

                def store(m):
                    e.wait_ge(x2_ok, 3 * m + 3)
                    e.dma_start(x2_view[:, :, ds(m * 128, 128)], x2_slab[:]).then_inc(st, 16)

                def fetch(m):
                    e.dma_start(x_slab[:], x_view[:, :, ds(m * 128, 128)]).then_inc(x_in, 16)

                def step(m, first=False, final=False):
                    own(m)
                    high(m)
                    if not final:
                        neigh(m + 1)
                    if not first:
                        store(m - 1)
                    fetch(m)

                neigh(0)
                step(0, first=True)
                with e.Fori(1, KT - 1) as m:
                    step(m)
                step(KT - 1, final=True)
                store(KT - 1)

            @on("vector")
            def _(e):
                free(e)

                def low(m):
                    for g, (t, n) in enumerate(GROUPS):
                        e.wait_ge(t_hi, 3 * m + g + 1)
                        e.tensor_tensor(y_lo[:, t:t + n, :], ps[0:P, 6 + g % 2, 0:128 * n].rearrange("p (k n) -> p k n", k=n),
                                        y_hi[:, t:t + n, :].bitcast(F32), ALU.subtract).then_inc(t_free, 1)

                def total(m):
                    for c, (a, w) in enumerate(COLS):
                        e.wait_ge(z_full, 6 * m + 3 + c + 1)
                        e.tensor_tensor(layer_out[:, a:a + w], ps[:, 3 + c, 0:w], dinv_row[:, a:a + w], ALU.mult).then_inc(agg_out, 1)
                        e.wait_ge(agg_out, 3 * m + c + 1 + 3)
                        e.tensor_tensor(layer_out[:, a:a + w], layer_out[:, a:a + w], self_part[:, a:a + w], ALU.add)\
                            .then_inc(u_done, 1)
                        e.wait_ge(u_done, 3 * m + c + 1)
                        e.sem_inc(sp_free, 1)

                def residual(m):
                    e.wait_ge(x_in, 16 * m + 16)
                    e.wait_ge(st, 16 * m + 16)
                    for g, (t, n) in enumerate(GROUPS):
                        e.wait_ge(t_full, T * m + 3 + g + 1)
                        e.tensor_tensor(x2_slab[:, t:t + n, :], ps[0:P, 6 + g % 2, 0:128 * n].rearrange("p (k n) -> p k n", k=n),
                                        x_slab[:, t:t + n, :], ALU.add).then_inc(x2_ok, 1)
                        e.wait_ge(x2_ok, 3 * m + g + 1)
                        e.sem_inc(t_free, 1)

                def step(m, first=False):
                    if not first:
                        residual(m - 1)
                    low(m)
                    total(m)

                step(0, first=True)
                with e.Fori(1, KT) as m:
                    step(m)
                residual(KT - 1)
            return dict(st=st, z_full=(z_full, 6 * KT), w_ok=w_ok, u_done=u_done)

        def relued(e):
            e.wait_ge(h_l, KT)

        l1 = layer("l1", slabs1, 1, relued)

        r_in = [sem(f"r_in{u}") for u in range(2)]
        r_ok = sem("r_ok")
        r_full = sem("r_full")
        rw1_view = I["L0_ffn_rw1"].rearrange("(k p) n -> p k n", p=128)

        @on("sync")
        def _(e):
            e.dma_start(rw2[:], I["L0_ffn_rw2"].rearrange("(k p) n -> p k n", p=128)).then_inc(s_small[2], 16)
            for u in range(2):
                e.wait_ge(l1["w_ok"][u], 2 * KT)
                e.dma_start(w_raw[:, u, :, :], rw1_view[:, :, 128 * u:128 * u + 128]).then_inc(r_in[u], 16)

        @on("gpsimd")
        def _(e):
            e.wait_ge(l1["z_full"][0], 6 * (KT - 1) + 3)
            for u in range(2):
                split_slab(e, u, r_in[u], 16, r_ok)
                rest_slab(e, u, r_ok, 2 * u + 1)

        ln2 = layer_norm("ln2", x2_d, lambda e: e.wait_ge(l1["st"], 16 * KT + 16), t_d, x2_all)

        r_hid = sem("r_hid")
        r_log = sem("r_log")
        r_zero = sem("r_zero")

        def normed(e):
            e.wait_ge(*ln2["lo"])

        @on("sync")
        def _(e):
            with e.Fori(1, KT // 2) as q:
                for u in range(2):
                    e.wait_ge(r_ok, 4 * q + 2 * u - 2)
                    e.dma_start(w_raw[:, u, :, :], rw1_view[:, :, ds(q * 256 + 128 * u, 128)]).then_inc(r_in[u], 16)

        @on("gpsimd")
        def _(e):
            with e.Fori(1, KT // 2) as q:
                for u in range(2):
                    e.wait_ge(r_full, 6 * q + 3 * u)
                    split_slab(e, u, r_in[u], 16 * q + 16, r_ok)
                    rest_slab(e, u, r_ok, 4 * q + 2 * u + 1)

        @on("tensor")
        def _(e):
            normed(e)
            e.wait_ge(s_small[2], 16)
            e.sem_inc(r_full, 3)
            e.sem_inc(r_hid, 6)
            e.wait_ge(r_zero, 1)
            e.matmul(ps[0:P, 6, 0:NT * NX], hidden[:, 0, 0:P], hidden[:, 0, 0:NT * NX], start=True, stop=True,
                     skip_group_check=True).then_inc(r_zero, 1)

            def head(m, u, q):
                e.wait_ge(r_ok, 2 * m + 2)
                product(e, 3 * u, u, lambda c: e.wait_ge(r_hid, 3 * m + c + 1), r_full)

            def tail(m, u, q):
                e.wait_ge(r_hid, 3 * m + 3 + 6)
                for i in range(NT):
                    mm = e.matmul(ps[0:P, 6, NX * i:NX * i + NX], hidden[:, u, P * i:P * i + P],
                                  rw2[:, ds(m, 1), :].rearrange("p a n -> p (a n)"), start=False, stop=True,
                                  skip_group_check=True)
                mm.then_inc(r_log, 1)
            skewed(e, KT, head, tail)

        @on("scalar")
        def _(e):
            e.wait_ge(s_small[5], 16)
            normed(e)
            e.sem_inc(r_log, 2)

            def head(m, u, q):
                e.wait_ge(r_log, m + 1)
                for c, (a, w) in enumerate(COLS):
                    wait_apart(e, r_full, 3 * m + c + 1 + 3)
                    e.activation(hidden[:, u, a:a + w], ps[:, 3 * u + c, 0:w], ACT.Silu, bias=bias[:, 2, ds(m, 1)])\
                        .then_inc(r_hid, 1)
            e.wait_ge(r_zero, 2)
            pipeline(e, KT, (0, head))

        @on("vector")
        def _(e):
            normed(e)
            e.memset(hidden[:, 0, :], 0.0).then_inc(r_zero, 1)
            e.wait_ge(r_log, KT + 2)

        b_st = sem("b_st")

        @on("sync")
        def _(e):
            e.wait_ge(*ln2["sm"])
            e.dma_start(r_d.rearrange("(t p) n -> p t n", p=P), x2_all[:]).then_inc(b_st, 16)

        g_c = sem("g_c")
        g_v = sem("g_v")
        g_ls = sem("g_ls")
        g_ex = sem("g_ex")
        g_r = sem("g_r")
        g_cnt = sem("g_cnt")
        g_hot = sem("g_hot")
        g_ids = sem("g_ids")
        g_x = sem("g_x")
        g_ok = sem("g_ok")
        g_eb = sem("g_eb")
        g_w = sem("g_w")
        g_wT = sem("g_wT")
        g_b2 = sem("g_b2")

        @on("sync")
        def _(e):
            e.dma_start(rb2b[:], I["L0_ffn_rb2"].partition_broadcast(P)).then_inc(s_rb2, 16)
            e.dma_start(eb1c[:], I["L0_ffn_eb1"].rearrange("e (k p) -> p (e k)", p=128),
                        allow_slow_non_contiguous=True).then_inc(g_eb, 16)
            e.wait_ge(r_full, 3 * KT + 3)
            e.dma_start(eb2[:], I["L0_ffn_eb2"]).then_inc(g_b2, 16)

        @on("gpsimd")
        def _(e):
            e.memset(below[:], 1.0).then_inc(g_c, 1)
            e.memset(before[:], 1.0).then_inc(g_c, 1)
            e.iota(toki[:], [[P, NT]], base=0, channel_multiplier=1).then_inc(g_c, 1)
            e.iota(seqi[:], [[1, 128]], base=0, channel_multiplier=0).then_inc(g_c, 1)
            e.wait_ge(g_c, 4)
            e.affine_select(out=below[:], in_=below[:], compare_op=ALU.is_gt, fill=0.0, base=0,
                            pattern=[[1, NX], [-1, NX]], channel_multiplier=0).then_inc(g_c, 1)
            e.affine_select(out=before[:], in_=before[:], compare_op=ALU.is_gt, fill=0.0, base=0,
                            pattern=[[1, P]], channel_multiplier=-1).then_inc(g_c, 1)
            e.tensor_copy(tokf[:], toki[:]).then_inc(g_c, 1)
            e.tensor_copy(seqf[:], seqi[:]).then_inc(g_c, 1)

        @on("vector")
        def _(e):
            n = [0]

            def link(ins):
                n[0] += 1
                ins.then_inc(g_v, 1)
                e.wait_ge(g_v, n[0])

            e.wait_ge(g_c, 8)
            e.wait_ge(s_rb2, 16)
            over = lambda ap, t: ap.rearrange("p (a n) -> p a n", a=1).to_broadcast([P, t, NX])
            each = lambda ap: ap.rearrange("p (t a) -> p t a", a=1).to_broadcast([P, NT, NX])
            link(e.tensor_tensor(logit[:], ps[0:P, 6, 0:NT * NX].rearrange("p (t n) -> p t n", n=NX), over(rb2b[:], NT), ALU.add))
            link(e.tensor_reduce(peak[:], logit[:], AX.X, ALU.max))
            e.tensor_tensor(less[:], logit[:], each(peak[:]), ALU.subtract).then_inc(g_ls, 1)
            lf = logit[:].rearrange("p t (a n) -> p t a n", a=1).to_broadcast([P, NT, NX, NX])
            le = logit[:].rearrange("p t (n a) -> p t n a", a=1).to_broadcast([P, NT, NX, NX])
            link(e.tensor_tensor(cmpa[:], lf, le, ALU.is_gt))
            link(e.tensor_tensor(cmpb[:], lf, le, ALU.is_ge))
            link(e.tensor_tensor(cmpb[:], cmpb[:],
                                 below[:].rearrange("p (a n) m -> p a n m", a=1).to_broadcast([P, NT, NX, NX]), ALU.mult))
            link(e.tensor_tensor(cmpa[:], cmpa[:], cmpb[:], ALU.max))
            link(e.tensor_reduce(rank[:], cmpa[:], AX.X, ALU.add))
            link(e.tensor_scalar(sel[:], rank[:], float(TOP - 1), None, ALU.is_le))
            e.tensor_reduce(taken[:], sel[:].rearrange("p t n -> p n t"), AX.X, ALU.add).then_inc(g_r, 1)
            e.wait_ge(g_ex, 1)
            link(e.tensor_tensor(less[:], less[:], sel[:], ALU.mult))
            link(e.tensor_reduce(peak[:], less[:], AX.X, ALU.add))
            link(e.reciprocal(peak[:], peak[:]))
            link(e.tensor_tensor(less[:], less[:], each(peak[:]), ALU.mult))
            e.sem_inc(g_w, 1)
            e.wait_ge(g_cnt, 1)
            link(e.tensor_copy(cum[:, 0, :], ps[0:P, 7, 0:NX]))
            for t in range(1, NT):
                link(e.tensor_tensor(cum[:, t, :], cum[:, t - 1, :], sel[:, t - 1, :], ALU.add))
            link(e.tensor_scalar(steps[:], ps[0:P, 7, NX:2 * NX], 1.0 / M, 0.5 - 0.5 / M, ALU.mult, ALU.add))
            link(e.tensor_scalar(steps[:], steps[:], ROUND, ROUND, ALU.add, ALU.subtract))
            link(e.memset(first[:], 0.0))
            for x in range(1, NX):
                link(e.tensor_tensor(first[:, x:x + 1], first[:, x - 1:x], steps[:, x - 1:x], ALU.add))
            ids = seqf[0:1, 0:NS].rearrange("p (n a) -> p n a", a=1).to_broadcast([1, NS, NX - 1])
            fst = first[0:1, 1:NX].rearrange("p (a n) -> p a n", a=1).to_broadcast([1, NS, NX - 1])
            link(e.tensor_tensor(step_past[:], fst, ids, ALU.is_le))
            link(e.tensor_reduce(step_f[:], step_past[:], AX.X, ALU.add))
            e.tensor_copy(step_x[:], step_f[:]).then_inc(g_x, 1)
            link(e.tensor_scalar(steps[:], first[:], float(M), None, ALU.mult))
            link(e.tensor_tensor(cum[:], cum[:], over(steps[:], NT), ALU.add))
            for c in range(TOP):
                link(e.tensor_scalar(sel[:], rank[:], float(c), None, ALU.is_equal))
                link(e.tensor_tensor(cmpa[:, :, 0, :], sel[:], cum[:], ALU.mult))
                link(e.tensor_tensor(cmpb[:, :, 0, :], sel[:], less[:], ALU.mult))
                link(e.tensor_reduce(slotf[:, c, :], cmpa[:, :, 0, :], AX.X, ALU.add))
                link(e.tensor_reduce(weight[:, c, :], cmpb[:, :, 0, :], AX.X, ALU.add))
            link(e.tensor_copy(sloti[:], slotf[:]))
            link(e.tensor_scalar(block_[:], slotf[:], 1.0 / 128, 0.5 / 128 - 0.5, ALU.mult, ALU.add))
            link(e.tensor_scalar(block_[:], block_[:], ROUND, ROUND, ALU.add, ALU.subtract))
            link(e.scalar_tensor_tensor(out=slotf[:], in0=block_[:], scalar=-128.0, in1=slotf[:], op0=ALU.mult, op1=ALU.add))
            flat = lambda t, w: t[:].rearrange("p c t -> p (c t)").rearrange("p (n a) -> p n a", a=1).to_broadcast([P, TOP * NT, w])
            row = lambda w: seqf[:, 0:w].rearrange("p (a n) -> p a n", a=1).to_broadcast([P, TOP * NT, w])
            link(e.tensor_tensor(place_hot[:], row(128), flat(slotf, 128), ALU.is_equal))
            link(e.tensor_tensor(block_hot[:], row(NS * SUB), flat(block_, NS * SUB), ALU.is_equal))
            for c in range(TOP):
                half = block_hot[:, c * NT:(c + 1) * NT, :]
                e.tensor_tensor(half, half, tokf[:].rearrange("p (n a) -> p n a", a=1).to_broadcast([P, NT, NS * SUB]),
                                ALU.mult).then_inc(g_hot, 1)
            e.wait_ge(g_ids, 1)
            e.tensor_copy(ids_i[:], ps[:, 7, 64:64 + NS * SUB]).then_inc(g_ok, 1)

        @on("scalar")
        def _(e):
            e.wait_ge(g_ls, 1)
            e.activation(less[:], less[:], ACT.Exp).then_inc(g_ex, 1)
            for g, (t, n) in enumerate(GROUPS):
                e.wait_ge(g_wT, g + 1)
                e.activation(gate_T[:, P * t:P * (t + n)], ps[0:NX, g, 0:P * n], ACT.Copy).then_inc(g_w, 1)

        @on("tensor")
        def _(e):
            e.wait_ge(g_r, 1)
            e.matmul(ps[0:P, 7, 0:NX], before[:], taken[:], start=True, stop=True, skip_group_check=True)
            e.matmul(ps[0:P, 7, NX:2 * NX], ones[0:P, 0:P], taken[:], start=False, stop=True,
                     skip_group_check=True).then_inc(g_cnt, 1)
            e.wait_ge(g_w, 1)
            e.wait_ge(r_hid, 3 * KT + 6)
            for g, (t, n) in enumerate(GROUPS):
                for i in range(n):
                    mm = e.transpose(ps[0:NX, g, P * i:P * i + P], less[:, t + i, :], ident[0:P, 0:P])
                mm.then_inc(g_wT, 1)
            e.wait_ge(g_hot, 2)
            for i in range(TOP * NT):
                mm = e.matmul(ps[:, 7, 64:64 + NS * SUB], place_hot[:, i, :], block_hot[:, i, :],
                              start=(i == 0), stop=(i == TOP * NT - 1))
            mm.then_inc(g_ids, 1)

        m_win = [[sem(f"m_win{w}{u}") for u in range(2)] for w in range(2)]
        m_whi = [sem(f"m_whi{w}") for w in range(2)]
        m_wlo = [sem(f"m_wlo{w}") for w in range(2)]
        m_idx = sem("m_idx")
        m_xin = [[sem(f"m_xin{u}{b}") for b in range(SUB)] for u in range(2)]
        m_tx = sem("m_tx")
        m_xhi = sem("m_xhi")
        m_xlo = sem("m_xlo")
        m_g1 = sem("m_g1")
        m_h = sem("m_h")
        m_hhi = sem("m_hhi")
        m_hlo = sem("m_hlo")
        m_g2 = sem("m_g2")
        m_out = sem("m_out")
        m_st = [sem(f"m_st{u}") for u in range(2)]
        NB = SUB * 2
        w1_view = I["L0_ffn_ew1"].rearrange("e (k p) h -> e p k h", p=128)
        w2_view = I["L0_ffn_ew2"].rearrange("e (k p) n -> e p k n", p=128)

        def gated(e):
            e.wait_ge(g_x, 1)
            e.wait_ge(b_st, 16)
            e.wait_ge(g_w, 4)
            for u in range(2):
                e.wait_ge(ln2["t_st"][u], 16 * (NT // 2) + 16)

        @on("sync")
        def _(e):
            gated(e)
            for w in range(2):
                e.sem_inc(m_wlo[w], 2)

            def head(s, u, q):
                x = e.value_load(step_x[0:1, ds(s, 1)], min_val=0, max_val=NX - 1)
                for w, (raw, view) in enumerate(((w1_raw, w1_view), (w2_raw, w2_view))):
                    e.wait_ge(m_wlo[w], s + 1)
                    e.dma_start(raw[:, u], view[ds(x, 1)].rearrange("a p k n -> p (a k) n")).then_inc(m_win[w][u], 16)
            pipeline(e, NS, (0, head))

        @on("gpsimd")
        def _(e):
            gated(e)
            e.wait_ge(g_ok, 1)
            e.sem_inc(m_tx, 8)

            def head(s, u, q):
                wait_apart(e, m_tx, 4 * s + 4)
                e.tensor_copy(id_now[:, u, :], ids_i[:, ds(s * SUB, SUB)]).then_inc(m_idx, 1)
                wait_apart(e, m_idx, s + 1)
                for b in range(SUB):
                    e.indirect_dma_start(out=x_rows[:, u, b, :], out_offset=None, in_=t_d[:, :],
                                         in_offset=bass.IndirectOffsetOnAxis(ap=id_now[:, u, b:b + 1], axis=0)).then_inc(m_xin[u][b], 16)
            pipeline(e, NS, (0, head))

        @on("tensor")
        def _(e):
            gated(e)
            e.sem_inc(m_xlo, 2)
            e.sem_inc(m_h, 2)
            e.sem_inc(m_g1, 4)
            e.sem_inc(m_g2, 2 * NB)

            def turn(s, u, q, groups=range(4)):
                if groups[0] == 0:
                    for b in range(SUB):
                        e.wait_ge(m_xin[u][b], 16 * q + 16)
                for g in groups:
                    e.wait_ge(m_xlo, 4 * s + g + 1)
                    for k in range(2):
                        for b in range(SUB):
                            mm = e.transpose(ps[:, g % 2, k * M + 128 * b:k * M + 128 * b + 128],
                                             x_rows[:, u, b, 128 * (2 * g + k):128 * (2 * g + k + 1)], ident[:])
                    mm.then_inc(m_tx, 1)

            def head(s, u, q):
                e.wait_ge(m_wlo[0], s + 3)
                e.wait_ge(m_xlo, 4 * s + 4 + 2)
                for j in range(HK):
                    e.wait_ge(m_h, HK * s + j + 1)
                    n = 0
                    for k in range(KT):
                        for wt, xt in ((w1_hi, xt_hi), (w1_hi, xt_lo), (w1_lo, xt_hi)):
                            n += 1
                            mm = e.matmul(ps[:, 2 + j, 0:M], wt[:, u, k, 128 * j:128 * j + 128], xt[:, u, k, :],
                                          start=(n == 1), stop=(n == 3 * KT))
                    mm.then_inc(m_g1, 1)
                    if not isinstance(s, int) or s < NS - 1:
                        turn(s + 1, 1 - u, q + u, range(2 * j, 2 * j + 2))

            def tail(s, u, q):
                e.wait_ge(m_hlo, s + 1)
                e.wait_ge(m_wlo[1], s + 3)
                for b in range(SUB):
                    for half in range(2):
                        e.wait_ge(m_out, NB * s + NB + 2 * b + half + 1)
                        n = 0
                        for j in range(HK):
                            for ht, wt in ((hid_hi, w2_hi), (hid_hi, w2_lo), (hid_lo, w2_hi)):
                                n += 1
                                mm = e.matmul(ps[:, 4 + 2 * b + half, :], ht[:, u, j, 128 * b:128 * b + 128],
                                              wt[:, u, j, 512 * half:512 * half + 512], start=(n == 1), stop=(n == 3 * HK))
                        mm.then_inc(m_g2, 1)
            turn(0, 0, 0)
            skewed(e, NS, head, tail)

        def more(s):
            return not isinstance(s, int) or s < NS - 1

        group = lambda t, u, g: t[:, u, 2 * g:2 * g + 2, :]
        bank = lambda g: ps[:, g % 2, :].rearrange("p (k n) -> p k n", k=2)

        @on("scalar")
        def _(e):
            gated(e)
            e.wait_ge(g_eb, 16)

            def w1(s, u, q):
                e.wait_ge(m_win[0][u], 16 * q + 16)
                e.wait_ge(m_g1, HK * s + HK)
                e.activation(w1_hi[:, u], w1_raw[:, u], ACT.Copy).then_inc(m_whi[0], 1)

            def w2(s, u, q):
                e.wait_ge(m_win[1][u], 16 * q + 16)
                e.wait_ge(m_g2, NB * s + NB)
                e.activation(w2_hi[:, u], w2_raw[:, u], ACT.Copy).then_inc(m_whi[1], 1)

            def rows(s, u, q, groups=range(4)):
                for g in groups:
                    e.wait_ge(m_tx, 4 * s + g + 1 + 8)
                    e.activation(group(xt_hi, u, g), bank(g), ACT.Copy).then_inc(m_xhi, 1)

            def head(s, u, q):
                x = e.value_load(step_x[0:1, ds(s, 1)], min_val=0, max_val=NX - 1)
                for j in range(HK):
                    wait_apart(e, m_g1, HK * s + j + 1 + 4)
                    e.activation(hid[:, u, j, :], ps[:, 2 + j, 0:M], ACT.Silu, bias=eb1c[:, ds(x * HK + j, 1)]).then_inc(m_h, 1)
                    if more(s):
                        rows(s + 1, 1 - u, q + u, range(2 * j, 2 * j + 2))
                e.wait_ge(m_h, HK * s + HK + 2)
                e.wait_ge(m_g2, NB * s + NB)
                e.activation(hid_hi[:, u], hid[:, u], ACT.Copy).then_inc(m_hhi, 1)
                if more(s):
                    w1(s + 1, 1 - u, q + u)
                w2(s, u, q)

            def tail(s, u, q):
                e.wait_ge(m_out, NB * s + NB + 2 * NB)
                e.dma_start(o_d[ds(s * M, M), :].rearrange("(b p) n -> p b n", p=128), o_rows[:, u]).then_inc(m_st[u], 16)

            e.sem_inc(m_out, 2 * NB)
            for u in range(2):
                e.sem_inc(m_st[u], 16)
            w1(0, 0, 0)
            rows(0, 0, 0)
            skewed(e, NS, head, tail)

        @on("vector")
        def _(e):
            gated(e)

            def w(i, raw, hi, lo, s, u, q):
                e.wait_ge(m_whi[i], s + 1)
                e.tensor_tensor(lo[:, u], raw[:, u], hi[:, u].bitcast(F32), ALU.subtract).then_inc(m_wlo[i], 1)

            def rows(s, u, q, groups=range(4)):
                for g in groups:
                    e.wait_ge(m_xhi, 4 * s + g + 1)
                    e.tensor_tensor(group(xt_lo, u, g), bank(g), group(xt_hi, u, g).bitcast(F32), ALU.subtract).then_inc(m_xlo, 1)

            def head(s, u, q):
                if more(s):
                    rows(s + 1, 1 - u, q + u)
                e.wait_ge(m_hhi, s + 1)
                e.tensor_tensor(hid_lo[:, u], hid[:, u], hid_hi[:, u].bitcast(F32), ALU.subtract).then_inc(m_hlo, 1)
                if more(s):
                    w(0, w1_raw, w1_hi, w1_lo, s + 1, 1 - u, q + u)
                w(1, w2_raw, w2_hi, w2_lo, s, u, q)

            def tail(s, u, q):
                e.wait_ge(m_st[u], 16 * q + 16)
                for b in range(SUB):
                    for half in range(2):
                        e.wait_ge(m_g2, NB * s + 2 * b + half + 1 + 2 * NB)
                        cols = slice(512 * half, 512 * half + 512)
                        e.tensor_copy(o_rows[:, u, b, cols], ps[:, 4 + 2 * b + half, :]).then_inc(m_out, 1)
            w(0, w1_raw, w1_hi, w1_lo, 0, 0, 0)
            rows(0, 0, 0)
            skewed(e, NS, head, tail)

        f_idx = sem("f_idx")
        f_oin = [[sem(f"f_oin{c}{u}") for u in range(2)] for c in range(TOP)]
        f_rin = sem("f_rin")
        f_bias = sem("f_bias")
        f_free = sem("f_free")
        f_y = sem("f_y")
        f_st = sem("f_st")
        r_row = lambda i: r_all[:, ds(i, 1), :].rearrange("p a n -> p (a n)")

        @on("sync")
        def _(e):
            e.sem_inc(f_y, 2)
            e.wait_ge(m_g1, HK * NS + 4)
            e.dma_start(r_all[:], r_d.rearrange("(t p) n -> p t n", p=P)).then_inc(f_rin, 16)

            def store(i, u, q):
                e.wait_ge(f_y, i + 3)
                e.dma_start(out[ds(i * P, P), :], r_row(i)).then_inc(f_st, 16)
            pipeline(e, NT, (0, store))
            e.wait_ge(f_st, 16 * NT)

        @on("gpsimd")
        def _(e):
            for u in range(2):
                e.wait_ge(m_st[u], 16 * ((NS + 1 - u) // 2) + 16)

            def head(i, u, q):
                wait_apart(e, f_y, i + 1)
                e.tensor_copy(slot_now[:, u, :], sloti[:, :, ds(i, 1)].rearrange("p c a -> p (c a)")).then_inc(f_idx, 1)
                wait_apart(e, f_idx, i + 1)
                for c in range(TOP):
                    e.indirect_dma_start(out=pick[:, u, c, :], out_offset=None, in_=o_d[:, :],
                                         in_offset=bass.IndirectOffsetOnAxis(ap=slot_now[:, u, c:c + 1], axis=0)).then_inc(f_oin[c][u], 16)
            pipeline(e, NT, (0, head))

        @on("vector")
        def _(e):
            def head(i, u, q):
                e.wait_ge(f_bias, i + 1)
                y = r_row(i)
                for half in range(2):
                    cols = slice(512 * half, 512 * half + 512)
                    mm = e.tensor_tensor(y[:, cols], ps[0:P, 4 + 2 * u + half, :], y[:, cols], ALU.add)
                mm.then_inc(f_free, 1)
                for c in range(TOP):
                    e.wait_ge(f_free, TOP * i + c + 1 + 2)
                    e.wait_ge(f_oin[c][u], 16 * q + 16)
                    e.scalar_tensor_tensor(out=y, in0=pick[:, u, c, :], scalar=weight[:, c, ds(i, 1)], in1=y,
                                           op0=ALU.mult, op1=ALU.add).then_inc((f_free, f_y)[c], 1)
            e.wait_ge(f_rin, 16)
            pipeline(e, NT, (0, head))

        @on("tensor")
        def _(e):
            e.wait_ge(g_b2, 16)
            e.wait_ge(m_out, NB * NS + 2 * NB)
            e.sem_inc(f_free, 2)

            for i in range(NT):
                u = i % 2
                e.wait_ge(f_free, max(TOP * i - 1, 1))
                for half in range(2):
                    mm = e.matmul(ps[0:P, 4 + 2 * u + half, :], gate_T[:, P * i:P * i + P], eb2[:, 512 * half:512 * half + 512],
                                  start=True, stop=True)
                mm.then_inc(f_bias, 1)

        with nc.Block() as block:
            for engine, parts in ((block.sync, prog["sync"]), (block.scalar, prog["scalar"]),
                                  (block.vector, prog["vector"]), (block.gpsimd, prog["gpsimd"]),
                                  (block.tensor, prog["tensor"])):
                @engine
                def _(e, parts=parts):
                    for part in parts:
                        part(e)


_INS = ["x", "src", "dst", "L0_gnn_W_self0", "L0_gnn_W_neigh0", "L0_gnn_b0", "L0_gnn_W_self1", "L0_gnn_W_neigh1",
        "L0_gnn_b1", "L0_ffn_rw1", "L0_ffn_rb1", "L0_ffn_rw2", "L0_ffn_rb2", "L0_ffn_ew1", "L0_ffn_eb1",
        "L0_ffn_ew2", "L0_ffn_eb2"]


def kernel(**inputs):
    import numpy as np
    import concourse.bacc as bacc
    from concourse.bass_utils import run_bass_kernel_spmd

    nc = bacc.Bacc("TRN2", target_bir_lowering=False, num_devices=1)
    arrays, aps = {}, {}
    for name in _INS:
        a = np.ascontiguousarray(inputs[name])
        arrays[f"in_{name}"] = a
        aps[name] = nc.dram_tensor(f"in_{name}", a.shape, mybir.dt.from_np(a.dtype), kind="ExternalInput").ap()
    out = nc.dram_tensor("out_0", (N, D), F32, kind="ExternalOutput").ap()
    build(nc, aps, out)
    r = run_bass_kernel_spmd(nc, [arrays], core_ids=[0])
    return r.results[0]["out_0"]
```
